# Optimizing a Trainium2 kernel written in Bass

```python
import numpy as np
import jax
import jax.numpy as jnp

def _softmax(x, axis=-1):
    return jax.nn.softmax(x, axis=axis)

def _gelu(x):
    return jax.nn.gelu(x, approximate=True)

def _silu(x):
    return jax.nn.silu(x)

def _sigmoid(x):
    return jax.nn.sigmoid(x)

def _layernorm(x, axis=-1, eps=1e-05):
    m = jnp.mean(x, axis=axis, keepdims=True)
    v = jnp.var(x, axis=axis, keepdims=True)
    return (x - m) / jnp.sqrt(v + eps)

def _scatter_add(tgt, idx, src, axis=0):
    return tgt.at[idx].add(src)

def _segment_sum(src, seg, n):
    return jax.ops.segment_sum(src, seg, n)
kernel_name = 'mk_xattn_ffn_d2_seqx_r4_41f6c6'

def setup_inputs(seed: int=0):
    np.random.seed(seed)
    _w = jnp.asarray

    def _rec_inputs():
        import jax
        import jax.numpy as jnp
        _rk = jax.random.key(seed)
        x = -0.000125 + 0.9999 * jax.random.normal(jax.random.fold_in(_rk, 1), (32, 100, 256), jnp.float32)
        _lenS = 100 - jax.random.randint(jax.random.fold_in(_rk, 7), (32,), 0, max(1, 100 // 4) + 1, jnp.int32)
        _lenS2 = 361 - jax.random.randint(jax.random.fold_in(_rk, 8), (32,), 0, max(1, 361 // 4) + 1, jnp.int32)
        _ctx_768P = jax.random.normal(jax.random.fold_in(_rk, 11), (32, 16, 192), jnp.float32)
        _ctx_768c = jax.random.dirichlet(jax.random.fold_in(_rk, 511), 0.3 * jnp.ones((16,), jnp.float32), (32, 361))
        _ctx_768t = jnp.einsum('bsk,bkd->bsd', _ctx_768c, _ctx_768P)
        _ctx_768t = _ctx_768t * jax.lax.rsqrt(jnp.mean(jnp.square(_ctx_768t)) + 1e-12) * 0.953939
        ctx_768 = 0.00272024 + 0.999456 * (_ctx_768t + 0.3 * jax.random.normal(jax.random.fold_in(_rk, 611), (32, 361, 192), jnp.float32))
        _validS = jnp.arange(100)[None, :] < _lenS[:, None]
        _validS2 = jnp.arange(361)[None, :] < _lenS2[:, None]
        _causal = jnp.tril(jnp.ones((100, 100), dtype=bool))
        mask_1x1xSxS2_bk0 = jnp.logical_not(jnp.broadcast_to(_validS2[0:1, None, None, :], (1, 1, 100, 361)))
        return (x, ctx_768, mask_1x1xSxS2_bk0)
    x, ctx_768, mask_1x1xSxS2_bk0 = _rec_inputs()

    def _L0_xattn_setup():
        import jax, jax.numpy as jnp
        import numpy as np
        B, N, M = (8, 1024, 77)
        Q_DIM, CTX_DIM = (256, 192)
        H, D = (16, 64)
        INNER = H * D
        key = jax.random.key(seed)
        ks = jax.random.split(key, 7)
        x = jax.random.normal(ks[0], (B, N, Q_DIM), dtype=jnp.float32)
        context = jax.random.normal(ks[1], (B, M, CTX_DIM), dtype=jnp.float32)
        Wq = jax.random.normal(ks[2], (Q_DIM, INNER), dtype=jnp.float32) * Q_DIM ** (-0.5)
        Wk = jax.random.normal(ks[3], (CTX_DIM, INNER), dtype=jnp.float32) * CTX_DIM ** (-0.5)
        Wv = jax.random.normal(ks[4], (CTX_DIM, INNER), dtype=jnp.float32) * CTX_DIM ** (-0.5)
        Wo = jax.random.normal(ks[5], (INNER, Q_DIM), dtype=jnp.float32) * INNER ** (-0.5)
        bo = jax.random.normal(ks[6], (Q_DIM,), dtype=jnp.float32) * 0.01
        return {'x': x, 'context': context, 'Wq': Wq, 'Wk': Wk, 'Wv': Wv, 'Wo': Wo, 'bo': bo}
    _L0_xattn_all = _L0_xattn_setup()
    _L0_xattn_in = {k: v for k, v in _L0_xattn_all.items() if k in ('Wq', 'Wk', 'Wv', 'Wo', 'bo')}
    del _L0_xattn_all

    def _L0_ffn_setup():
        import jax, jax.numpy as jnp
        import numpy as np
        from jax import lax
        B, S, D = (4, 512, 256)
        E = 8
        K = 2
        F = 816
        NORM_TOPK = True
        key = jax.random.key(seed)
        ks = jax.random.split(key, 8)
        sd = 0.02
        return {'x': jax.random.normal(ks[0], (B, S, D), jnp.float32), 'gate_w': jax.random.normal(ks[1], (E, D), jnp.float32) * sd, 'gate_b': jnp.zeros((E,), jnp.float32), 'up_w': jax.random.normal(ks[2], (E, F, D), jnp.float32) * sd, 'up_b': jnp.zeros((E, F), jnp.float32), 'gp_w': jax.random.normal(ks[3], (E, F, D), jnp.float32) * sd, 'gp_b': jnp.zeros((E, F), jnp.float32), 'down_w': jax.random.normal(ks[4], (E, D, F), jnp.float32) * sd, 'down_b': jnp.zeros((E, D), jnp.float32)}
    _L0_ffn_all = _L0_ffn_setup()
    _L0_ffn_in = {k: v for k, v in _L0_ffn_all.items() if k in ('gate_w', 'gate_b', 'up_w', 'up_b', 'gp_w', 'gp_b', 'down_w', 'down_b')}
    del _L0_ffn_all

    def _L1_xattn_setup():
        import jax, jax.numpy as jnp
        import numpy as np
        B, T, Q_DIM, KV_DIM = (4, 512, 256, 192)
        HEADS, DIM_HEAD = (16, 64)
        INNER = HEADS * DIM_HEAD
        NUM_FRAMES, NUM_PATCHES = (8, 64)
        LN_EPS = 1e-05

        def diagonal_frame_mask(num_patches, num_frames):
            fid = np.repeat(np.arange(num_frames), num_patches)
            m = fid[:, None] == fid[None, :]
            return jnp.asarray(m[None, None])
        key = jax.random.key(seed)
        ks = jax.random.split(key, 6)
        s = lambda d: 1.0 / np.sqrt(d)
        return {'x': jax.random.normal(ks[0], (B, T, Q_DIM), jnp.float32), 'context': jax.random.normal(ks[1], (B, T, KV_DIM), jnp.float32), 'ln_gamma': jnp.ones((Q_DIM,), jnp.float32), 'ln_beta': jnp.zeros((Q_DIM,), jnp.float32), 'Wq': jax.random.normal(ks[2], (Q_DIM, INNER), jnp.float32) * s(Q_DIM), 'Wkv': jax.random.normal(ks[3], (KV_DIM, 2 * INNER), jnp.float32) * s(KV_DIM), 'Wo': jax.random.normal(ks[4], (INNER, Q_DIM), jnp.float32) * s(INNER), 'bo': jnp.zeros((Q_DIM,), jnp.float32), 'mask': diagonal_frame_mask(NUM_PATCHES, NUM_FRAMES)}
    _L1_xattn_all = _L1_xattn_setup()
    _L1_xattn_in = {k: v for k, v in _L1_xattn_all.items() if k in ('ln_gamma', 'ln_beta', 'Wq', 'Wkv', 'Wo', 'bo')}
    del _L1_xattn_all

    def _L1_ffn_setup():
        import jax, jax.numpy as jnp
        import numpy as np
        QMAX = 127.0

        def _ste_round(v):
            return v + jax.lax.stop_gradient(jnp.round(v) - v)

        def _act_fake_quant(x, clip_factor):
            scale = jax.nn.sigmoid(clip_factor) * jnp.max(jnp.abs(x)) / QMAX
            return jnp.clip(_ste_round(x / scale), -QMAX - 1.0, QMAX) * scale

        def _weight_fake_quant(w):
            scale = jnp.max(jnp.abs(w), axis=1, keepdims=True) / QMAX
            return jnp.clip(_ste_round(w / scale), -QMAX - 1.0, QMAX) * scale
        key = jax.random.key(seed)
        k1, k2, k3, k4 = jax.random.split(key, 4)
        B, S, H, I = (8, 2048, 256, 704)
        return {'x': jax.random.normal(k1, (B, S, H), dtype=jnp.float32), 'clip_x': jnp.full((1,), 4.0, dtype=jnp.float32), 'clip_down': jnp.full((1,), 4.0, dtype=jnp.float32), 'w_gate': jax.random.normal(k2, (I, H), dtype=jnp.float32) * 0.02, 'w_up': jax.random.normal(k3, (I, H), dtype=jnp.float32) * 0.02, 'w_down': jax.random.normal(k4, (H, I), dtype=jnp.float32) * 0.02}
    _L1_ffn_all = _L1_ffn_setup()
    _L1_ffn_in = {k: v for k, v in _L1_ffn_all.items() if k in ('clip_x', 'clip_down', 'w_gate', 'w_up', 'w_down')}
    del _L1_ffn_all
    return {'x': x, 'ctx_768': ctx_768, 'mask_1x1xSxS2_bk0': mask_1x1xSxS2_bk0, 'L0_xattn_Wq': _L0_xattn_in['Wq'], 'L0_xattn_Wk': _L0_xattn_in['Wk'], 'L0_xattn_Wv': _L0_xattn_in['Wv'], 'L0_xattn_Wo': _L0_xattn_in['Wo'], 'L0_xattn_bo': _L0_xattn_in['bo'], 'L0_ffn_gate_w': _L0_ffn_in['gate_w'], 'L0_ffn_gate_b': _L0_ffn_in['gate_b'], 'L0_ffn_up_w': _L0_ffn_in['up_w'], 'L0_ffn_up_b': _L0_ffn_in['up_b'], 'L0_ffn_gp_w': _L0_ffn_in['gp_w'], 'L0_ffn_gp_b': _L0_ffn_in['gp_b'], 'L0_ffn_down_w': _L0_ffn_in['down_w'], 'L0_ffn_down_b': _L0_ffn_in['down_b'], 'L1_xattn_ln_gamma': _L1_xattn_in['ln_gamma'], 'L1_xattn_ln_beta': _L1_xattn_in['ln_beta'], 'L1_xattn_Wq': _L1_xattn_in['Wq'], 'L1_xattn_Wkv': _L1_xattn_in['Wkv'], 'L1_xattn_Wo': _L1_xattn_in['Wo'], 'L1_xattn_bo': _L1_xattn_in['bo'], 'L1_ffn_clip_x': _L1_ffn_in['clip_x'], 'L1_ffn_clip_down': _L1_ffn_in['clip_down'], 'L1_ffn_w_gate': _L1_ffn_in['w_gate'], 'L1_ffn_w_up': _L1_ffn_in['w_up'], 'L1_ffn_w_down': _L1_ffn_in['w_down']}

def reference(x, ctx_768, mask_1x1xSxS2_bk0, L0_xattn_Wq, L0_xattn_Wk, L0_xattn_Wv, L0_xattn_Wo, L0_xattn_bo, L0_ffn_gate_w, L0_ffn_gate_b, L0_ffn_up_w, L0_ffn_up_b, L0_ffn_gp_w, L0_ffn_gp_b, L0_ffn_down_w, L0_ffn_down_b, L1_xattn_ln_gamma, L1_xattn_ln_beta, L1_xattn_Wq, L1_xattn_Wkv, L1_xattn_Wo, L1_xattn_bo, L1_ffn_clip_x, L1_ffn_clip_down, L1_ffn_w_gate, L1_ffn_w_up, L1_ffn_w_down):
    import jax
    import jax.numpy as jnp

    def _L0_xattn_ref(x, context, Wq, Wk, Wv, Wo, bo):
        import jax, jax.numpy as jnp
        import numpy as np
        B, N, M = (8, 1024, 77)
        Q_DIM, CTX_DIM = (256, 192)
        H, D = (16, 64)
        INNER = H * D
        scale = D ** (-0.5)

        def heads(t):
            b, s, _ = t.shape
            return t.reshape(b, s, H, D).transpose(0, 2, 1, 3)
        q = heads(x @ Wq)
        k = heads(context @ Wk)
        v = heads(context @ Wv)
        scores = jnp.einsum('bhid,bhjd->bhij', q, k) * scale
        attn = jax.nn.softmax(scores, axis=-1)
        out = jnp.einsum('bhij,bhjd->bhid', attn, v)
        out = out.transpose(0, 2, 1, 3).reshape(x.shape[0], x.shape[1], INNER)
        return out @ Wo + bo

    def _L0_ffn_ref(x, gate_w, gate_b, up_w, up_b, gp_w, gp_b, down_w, down_b):
        import jax, jax.numpy as jnp
        import numpy as np
        from jax import lax
        B, S, D = (4, 512, 256)
        E = 8
        K = 2
        F = 816
        NORM_TOPK = True
        bs, slen, dim = x.shape
        xf = x.reshape(-1, dim)
        N = xf.shape[0]
        scores = jax.nn.softmax(xf @ gate_w.T + gate_b, axis=-1)
        top_w, top_idx = lax.top_k(scores, K)
        if NORM_TOPK:
            top_w = top_w / (top_w.sum(-1, keepdims=True) + 1e-20)
        comb = jnp.zeros((N, E), xf.dtype).at[jnp.arange(N)[:, None], top_idx].add(top_w)

        def step(acc, p):
            uw, ub, gw, gb, dw, db, w = p
            h = jax.nn.silu((xf @ gw.T + gb) * (xf @ uw.T + ub))
            return (acc + w[:, None] * (h @ dw.T + db), None)
        y0 = jnp.zeros_like(xf)
        y, _ = lax.scan(step, y0, (up_w, up_b, gp_w, gp_b, down_w, down_b, comb.T))
        return y.reshape(bs, slen, dim)

    def _L1_xattn_ref(x, context, ln_gamma, ln_beta, Wq, Wkv, Wo, bo, mask):
        import jax, jax.numpy as jnp
        import numpy as np
        B, T, Q_DIM, KV_DIM = (4, 512, 256, 192)
        HEADS, DIM_HEAD = (16, 64)
        INNER = HEADS * DIM_HEAD
        NUM_FRAMES, NUM_PATCHES = (8, 64)
        LN_EPS = 1e-05

        def diagonal_frame_mask(num_patches, num_frames):
            fid = np.repeat(np.arange(num_frames), num_patches)
            m = fid[:, None] == fid[None, :]
            return jnp.asarray(m[None, None])
        mu = jnp.mean(x, axis=-1, keepdims=True)
        var = jnp.mean(jnp.square(x - mu), axis=-1, keepdims=True)
        xn = (x - mu) * jax.lax.rsqrt(var + LN_EPS) * ln_gamma + ln_beta
        scale = DIM_HEAD ** (-0.5)
        q = xn @ Wq
        kv = context @ Wkv
        k, v = jnp.split(kv, 2, axis=-1)
        split_heads = lambda t: t.reshape(t.shape[0], t.shape[1], HEADS, DIM_HEAD).transpose(0, 2, 1, 3)
        q, k, v = (split_heads(q), split_heads(k), split_heads(v))
        dots = jnp.einsum('bhnd,bhmd->bhnm', q, k) * scale
        dots = jnp.where(mask, dots, -jnp.inf)
        attn = jax.nn.softmax(dots, axis=-1)
        out = jnp.einsum('bhnm,bhmd->bhnd', attn, v)
        out = out.transpose(0, 2, 1, 3).reshape(x.shape[0], x.shape[1], INNER)
        return out @ Wo + bo

    def _L1_ffn_ref(x, clip_x, clip_down, w_gate, w_up, w_down):
        import jax, jax.numpy as jnp
        import numpy as np
        QMAX = 127.0

        def _ste_round(v):
            return v + jax.lax.stop_gradient(jnp.round(v) - v)

        def _act_fake_quant(x, clip_factor):
            scale = jax.nn.sigmoid(clip_factor) * jnp.max(jnp.abs(x)) / QMAX
            return jnp.clip(_ste_round(x / scale), -QMAX - 1.0, QMAX) * scale

        def _weight_fake_quant(w):
            scale = jnp.max(jnp.abs(w), axis=1, keepdims=True) / QMAX
            return jnp.clip(_ste_round(w / scale), -QMAX - 1.0, QMAX) * scale
        xq = _act_fake_quant(x, clip_x[0])
        gate = jnp.einsum('bsh,ih->bsi', xq, _weight_fake_quant(w_gate))
        up = jnp.einsum('bsh,ih->bsi', xq, _weight_fake_quant(w_up))
        h = _act_fake_quant(jax.nn.silu(gate) * up, clip_down[0])
        return jnp.einsum('bsi,hi->bsh', h, _weight_fake_quant(w_down))
    x = x + _L0_xattn_ref(_layernorm(x, axis=-1), ctx_768, L0_xattn_Wq, L0_xattn_Wk, L0_xattn_Wv, L0_xattn_Wo, L0_xattn_bo)
    x = x + _L0_ffn_ref(_layernorm(x, axis=-1), L0_ffn_gate_w, L0_ffn_gate_b, L0_ffn_up_w, L0_ffn_up_b, L0_ffn_gp_w, L0_ffn_gp_b, L0_ffn_down_w, L0_ffn_down_b)
    x = x + _L1_xattn_ref(_layernorm(x, axis=-1), ctx_768, L1_xattn_ln_gamma, L1_xattn_ln_beta, L1_xattn_Wq, L1_xattn_Wkv, L1_xattn_Wo, L1_xattn_bo, mask_1x1xSxS2_bk0)
    x = x + _L1_ffn_ref(_layernorm(x, axis=-1), L1_ffn_clip_x, L1_ffn_clip_down, L1_ffn_w_gate, L1_ffn_w_up, L1_ffn_w_down)
    return x

_drawn_inputs = setup_inputs


def setup_inputs(seed=0):
    import zlib

    import numpy as np

    out = dict(_drawn_inputs(seed))
    spreads = {'L0_ffn_gate_b': (0.0, 0.1),
     'L0_ffn_up_b': (0.0, 0.8),
     'L0_ffn_gp_b': (0.0, 0.8),
     'L0_ffn_down_b': (0.0, 0.1),
     'L1_xattn_ln_gamma': (1.0, 0.569),
     'L1_xattn_ln_beta': (0.0, 0.394),
     'L1_xattn_bo': (0.0, 0.1)}
    factors = {'L0_xattn_bo': 5.872,
     'L0_ffn_up_w': 3.177,
     'L0_ffn_gp_w': 3.188,
     'L0_ffn_down_w': 3.019,
     'L1_ffn_w_gate': 3.789,
     'L1_ffn_w_up': 3.704,
     'L1_ffn_w_down': 3.693}
    for name, (base, spread) in spreads.items():
        noise = np.random.default_rng([zlib.crc32(name.encode()), seed]).standard_normal(out[name].shape)
        drawn = base * np.exp(spread * noise) if base else spread * noise
        out[name] = jnp.asarray(drawn.astype(out[name].dtype))
    for name, factor in factors.items():
        out[name] = (out[name] * factor).astype(out[name].dtype)
    return out
```

```python
from contextlib import ExitStack

import numpy as np

import concourse.bass as bass
from concourse import mybir

F32 = mybir.dt.float32
F16 = mybir.dt.float16
ALU = mybir.AluOpType
ACT = mybir.ActivationFunctionType
AX = mybir.AxisListType

P = 128
BATCH, SEQ, DIM = 32, 100, 256
KEYS, CTX = 361, 192
HEADS, HEAD = 16, 64
INNER = HEADS * HEAD
PAIRS = HEADS // 2
KEY_TILES = 3
LAST_KEYS = KEYS - 2 * P
TOKENS = BATCH * SEQ
LN_EPS = 1e-5

X_SCALE = 64.0
CTX_SCALE = 64.0
W_SCALE = 256.0
QK_SCALE = 16.0
Q_EVAC = QK_SCALE / (X_SCALE * W_SCALE)
K_EVAC = QK_SCALE / (CTX_SCALE * W_SCALE)
V_EVAC = 1.0 / (CTX_SCALE * W_SCALE)
SCORE_SCALE = HEAD ** -0.5 / (QK_SCALE * QK_SCALE)
MASKED = -1e30

T_LAG, AV_LAG = 3, 4
O_STEP, XT_STEP = 5, 6
K_JOBS, Q_JOBS, V_JOBS = 8, 2, 6


def attention_phase(nc, name, x_in, x_out, ctx_main, ctx_rem, wq, wk_main, wk_rem, wv_main, wv_rem, wo,
                    bo_row, identity, mask=None, gamma=None, beta=None):
    second_ln = gamma is not None
    LNS = 2 if second_ln else 1
    with ExitStack() as ctx:
        def sb(label, shape, dt):
            return ctx.enter_context(nc.sbuf_tensor(f"{name}_{label}", shape, dt))

        def sem(label):
            return ctx.enter_context(nc.semaphore(f"{name}_{label}"))

        w_stage = sb("w_stage", [P, 2, 2 * INNER], F32)
        wq_hi, wq_lo = sb("wq_hi", [P, 2 * INNER], F16), sb("wq_lo", [P, 2 * INNER], F16)
        wkv_hi = sb("wkv_hi", [P, 2, INNER], F16)
        wkv_lo = sb("wkv_lo", [P, 2, INNER], F16)
        wkv_rem_hi = sb("wkv_rem_hi", [P, 2, INNER], F16)
        wkv_rem_lo = sb("wkv_rem_lo", [P, 2, INNER], F16)
        wo_sb = sb("wo", [P, PAIRS, DIM], F32)
        bo_sb = sb("bo", [SEQ, DIM], F32)
        ident = sb("ident", [P, P], F32)
        expo = sb("expo", [SEQ, 1], F32)
        if second_ln:
            gb = sb("gb", [P, 2, 2], F32)
            gbs = sb("gbs", [P, 2, 2], F32)
            maskb = sb("maskb", [SEQ, KEYS], F32)
            mask_in = sb("mask_in", [SEQ, KEYS], mask.dtype)
            masked = sb("masked", [SEQ, 2, KEYS], F32)

        x_sb = sb("x", [SEQ, 2, DIM], F32)
        xb = sb("xb", [SEQ, 2, DIM], F32)
        xn = sb("xn", [SEQ, LNS, DIM], F32)
        stats = sb("stats", [SEQ, LNS, 6], F32)
        mv = sb("mv", [SEQ, LNS, 2], F32)
        veps = sb("veps", [SEQ, LNS], F32)
        rstd = sb("rstd", [SEQ, LNS], F32)
        c_main = sb("c_main", [P, 2, KEYS], F32)
        c_rem = sb("c_rem", [P, 2, KEYS], F32)
        c_hi = sb("c_hi", [P, 2, KEYS], F16)
        c_lo = sb("c_lo", [P, 2, KEYS], F16)
        c_stack = sb("c_stack", [P, 2, KEYS], F16)
        xt32 = sb("xt32", [P, 2 * SEQ], F32)
        xt_hi, xt_lo = sb("xt_hi", [P, 2 * SEQ], F16), sb("xt_lo", [P, 2 * SEQ], F16)
        k_stack = sb("k_stack", [P, 2, HEADS, KEYS], F16)
        q_hi = sb("q_hi", [P, 2, 2, PAIRS * SEQ], F16)
        q_lo = sb("q_lo", [P, 2, PAIRS * SEQ], F16)
        v_sb = sb("v", [P, 2, KEY_TILES, INNER], F32)
        probs = sb("probs", [SEQ, 4, KEY_TILES * P], F32)
        rowmax = sb("rowmax", [SEQ, HEADS], F32)
        bias = sb("bias", [SEQ, HEADS], F32)
        rowsum = sb("rowsum", [SEQ, HEADS], F32)
        rinv = sb("rinv", [SEQ, HEADS], F32)
        pt_sb = sb("pt", [P, 2, KEY_TILES * SEQ], F32)
        ot_sb = sb("ot", [P, PAIRS * SEQ], F32)
        out_sb = sb("out", [SEQ, 2, DIM], F32)

        def bank(label):
            return ctx.enter_context(nc.psum_tensor(f"{name}_{label}", [P, 512], F32))

        score_ps = [bank(f"score{i}") for i in range(2)]
        ring_ps = [bank(f"ring{i}") for i in range(2)]
        pt_ps = [bank(f"ptps{i}") for i in range(2)]
        av_ps = [bank(f"av{i}") for i in range(2)]

        const_in = sem("const_in")
        stage_in = [sem(f"stage_in{i}") for i in range(2)]
        stage_hi, stage_lo = sem("stage_hi"), sem("stage_lo")
        consts_ready = sem("consts_ready")
        carried = sem("carried")
        mask_step = sem("mask_step")
        x_landed = [sem(f"x_landed{i}") for i in range(2)]
        c_landed = [sem(f"c_landed{i}") for i in range(2)]
        stored = [sem(f"stored{i}") for i in range(2)]
        ln_stats, ln_aggr, ln_eps, ln_rstd, xn_ready = (sem(s) for s in ("ln_stats", "ln_aggr", "ln_eps", "ln_rstd", "xn_ready"))
        xb_ready, c_scaled, c_his, c_los, c_ready = (sem(s) for s in ("xb_ready", "c_scaled", "c_his", "c_los", "c_ready"))
        xth_ready, xt_ready = sem("xth_ready"), sem("xt_ready")
        ring_full = [sem(f"ring_full{i}") for i in range(2)]
        ring_free = [sem(f"ring_free{i}") for i in range(2)]
        hi_done = sem("hi_done")
        score_full, max_done, bias_done, exp_done = (sem(s) for s in ("score_full", "max_done", "bias_done", "exp_done"))
        rinv_done, norm_done, pt_full, pt_done = (sem(s) for s in ("rinv_done", "norm_done", "pt_full", "pt_done"))
        av_full, ot_done = sem("av_full"), sem("ot_done")

        JOBS = [("k", j) for j in range(K_JOBS)] + [("q", j) for j in range(Q_JOBS)] + [("v", j) for j in range(V_JOBS)]
        PER_BODY = len(JOBS) + 2

        def step_slots(s, project, output):
            out = [JOBS[s]] if project else []
            if output and s == O_STEP:
                out.append(("o", 0))
            if project and s == XT_STEP:
                out.append(("xt", 0))
            return out

        def slot_number(b, slot, kind):
            if kind == "prologue":
                n = ([("xt", 0)] + JOBS).index(slot)
                return n % 2, n // 2
            base = len(JOBS) + 1
            if kind == "tail":
                n = base + PER_BODY * (BATCH - 1) - 1 + 1
                return n % 2, n // 2
            order = [x for s in range(HEADS) for x in step_slots(s, kind != "last", kind != "first")]
            n = base + order.index(slot)
            if kind != "first":
                n -= 1
            return n % 2, n // 2 + (PER_BODY // 2) * b

        def carry(eng):
            eng.sem_inc(carried, 1)

        def alone(eng, semaphore, value):
            eng.wait_ge(semaphore, value)
            if not isinstance(value, int):
                carry(eng)

        def wait_emptied(eng, b, slot, kind):
            bk, used = slot_number(b, slot, kind)
            eng.wait_ge(ring_free[bk], used + 1)

        def wait_projected(eng, b, slot):
            if isinstance(b, int) and b == 0:
                wait_emptied(eng, 0, slot, "prologue")
            else:
                wait_emptied(eng, b - 1, slot, "mid")

        last_b = BATCH - 1

        def wait_output(eng, b, kind):
            wait_emptied(eng, b + 1, ("o", 0), kind)

        def each_batch(eng, body):
            body(0, 0, 0, "first")
            with eng.Fori(0, (BATCH - 4) // 2) as i:
                body(2 * i + 1, 1, i, "mid")
                body(2 * i + 2, 0, i + 1, "mid")
            body(BATCH - 3, 1, (BATCH - 3) // 2, "mid")
            body(BATCH - 2, 0, (BATCH - 2) // 2, "penultimate")
            body(BATCH - 1, 1, (BATCH - 1) // 2, "last")

        with nc.Block() as block:

            @block.sync
            def _(sp):
                def load_x(b, par, half, reuse):
                    if reuse:
                        sp.wait_ge(xb_ready, b - 1)
                        carry(sp)
                        sp.wait_ge(xn_ready, LNS * (b - 1))
                        carry(sp)
                    sp.dma_start(x_sb[:, par, :], x_in[bass.ds(b * SEQ, SEQ), :]).then_inc(x_landed[par], 16)

                def load_c(b, par, half, reuse):
                    if reuse:
                        sp.wait_ge(c_ready, b - 1)
                        carry(sp)
                        sp.wait_ge(c_los, b - 1)
                        carry(sp)
                    sp.dma_start(c_main[:, par, :], ctx_main[:, bass.ds(b * KEYS, KEYS)]).then_inc(c_landed[par], 16)
                    sp.dma_start(c_rem[:, par, :], ctx_rem[:, bass.ds(b * KEYS, KEYS)]).then_inc(c_landed[par], 16)

                def store(b, par, half, kind="mid"):
                    wait_output(sp, b, kind)
                    carry(sp)
                    sp.dma_start(x_out[bass.ds(b * SEQ, SEQ), :], out_sb[:, par, :]).then_inc(stored[par], 16)

                sp.dma_start(ident[:, :], identity).then_inc(const_in, 16)
                sp.dma_start(w_stage[:, 0, :], wq).then_inc(stage_in[0], 16)
                load_c(0, 0, 0, False)
                load_x(0, 0, 0, False)
                sp.dma_start(w_stage[:, 1, 0:INNER], wk_main).then_inc(stage_in[1], 16)
                sp.dma_start(w_stage[:, 1, INNER:2 * INNER], wv_main).then_inc(stage_in[1], 16)
                if second_ln:
                    sp.dma_start(gb[:, 0, :], gamma).then_inc(const_in, 16)
                    sp.dma_start(gb[:, 1, :], beta).then_inc(const_in, 16)
                    sp.dma_start(mask_in[:, :], mask).then_inc(const_in, 16)
                sp.dma_start(bo_sb[:, :], bo_row.to_broadcast([SEQ, DIM])).then_inc(const_in, 16)
                sp.dma_start(wo_sb[:, :, :], wo).then_inc(const_in, 16)
                load_c(1, 1, 0, False)
                load_x(1, 1, 0, False)
                sp.wait_ge(stage_lo, 1)
                sp.dma_start(w_stage[:, 0, 0:INNER], wk_rem).then_inc(stage_in[0], 16)
                sp.dma_start(w_stage[:, 0, INNER:2 * INNER], wv_rem).then_inc(stage_in[0], 16)

                def body(b, par, half, kind):
                    if kind != "last":
                        load_later(b + 2, par, half + 1)
                    if kind != "first":
                        store(b - 1, 1 - par, half - 1 if par == 0 else half)

                def load_later(b, par, half):
                    load_x(b, par, half, True)
                    load_c(b, par, half, True)

                body(0, 0, 0, "first")
                with sp.Fori(0, (BATCH - 4) // 2) as i:
                    body(2 * i + 1, 1, i, "mid")
                    body(2 * i + 2, 0, i + 1, "mid")
                body(BATCH - 3, 1, 0, "mid")
                store(BATCH - 3, 1, 0)
                store(BATCH - 2, 0, 0, "last")
                store(BATCH - 1, 1, 0, "tail")
                for par in range(2):
                    sp.wait_ge(stored[par], 16 * (BATCH // 2))

            @block.gpsimd
            def _(pool):
                def rstds(n, ln):
                    k = LNS * n + ln
                    alone(pool, ln_aggr, k + 1)
                    nc.gpsimd.tensor_scalar(veps[:, ln:ln + 1], mv[:, ln, 1:2], LN_EPS, None, ALU.add).then_inc(ln_eps, 1)
                    pool.wait_ge(ln_eps, k + 1)
                    nc.gpsimd.tensor_tensor(rstd[:, ln:ln + 1], veps[:, ln:ln + 1], expo[:, :], ALU.pow).then_inc(ln_rstd, 1)

                def add_bias(n, par, reuse):
                    if reuse:
                        wait_output(pool, n - 2, "mid")
                    nc.gpsimd.tensor_tensor(xb[:, par, :], x_sb[:, par, :], bo_sb[:, :], ALU.add).then_inc(xb_ready, 1)

                def scale_context(n, par, half, reuse):
                    if reuse:
                        pool.wait_ge(score_full, HEADS * (n - 2) + 1)
                    alone(pool, c_landed[par], 32 * half + 32)
                    nc.gpsimd.tensor_scalar(c_main[:, par, :], c_main[:, par, :], CTX_SCALE, 1.0, ALU.mult, ALU.mult)
                    nc.gpsimd.tensor_scalar(c_rem[:, par, :], c_rem[:, par, :], CTX_SCALE, 1.0, ALU.mult, ALU.mult).then_inc(c_scaled, 1)

                def context_lo(n, par):
                    pool.wait_ge(c_his, n + 1)
                    nc.gpsimd.tensor_tensor(c_lo[:, par, :], c_main[:, par, :], c_hi[:, par, :], ALU.subtract).then_inc(c_los, 1)

                def split_xt(n):
                    wait_projected(pool, n, ("xt", 0))
                    carry(pool)
                    nc.gpsimd.tensor_copy(xt_hi[:, :], xt32[:, :]).then_inc(xth_ready, 1)
                    pool.wait_ge(xth_ready, n + 1)
                    nc.gpsimd.tensor_tensor(xt_lo[:, :], xt32[:, :], xt_hi[:, :], ALU.subtract).then_inc(xt_ready, 1)

                def normalise(b, h):
                    alone(pool, rinv_done, HEADS * b + h + 1)
                    nc.gpsimd.tensor_scalar(probs[:, h % 4, 0:KEYS], probs[:, h % 4, 0:KEYS], rinv[:, h:h + 1], 1.0,
                                            ALU.mult, ALU.mult).then_inc(norm_done, 1)

                nc.gpsimd.memset(expo[:, :], -0.5).then_inc(consts_ready, 1)
                nc.gpsimd.memset(probs[:, :, KEYS:KEY_TILES * P], 0.0).then_inc(consts_ready, 1)
                pool.wait_ge(consts_ready, 2)
                scale_context(0, 0, 0, False)
                context_lo(0, 0)
                for ln in range(LNS):
                    rstds(0, ln)
                pool.wait_ge(const_in, 16 * (6 if second_ln else 3))
                if second_ln:
                    nc.gpsimd.tensor_scalar(gbs[:, :, :].rearrange("p a b -> p (a b)"), gb[:, :, :].rearrange("p a b -> p (a b)"),
                                            X_SCALE, 1.0, ALU.mult, ALU.mult).then_inc(consts_ready, 1)
                    nc.gpsimd.tensor_copy(maskb[:, :], mask_in[:, :]).then_inc(mask_step, 1)
                    pool.wait_ge(mask_step, 1)
                    nc.gpsimd.tensor_scalar(maskb[:, :], maskb[:, :], -MASKED, MASKED, ALU.mult, ALU.add).then_inc(mask_step, 1)
                add_bias(0, 0, False)
                split_xt(0)
                scale_context(1, 1, 0, False)
                context_lo(1, 1)

                def body(b, par, half, kind):
                    if kind != "first":
                        normalise(b - 1, HEADS - 1)
                    for s in range(HEADS):
                        if s >= 1:
                            normalise(b, s - 1)
                        if kind == "last":
                            continue
                        if s == 1:
                            rstds(b + 1, 0)
                        if s == 3 and second_ln:
                            rstds(b + 1, 1)
                        if s == XT_STEP + 1:
                            split_xt(b + 1)
                        if s == 10:
                            add_bias(b + 1, 1 - par, kind != "first")
                        if kind in ("first", "mid"):
                            if s == 2:
                                scale_context(b + 2, par, half + 1, True)
                            if s == 4:
                                context_lo(b + 2, par)

                each_batch(pool, body)
                normalise(BATCH - 1, HEADS - 1)

            @block.scalar
            def _(act):
                def context_hi(n, par):
                    alone(act, c_scaled, n + 1)
                    nc.scalar.activation(c_hi[:, par, :], c_main[:, par, :], ACT.Copy)
                    nc.scalar.activation(c_stack[:, par, :], c_rem[:, par, :], ACT.Copy).then_inc(c_his, 1)

                context_hi(0, 0)
                for k, (src, dst) in enumerate(((0, wq_hi), (1, wkv_hi), (0, wkv_rem_hi))):
                    act.wait_ge(stage_in[src], (16, 32, 48)[k])
                    flat = dst[:, :] if k == 0 else dst[:, :, :].rearrange("p a b -> p (a b)")
                    nc.scalar.activation(flat, w_stage[:, src, :], ACT.Copy, scale=W_SCALE).then_inc(stage_hi, 1)

                def evac_xt(n, kind, b):
                    bk, used = slot_number(b, ("xt", 0), kind)
                    act.wait_ge(ring_full[bk], used + 1)
                    if kind == "prologue":
                        if second_ln:
                            act.wait_ge(consts_ready, 3)
                    else:
                        act.wait_ge(xt_ready, n)
                    if second_ln:
                        for t in range(2):
                            last = nc.scalar.activation(xt32[:, t * SEQ:(t + 1) * SEQ], ring_ps[bk][:, t * SEQ:(t + 1) * SEQ],
                                                        ACT.Identity, scale=gbs[:, 0, t:t + 1], bias=gbs[:, 1, t:t + 1])
                    else:
                        last = nc.scalar.activation(xt32[:, :], ring_ps[bk][:, 0:2 * SEQ], ACT.Copy, scale=X_SCALE)
                    last.then_inc(ring_free[bk], 1)

                def job(n, par, slot, kind, b):
                    what, j = slot
                    bk, used = slot_number(b, slot, kind)
                    act.wait_ge(ring_full[bk], used + 1)
                    if what == "k":
                        for r in range(2):
                            rows = slice(HEAD * r, HEAD * r + HEAD)
                            last = nc.scalar.activation(k_stack[rows, par, 2 * j + r, :], ring_ps[bk][rows, 0:KEYS],
                                                        ACT.Copy, scale=K_EVAC)
                            last.then_inc(hi_done, 1)
                    if what == "q":
                        cols = slice(4 * SEQ * j, 4 * SEQ * (j + 1))
                        for r in range(2):
                            for half_rows in range(2):
                                last = nc.scalar.activation(q_hi[HEAD * half_rows:HEAD * (half_rows + 1), par, r, cols],
                                                            ring_ps[bk][HEAD * r:HEAD * (r + 1), 0:4 * SEQ],
                                                            ACT.Copy, scale=Q_EVAC)
                        last.then_inc(hi_done, 2)
                    if what == "v":
                        t, c = j // 2, j % 2
                        rows = LAST_KEYS if t == 2 else P
                        last = nc.scalar.activation(v_sb[0:rows, par, t, 512 * c:512 * (c + 1)], ring_ps[bk][0:rows, :],
                                                    ACT.Copy, scale=V_EVAC)
                        last.then_inc(ring_free[bk], 1)

                def exp(b, h):
                    act.wait_ge(bias_done, HEADS * b + h + 1)
                    if not (isinstance(b, int) and b == 0 and h < 4):
                        act.wait_ge(pt_full, HEADS * b + h - 3)
                    src = masked[:, h % 2, :] if second_ln else score_ps[h % 2][0:SEQ, 0:KEYS]
                    nc.scalar.activation(probs[:, h % 4, 0:KEYS], src, ACT.Exp, scale=SCORE_SCALE, bias=bias[:, h:h + 1],
                                         accum_out=rowsum[:, h:h + 1]).then_inc(exp_done, 1)

                def evac_av(b, c):
                    act.wait_ge(av_full, HEADS * b + 8 * (c + 1))
                    nc.scalar.activation(ot_sb[:, 4 * SEQ * c:4 * SEQ * (c + 1)], av_ps[c][:, 0:4 * SEQ], ACT.Copy).then_inc(ot_done, 1)

                act.wait_ge(consts_ready, 2)
                evac_xt(0, "prologue", 0)
                for slot in JOBS:
                    job(0, 0, slot, "prologue", 0)
                context_hi(1, 1)

                def body(b, par, half, kind):
                    for s in range(HEADS):
                        for slot in step_slots(s, kind != "last", kind != "first"):
                            if slot[0] == "xt":
                                evac_xt(b + 1, kind, b)
                            elif slot[0] != "o":
                                job(b + 1, 1 - par, slot, kind, b)
                        exp(b, s)
                        if s == 3 and kind in ("first", "mid"):
                            context_hi(b + 2, par)
                        if kind != "first" and s == AV_LAG - 1:
                            evac_av(b - 1, 1)
                        if s == 8 + AV_LAG - 1:
                            evac_av(b, 0)

                each_batch(act, body)
                evac_av(last_b, 1)

            @block.vector
            def _(dve):
                def split_weights(k, src, hi, lo):
                    dve.wait_ge(stage_hi, k + 1)
                    flat_hi = hi[:, :] if k == 0 else hi[:, :, :].rearrange("p a b -> p (a b)")
                    flat_lo = lo[:, :] if k == 0 else lo[:, :, :].rearrange("p a b -> p (a b)")
                    nc.vector.scalar_tensor_tensor(flat_lo, w_stage[:, src, :], W_SCALE, flat_hi, ALU.mult,
                                                   ALU.subtract).then_inc(stage_lo, 1)

                def layernorm_stats(n, par, half):
                    dve.wait_ge(x_landed[par], 16 * half + 16)
                    nc.vector.bn_stats(stats[:, 0, :], x_sb[:, par, :]).then_inc(ln_stats, 1)
                    alone(dve, ln_stats, LNS * n + 1)
                    nc.vector.bn_aggr(mv[:, 0, :], stats[:, 0, :]).then_inc(ln_aggr, 1)

                def layernorm_apply(n, par):
                    dve.wait_ge(ln_rstd, LNS * n + 1)
                    nc.vector.tensor_scalar(xn[:, 0, :], x_sb[:, par, :], mv[:, 0, 0:1], rstd[:, 0:1], ALU.subtract,
                                            ALU.mult).then_inc(xn_ready, 1)
                    if second_ln:
                        dve.wait_ge(xn_ready, LNS * n + 1)
                        nc.vector.bn_stats(stats[:, 1, :], xn[:, 0, :]).then_inc(ln_stats, 1)
                        alone(dve, ln_stats, LNS * n + 2)
                        nc.vector.bn_aggr(mv[:, 1, :], stats[:, 1, :]).then_inc(ln_aggr, 1)

                def layernorm_apply2(n):
                    dve.wait_ge(ln_rstd, LNS * n + 2)
                    nc.vector.tensor_scalar(xn[:, 1, :], xn[:, 0, :], mv[:, 1, 0:1], rstd[:, 1:2], ALU.subtract,
                                            ALU.mult).then_inc(xn_ready, 1)

                hi_per_batch = 2 * (K_JOBS + Q_JOBS)

                def job(n, par, slot, kind, b):
                    what, j = slot
                    bk, used = slot_number(b, slot, kind)
                    at = JOBS.index(slot)
                    for r in range(2):
                        rows, other = slice(HEAD * r, HEAD * r + HEAD), slice(HEAD * (1 - r), HEAD * (2 - r))
                        dve.wait_ge(hi_done, hi_per_batch * n + 2 * at + (r + 1 if what == "k" else 2))
                        if what == "k":
                            last = nc.vector.scalar_tensor_tensor(k_stack[other, par, 2 * j + r, :], ring_ps[bk][rows, 0:KEYS], K_EVAC,
                                                                  k_stack[rows, par, 2 * j + r, :], ALU.mult, ALU.subtract)
                        else:
                            cols = slice(4 * SEQ * j, 4 * SEQ * (j + 1))
                            last = nc.vector.scalar_tensor_tensor(q_lo[rows, par, cols], ring_ps[bk][rows, 0:4 * SEQ], Q_EVAC,
                                                                  q_hi[rows, par, r, cols], ALU.mult, ALU.subtract)
                    last.then_inc(ring_free[bk], 1)

                def row_max(b, h):
                    dve.wait_ge(score_full, HEADS * b + h + 1)
                    src = score_ps[h % 2][0:SEQ, 0:KEYS]
                    if second_ln:
                        if not (isinstance(b, int) and b == 0 and h < 2):
                            dve.wait_ge(exp_done, HEADS * b + h - 1)
                        carry(dve)
                        nc.vector.tensor_tensor_reduce(masked[:, h % 2, :], src, maskb[:, :], 1.0, -3.0e38, ALU.add, ALU.max,
                                                       rowmax[:, h:h + 1]).then_inc(max_done, 1)
                    else:
                        nc.vector.reduce_max(rowmax[:, h:h + 1], src, AX.X).then_inc(max_done, 1)
                    dve.wait_ge(max_done, HEADS * b + h + 1)
                    nc.vector.tensor_scalar(bias[:, h:h + 1], rowmax[:, h:h + 1], -SCORE_SCALE, None, ALU.mult).then_inc(bias_done, 1)

                def invert(b, h):
                    dve.wait_ge(exp_done, HEADS * b + h + 1)
                    nc.vector.reciprocal(rinv[:, h:h + 1], rowsum[:, h:h + 1]).then_inc(rinv_done, 1)

                def evac_pt(b, h):
                    dve.wait_ge(pt_full, HEADS * b + h + 1)
                    if not (isinstance(b, int) and b == 0 and h < 2):
                        dve.wait_ge(av_full, HEADS * b + h - 1)
                    nc.vector.tensor_copy(pt_sb[:, h % 2, :], pt_ps[h % 2][:, 0:KEY_TILES * SEQ]).then_inc(pt_done, 1)

                def output_sum(b, par, half, kind, body_b):
                    bk, used = slot_number(body_b, ("o", 0), kind)
                    dve.wait_ge(ring_full[bk], used + 1)
                    dve.wait_ge(xb_ready, b + 1)
                    dve.wait_ge(stored[par], 16 * half)
                    nc.vector.tensor_tensor(out_sb[:, par, :], ring_ps[bk][0:SEQ, 0:DIM], xb[:, par, :],
                                            ALU.add).then_inc(ring_free[bk], 1)

                def context_stack_lo(n, par):
                    alone(dve, c_his, n + 1)
                    nc.vector.tensor_tensor(c_stack[HEAD:P, par, :], c_rem[HEAD:P, par, :], c_stack[HEAD:P, par, :],
                                            ALU.subtract).then_inc(c_ready, 1)

                layernorm_stats(0, 0, 0)
                context_stack_lo(0, 0)
                split_weights(0, 0, wq_hi, wq_lo)
                dve.wait_ge(consts_ready, 2)
                layernorm_apply(0, 0)
                split_weights(1, 1, wkv_hi, wkv_lo)
                if second_ln:
                    layernorm_apply2(0)
                    dve.wait_ge(mask_step, 2)
                split_weights(2, 0, wkv_rem_hi, wkv_rem_lo)
                for slot in JOBS:
                    if slot[0] != "v":
                        job(0, 0, slot, "prologue", 0)
                context_stack_lo(1, 1)

                def body(b, par, half, kind):
                    late = []
                    for s in range(HEADS):
                        for slot in late:
                            if slot[0] in "kq":
                                job(b + 1, 1 - par, slot, kind, b)
                            if slot[0] == "o":
                                output_sum(b - 1, 1 - par, half if par == 1 else half - 1, kind, b)
                        late = step_slots(s, kind != "last", kind != "first")
                        row_max(b, s)
                        if s >= 1:
                            invert(b, s - 1)
                        elif kind != "first":
                            invert(b - 1, HEADS - 1)
                        if s >= T_LAG:
                            evac_pt(b, s - T_LAG)
                        elif kind != "first":
                            evac_pt(b - 1, HEADS + s - T_LAG)
                        if kind != "last":
                            if s == 0:
                                layernorm_stats(b + 1, 1 - par, half if par == 0 else half + 1)
                            if s == 2:
                                layernorm_apply(b + 1, 1 - par)
                            if s == 5 and kind != "penultimate":
                                context_stack_lo(b + 2, par)
                            if s == 4 and second_ln:
                                layernorm_apply2(b + 1)

                each_batch(dve, body)
                invert(last_b, HEADS - 1)
                for h in range(HEADS - T_LAG, HEADS):
                    evac_pt(last_b, h)
                output_sum(last_b, 1, last_b // 2, "tail", 0)

            @block.tensor
            def _(pe):
                def take_slot(slot, kind, b):
                    bk, used = slot_number(b, slot, kind)
                    if not (isinstance(used, int) and used == 0):
                        pe.wait_ge(ring_free[bk], used)
                    return bk

                def transpose_x(kind, n, b):
                    bk = take_slot(("xt", 0), kind, b)
                    pe.wait_ge(xn_ready, LNS * (n + 1))
                    for t in range(2):
                        last = nc.tensor.transpose(ring_ps[bk][:, t * SEQ:(t + 1) * SEQ], xn[:, LNS - 1, t * P:(t + 1) * P],
                                                   ident[0:SEQ, 0:SEQ])
                    last.then_inc(ring_full[bk], 1)

                def job(slot, par, kind, n, b):
                    what, j = slot
                    bk = take_slot(slot, kind, b)
                    if slot == ("k", 0):
                        pe.wait_ge(c_los, n + 1)
                        pe.wait_ge(c_ready, n + 1)
                    if slot == ("q", 0):
                        pe.wait_ge(xt_ready, n + 1)
                    if what == "k":
                        cols = slice(P * j, P * (j + 1))
                        out = ring_ps[bk][:, 0:KEYS]
                        nc.tensor.matmul(out, wkv_hi[:, 0, cols], c_hi[:, par, :], start=True, stop=False)
                        nc.tensor.matmul(out, wkv_hi[:, 0, cols], c_lo[:, par, :], start=False, stop=False)
                        nc.tensor.matmul(out, wkv_lo[:, 0, cols], c_hi[:, par, :], start=False, stop=False)
                        nc.tensor.matmul(out, wkv_rem_hi[:, 0, cols], c_stack[:, par, :], start=False, stop=False)
                        last = nc.tensor.matmul(out, wkv_rem_lo[0:HEAD, 0, cols], c_stack[0:HEAD, par, :], start=False, stop=True)
                    if what == "q":
                        for g in range(4):
                            out = ring_ps[bk][:, SEQ * g:SEQ * (g + 1)]
                            for t in range(2):
                                w = slice(INNER * t + P * (4 * j + g), INNER * t + P * (4 * j + g + 1))
                                xs = slice(SEQ * t, SEQ * (t + 1))
                                nc.tensor.matmul(out, wq_hi[:, w], xt_hi[:, xs], start=(t == 0), stop=False)
                                nc.tensor.matmul(out, wq_hi[:, w], xt_lo[:, xs], start=False, stop=False)
                                last = nc.tensor.matmul(out, wq_lo[:, w], xt_hi[:, xs], start=False, stop=(t == 1))
                    if what == "v":
                        t, c = j // 2, j % 2
                        rows = LAST_KEYS if t == 2 else P
                        keys, cols = slice(P * t, P * t + rows), slice(512 * c, 512 * (c + 1))
                        out = ring_ps[bk][0:rows, :]
                        nc.tensor.matmul(out, c_hi[:, par, keys], wkv_hi[:, 1, cols], start=True, stop=False)
                        nc.tensor.matmul(out, c_hi[:, par, keys], wkv_lo[:, 1, cols], start=False, stop=False)
                        nc.tensor.matmul(out, c_lo[:, par, keys], wkv_hi[:, 1, cols], start=False, stop=False)
                        nc.tensor.matmul(out, c_stack[:, par, keys], wkv_rem_hi[:, 1, cols], start=False, stop=False)
                        last = nc.tensor.matmul(out, c_stack[0:HEAD, par, keys], wkv_rem_lo[0:HEAD, 1, cols], start=False, stop=True)
                    last.then_inc(ring_full[bk], 1)

                def scores(b, par, h):
                    if h == 0:
                        wait_projected(pe, b, ("q", Q_JOBS - 1))
                    if not (isinstance(b, int) and b == 0 and h < 2):
                        pe.wait_ge(max_done if second_ln else exp_done, HEADS * b + h - 1)
                    j, r = h // 2, h % 2
                    rows, cols = slice(HEAD * r, HEAD * (r + 1)), slice(SEQ * j, SEQ * (j + 1))
                    out = score_ps[h % 2][0:SEQ, 0:KEYS]
                    nc.tensor.matmul(out, q_hi[:, par, r, cols], k_stack[:, par, h, :], start=True, stop=False)
                    nc.tensor.matmul(out, q_lo[rows, par, cols], k_stack[rows, par, h, :], start=False, stop=True).then_inc(score_full, 1)

                def transpose_probs(b, h):
                    pe.wait_ge(norm_done, HEADS * b + h + 1)
                    if not (isinstance(b, int) and b == 0 and h < 2):
                        pe.wait_ge(pt_done, HEADS * b + h - 1)
                    for t in range(KEY_TILES):
                        last = nc.tensor.transpose(pt_ps[h % 2][:, SEQ * t:SEQ * (t + 1)], probs[:, h % 4, P * t:P * (t + 1)],
                                                   ident[0:SEQ, 0:SEQ])
                    last.then_inc(pt_full, 1)

                def values(b, par, h):
                    c, j, r = h // 8, (h % 8) // 2, h % 2
                    pe.wait_ge(pt_done, HEADS * b + h + 1)
                    if h == 0:
                        wait_projected(pe, b, ("v", V_JOBS - 2))
                        wait_projected(pe, b, ("v", V_JOBS - 1))
                    if h % 8 == 0 and not (isinstance(b, int) and b == 0):
                        pe.wait_ge(ot_done, 2 * b - 1 + c)
                    out = av_ps[c][HEAD * r:HEAD * (r + 1), SEQ * j:SEQ * (j + 1)]
                    for t in range(KEY_TILES):
                        rows = LAST_KEYS if t == 2 else P
                        last = nc.tensor.matmul(out, v_sb[0:rows, par, t, HEAD * h:HEAD * (h + 1)],
                                                pt_sb[0:rows, h % 2, SEQ * t:SEQ * (t + 1)], start=(t == 0), stop=(t == 2))
                    last.then_inc(av_full, 1)

                def output(b, kind, body_b):
                    bk = take_slot(("o", 0), kind, body_b)
                    pe.wait_ge(ot_done, 2 * b + 2)
                    for j in range(PAIRS):
                        last = nc.tensor.matmul(ring_ps[bk][0:SEQ, 0:DIM], ot_sb[:, SEQ * j:SEQ * (j + 1)], wo_sb[:, j, :],
                                                start=(j == 0), stop=(j == PAIRS - 1))
                    last.then_inc(ring_full[bk], 1)

                pe.wait_ge(const_in, 16 * (6 if second_ln else 3))
                transpose_x("prologue", 0, 0)
                pe.wait_ge(stage_lo, 3)
                for slot in JOBS:
                    job(slot, 0, "prologue", 0, 0)

                def body(b, par, half, kind):
                    for s in range(HEADS):
                        scores(b, par, s)
                        if s >= T_LAG:
                            transpose_probs(b, s - T_LAG)
                        elif kind != "first":
                            transpose_probs(b - 1, HEADS + s - T_LAG)
                        for slot in step_slots(s, kind != "last", kind != "first"):
                            if slot[0] == "xt":
                                transpose_x(kind, b + 1, b)
                            elif slot[0] == "o":
                                output(b - 1, kind, b)
                            else:
                                job(slot, 1 - par, kind, b + 1, b)
                        if s >= AV_LAG:
                            values(b, par, s - AV_LAG)
                        elif kind != "first":
                            values(b - 1, 1 - par, HEADS + s - AV_LAG)

                each_batch(pe, body)
                for s in range(HEADS, HEADS + AV_LAG):
                    if s < HEADS + T_LAG:
                        transpose_probs(last_b, s - T_LAG)
                    values(last_b, 1, s - AV_LAG)
                output(last_b, "tail", 0)


EXPERTS, FF = 8, 816
FULL_F = FF // P
REM_F = FF - FULL_F * P
EXPERT_PAIRS = EXPERTS // 2
F_TILES = 2 * FULL_F + 1
SHARED = 2 * FULL_F
TILES = TOKENS // P
GROUP = 5
CHUNKS = TILES // GROUP
CHUNK = GROUP * P
HALF = CHUNK // 2
H_SCALE = 16.0
GU_SCALE = X_SCALE * W_SCALE
Y_SCALE = H_SCALE * W_SCALE
HW_COLS = 3 * DIM
T_BANK = 4 * P


def moe_phase(nc, x_in, x_out, weights, gate_bias, up_bias, down_bias, router, router_bias, descending, identity):
    name = "moe"
    with ExitStack() as ctx:
        def sb(label, shape, dt):
            return ctx.enter_context(nc.sbuf_tensor(f"{name}_{label}", shape, dt))

        def sem(label):
            return ctx.enter_context(nc.semaphore(f"{name}_{label}"))

        acc = sb("acc", [P, TILES, DIM], F32)
        xt_hi = sb("xt_hi", [P, 2, TOKENS], F16)
        xt_lo = sb("xt_lo", [P, 2, TOKENS], F16)
        w_stage = sb("w_stage", [P, 2, HW_COLS], F32)
        w_hi = sb("w_hi", [P, 2, F_TILES, HW_COLS], F16)
        w_lo = sb("w_lo", [P, 2, F_TILES, HW_COLS], F16)
        h_hi = sb("h_hi", [P, F_TILES, CHUNK], F16)
        h_lo = sb("h_lo", [P, F_TILES, CHUNK], F16)
        up_sb = sb("up", [P, 2, HALF], F32)
        z_sb = sb("z", [P, 2, HALF], F32)
        h_sb = sb("h", [P, 2, HALF], F32)
        gb = sb("gb", [P, EXPERT_PAIRS * F_TILES], F32)
        gbs = sb("gbs", [P, EXPERT_PAIRS * F_TILES], F32)
        ub = sb("ub", [P, EXPERT_PAIRS * F_TILES], F32)
        db = sb("db", [EXPERTS, DIM], F32)
        ident = sb("ident", [P, P], F32)
        expo = sb("expo", [P, GROUP], F32)
        xn = sb("xn", [P, GROUP, DIM], F32)
        stats = sb("stats", [P, GROUP, 6], F32)
        mv = sb("mv", [P, GROUP, 2], F32)
        veps = sb("veps", [P, GROUP], F32)
        rstd = sb("rstd", [P, GROUP], F32)
        rt_in = sb("rt_in", [P, 2 * EXPERTS], F32)
        rt_hi = sb("rt_hi", [P, 2 * EXPERTS], F16)
        rt_lo = sb("rt_lo", [P, 2 * EXPERTS], F16)
        rtb = sb("rtb", [P, EXPERTS], F32)
        desc = sb("desc", [P, EXPERTS], F32)
        R = TILES * EXPERTS
        logits = sb("logits", [P, R], F32)
        pr = sb("pr", [P, R], F32)
        one = [sb(f"onehot{i}", [P, R], F32) for i in range(2)]
        pick = sb("pick", [P, R], F32)
        top = [sb(f"top{i}", [P, TILES], F32) for i in range(2)]
        first = sb("first", [P, TILES], F32)
        tsum = sb("tsum", [P, TILES], F32)
        comb = sb("comb", [P, R], F32)
        combs = sb("combs", [P, R], F32)
        comb_t = sb("comb_t", [EXPERTS, 2, P], F32)

        banks = [ctx.enter_context(nc.psum_tensor(f"{name}_bank{i}", [P, 512], F32)) for i in range(8)]
        gate_ps, up_ps, y_ps = banks[0:2], banks[2:4], banks[4:6]

        const_in, x_first, x_rest = sem("const_in"), sem("x_first"), sem("x_rest")
        w_landed = [sem(f"w_landed{i}") for i in range(2)]
        w_scaled, w_his, w_ready = sem("w_scaled"), sem("w_his"), sem("w_ready")
        consts_ready, carried = sem("consts_ready"), sem("carried")
        ln_stats, ln_aggr, ln_eps, ln_rstd, xn_ready = (sem(s) for s in ("ln_stats", "ln_aggr", "ln_eps", "ln_rstd", "xn_ready"))
        xt_full, xt_his, xt_los = sem("xt_full"), sem("xt_his"), sem("xt_los")
        logit_full, logit_done = sem("logit_full"), sem("logit_done")
        route = sem("route")
        exp_done, comb_ready = sem("exp_done"), sem("comb_ready")
        ct_full, ct_done, bias_full, bias_done = (sem(s) for s in ("ct_full", "ct_done", "bias_full", "bias_done"))
        gu_full, up_done, z_done, h_done, hhi_done, hlo_done = (sem(s) for s in ("gu_full", "up_done", "z_done", "h_done", "hhi_done", "hlo_done"))
        y_full, y_done, stored = sem("y_full"), sem("y_done"), sem("stored")

        UNITS = 2 * F_TILES
        YS = 2 * GROUP
        order = list(range(FULL_F)) + [SHARED] + list(range(FULL_F, 2 * FULL_F))

        def alone(eng, semaphore, value):
            eng.wait_ge(semaphore, value)
            if not isinstance(value, int):
                eng.sem_inc(carried, 1)

        def groups(eng, body):
            body(0)
            with eng.Fori(1, CHUNKS) as g:
                body(g)

        def all_chunks(eng, body):
            with eng.Fori(0, EXPERT_PAIRS // 2) as i:
                for par in range(2):
                    with eng.Fori(0, CHUNKS) as c:
                        body(2 * i + par, par, c, (2 * i + par) * CHUNKS + c)

        def xt_pieces():
            return [(2 * t + k, t, k * T_BANK, (T_BANK, CHUNK - T_BANK)[k]) for t in range(2) for k in range(2)]

        with nc.Block() as block:

            @block.sync
            def _(sp):
                x_tiles = x_in.rearrange("(t p) d -> p t d", p=P)
                sp.dma_start(acc[:, 0:GROUP, :], x_tiles[:, 0:GROUP, :]).then_inc(x_first, 16)
                sp.dma_start(acc[:, GROUP:TILES, :], x_tiles[:, GROUP:TILES, :]).then_inc(x_rest, 16)
                for dst, src in ((ident[:, :], identity), (gb[:, :], gate_bias), (ub[:, :], up_bias), (db[:, :], down_bias),
                                 (rt_in[:, :], router), (rtb[:, :], router_bias.to_broadcast([P, EXPERTS])),
                                 (desc[:, :], descending.to_broadcast([P, EXPERTS]))):
                    sp.dma_start(dst, src).then_inc(const_in, 16)

                def load_tile(n, buf, half, reuse):
                    if reuse:
                        sp.wait_ge(w_ready, n - 1)
                    sp.dma_start(w_stage[:, buf, :], weights[:, bass.ds(n * HW_COLS, HW_COLS)]).then_inc(w_landed[buf], 16)

                load_tile(0, 0, 0, False)
                load_tile(1, 1, 0, False)
                with sp.Fori(1, EXPERT_PAIRS * F_TILES // 2) as i:
                    load_tile(2 * i, 0, i, True)
                    load_tile(2 * i + 1, 1, i, True)
                out_tiles = x_out.rearrange("(t p) d -> p t d", p=P)
                done = (EXPERT_PAIRS - 1) * CHUNKS * YS
                for c in range(CHUNKS):
                    sp.wait_ge(y_done, done + (c + 1) * YS)
                    tiles = slice(GROUP * c, GROUP * (c + 1))
                    sp.dma_start(out_tiles[:, tiles, :], acc[:, tiles, :]).then_inc(stored, 16)
                sp.wait_ge(stored, 16 * CHUNKS)

            @block.gpsimd
            def _(pool):
                def rstds(g):
                    pool.wait_ge(ln_eps, g + 1)
                    nc.gpsimd.tensor_tensor(rstd[:, :], veps[:, :], expo[:, :], ALU.pow).then_inc(ln_rstd, 1)

                def split_tile(n, par, f, buf, landed):
                    alone(pool, w_landed[buf], landed)
                    nc.gpsimd.tensor_scalar(w_stage[:, buf, :], w_stage[:, buf, :], W_SCALE, 1.0, ALU.mult, ALU.mult).then_inc(w_scaled, 1)
                    alone(pool, w_scaled, n + 1)
                    nc.gpsimd.tensor_copy(w_hi[:, par, f, :], w_stage[:, buf, :]).then_inc(w_his, 1)
                    pool.wait_ge(w_his, n + 1)
                    nc.gpsimd.tensor_tensor(w_lo[:, par, f, :], w_stage[:, buf, :], w_hi[:, par, f, :], ALU.subtract).then_inc(w_ready, 1)

                def split_pair(pair, par, n0, reuse):
                    if reuse:
                        alone(pool, y_full, (pair - 1) * CHUNKS * YS)
                    for f in range(F_TILES):
                        n = n0 + f
                        buf = (par * F_TILES + f) % 2
                        before = (par * F_TILES + f) // 2
                        split_tile(n, par, f, buf, (pair - par) * F_TILES * 8 + 16 * before + 16)

                nc.gpsimd.memset(expo[:, :], -0.5).then_inc(consts_ready, 1)
                pool.wait_ge(consts_ready, 1)
                groups(pool, rstds)
                split_pair(0, 0, 0, False)
                split_pair(1, 1, F_TILES, False)
                split_pair(2, 0, 2 * F_TILES, True)
                split_pair(3, 1, 3 * F_TILES, True)

            @block.scalar
            def _(act):
                act.wait_ge(const_in, 16 * 7)
                nc.scalar.activation(rt_hi[:, :], rt_in[:, :], ACT.Copy, scale=W_SCALE).then_inc(consts_ready, 1)
                nc.scalar.activation(gbs[:, :], gb[:, :], ACT.Copy, scale=GU_SCALE).then_inc(consts_ready, 1)

                def evac_xt(g):
                    for n, (bk, t, at, cols) in enumerate(xt_pieces()):
                        act.wait_ge(xt_full, 4 * g + n + 1)
                        nc.scalar.activation(xt_hi[:, t, bass.ds(g * CHUNK + at, cols)], banks[bk][:, 0:cols], ACT.Copy,
                                             scale=X_SCALE).then_inc(xt_his, 1)

                groups(act, evac_xt)
                act.wait_ge(route, 3)
                nc.scalar.activation(pr[:, :], logits[:, :], ACT.Exp).then_inc(exp_done, 1)
                for k in range(TILES):
                    act.wait_ge(ct_full, k + 1)
                    nc.scalar.activation(comb_t[:, k % 2, :], banks[2 + k % 2][0:EXPERTS, 0:P], ACT.Copy).then_inc(ct_done, 1)

                def chunk(pair, par, c, n):
                    for u in range(UNITS):
                        f, b = order[u // 2], u % 2
                        k = n * UNITS + u
                        alone(act, gu_full, k + 1)
                        nc.scalar.activation(up_sb[:, b, :], up_ps[b][:, 0:HALF], ACT.Identity, scale=1.0 / GU_SCALE,
                                             bias=ub[:, bass.ds(pair * F_TILES + f, 1)]).then_inc(up_done, 1)
                        act.wait_ge(z_done, k + 1)
                        if u >= 2:
                            act.wait_ge(hlo_done, k - 1)
                        nc.scalar.activation(h_sb[:, b, :], z_sb[:, b, :], ACT.Silu, scale=1.0 / GU_SCALE).then_inc(h_done, 1)

                all_chunks(act, chunk)

            @block.vector
            def _(dve):
                def layernorm(g):
                    dve.wait_ge(x_first if isinstance(g, int) else x_rest, 16)
                    for k in range(GROUP):
                        nc.vector.bn_stats(stats[:, k, :], acc[:, bass.ds(g * GROUP + k, 1), :].rearrange("p a d -> p (a d)")).then_inc(ln_stats, 1)
                    alone(dve, ln_stats, GROUP * g + GROUP)
                    for k in range(GROUP):
                        nc.vector.bn_aggr(mv[:, k, :], stats[:, k, :]).then_inc(ln_aggr, 1)
                    dve.wait_ge(ln_aggr, GROUP * g + GROUP)
                    nc.vector.tensor_scalar(veps[:, :], mv[:, :, 1], LN_EPS, None, ALU.add).then_inc(ln_eps, 1)
                    if not isinstance(g, int):
                        dve.wait_ge(xt_full, 4 * g)
                    dve.wait_ge(ln_rstd, g + 1)
                    for k in range(GROUP):
                        nc.vector.tensor_scalar(xn[:, k, :], acc[:, bass.ds(g * GROUP + k, 1), :].rearrange("p a d -> p (a d)"),
                                                mv[:, k, 0:1], rstd[:, k:k + 1], ALU.subtract, ALU.mult).then_inc(xn_ready, 1)
                    for n, (bk, t, at, cols) in enumerate(xt_pieces()):
                        dve.wait_ge(xt_his, 4 * g + n + 1)
                        where = bass.ds(g * CHUNK + at, cols)
                        nc.vector.scalar_tensor_tensor(xt_lo[:, t, where], banks[bk][:, 0:cols], X_SCALE, xt_hi[:, t, where],
                                                       ALU.mult, ALU.subtract).then_inc(xt_los, 1)
                    dve.wait_ge(logit_full, g + 1)
                    nc.vector.tensor_scalar(logits[:, bass.ds(g * GROUP * EXPERTS, GROUP * EXPERTS)], banks[4][:, 0:GROUP * EXPERTS],
                                            1.0 / GU_SCALE, None, ALU.mult).then_inc(logit_done, 1)

                dve.wait_ge(consts_ready, 3)
                nc.vector.scalar_tensor_tensor(rt_lo[:, :], rt_in[:, :], W_SCALE, rt_hi[:, :], ALU.mult, ALU.subtract).then_inc(consts_ready, 1)
                groups(dve, layernorm)

                steps = [0]

                def step(instruction):
                    steps[0] += 1
                    instruction.then_inc(route, 1)
                    dve.wait_ge(route, steps[0])

                def by_tile(t):
                    return t[:, :].rearrange("p (t e) -> p t e", e=EXPERTS)

                def wide(t):
                    return t[:, :].unsqueeze(2).to_broadcast([P, TILES, EXPERTS])

                def each(t):
                    return t[:, :].unsqueeze(1).to_broadcast([P, TILES, EXPERTS])

                dve.wait_ge(logit_done, CHUNKS)
                step(nc.vector.tensor_tensor(by_tile(logits), by_tile(logits), each(rtb), ALU.add))
                step(nc.vector.reduce_max(top[0][:, :], by_tile(logits), AX.X))
                step(nc.vector.tensor_tensor(by_tile(logits), by_tile(logits), wide(top[0]), ALU.subtract))
                dve.wait_ge(exp_done, 1)
                step(nc.vector.reduce_sum(tsum[:, :], by_tile(pr), AX.X))
                step(nc.vector.reciprocal(first[:, :], tsum[:, :]))
                step(nc.vector.tensor_tensor(by_tile(pr), by_tile(pr), wide(first), ALU.mult))
                step(nc.vector.tensor_copy(comb[:, :], pr[:, :]))
                for i in range(2):
                    step(nc.vector.reduce_max(top[i][:, :], by_tile(comb), AX.X))
                    step(nc.vector.tensor_tensor(by_tile(pick), by_tile(comb), wide(top[i]), ALU.is_equal))
                    step(nc.vector.tensor_tensor(by_tile(pick), by_tile(pick), each(desc), ALU.mult))
                    step(nc.vector.reduce_max(first[:, :], by_tile(pick), AX.X))
                    step(nc.vector.tensor_tensor(by_tile(one[i]), by_tile(pick), wide(first), ALU.is_equal))
                    if i == 0:
                        step(nc.vector.scalar_tensor_tensor(comb[:, :], one[0][:, :], -2.0, comb[:, :], ALU.mult, ALU.add))
                step(nc.vector.tensor_tensor(tsum[:, :], top[0][:, :], top[1][:, :], ALU.add))
                step(nc.vector.tensor_scalar(tsum[:, :], tsum[:, :], 1e-20, None, ALU.add))
                step(nc.vector.reciprocal(first[:, :], tsum[:, :]))
                step(nc.vector.tensor_tensor(one[0][:, :], one[0][:, :], one[1][:, :], ALU.add))
                step(nc.vector.tensor_tensor(one[0][:, :], one[0][:, :], pr[:, :], ALU.mult))
                step(nc.vector.tensor_tensor(by_tile(comb), by_tile(one[0]), wide(first), ALU.mult))
                nc.vector.tensor_scalar(combs[:, :], comb[:, :], 1.0 / Y_SCALE, None, ALU.mult).then_inc(comb_ready, 1)
                for k in range(TILES):
                    dve.wait_ge(bias_full, k + 1)
                    nc.vector.tensor_tensor(acc[:, k, :], acc[:, k, :], banks[4 + k % 2][:, 0:DIM], ALU.add).then_inc(bias_done, 1)
                dve.wait_ge(comb_ready, 1)

                def chunk(pair, par, c, n):
                    def cut(u):
                        f, b = order[u // 2], u % 2
                        k = n * UNITS + u
                        cols = slice(HALF * b, HALF * (b + 1))
                        dve.wait_ge(h_done, k + 1)
                        nc.vector.tensor_scalar(h_hi[:, f, cols], h_sb[:, b, :], H_SCALE, None, ALU.mult).then_inc(hhi_done, 1)
                        dve.wait_ge(hhi_done, k + 1)
                        nc.vector.scalar_tensor_tensor(h_lo[:, f, cols], h_sb[:, b, :], H_SCALE, h_hi[:, f, cols], ALU.mult,
                                                       ALU.subtract).then_inc(hlo_done, 1)

                    for u in range(UNITS):
                        f, b = order[u // 2], u % 2
                        k = n * UNITS + u
                        dve.wait_ge(up_done, k + 1)
                        nc.vector.scalar_tensor_tensor(z_sb[:, b, :], gate_ps[b][:, 0:HALF], gbs[:, bass.ds(pair * F_TILES + f, 1)],
                                                       up_sb[:, b, :], ALU.add, ALU.mult).then_inc(z_done, 1)
                        if u >= 1:
                            cut(u - 1)
                    cut(UNITS - 1)
                    for y in range(YS):
                        e, t = y // GROUP, y % GROUP
                        dve.wait_ge(y_full, n * YS + y + 1)
                        tile = acc[:, bass.ds(c * GROUP + t, 1), :].rearrange("p a d -> p (a d)")
                        nc.vector.scalar_tensor_tensor(tile, y_ps[y % 2][:, 0:DIM], combs[:, bass.ds((c * GROUP + t) * EXPERTS + 2 * pair + e, 1)],
                                                       tile, ALU.mult, ALU.add).then_inc(y_done, 1)

                all_chunks(dve, chunk)

            @block.tensor
            def _(pe):
                def transposes(g):
                    pieces = xt_pieces()
                    for k, (bk, t, at, cols) in enumerate(pieces):
                        if not isinstance(g, int):
                            pe.wait_ge(xt_los, 4 * g - 3 + k)
                        pe.wait_ge(xn_ready, GROUP * g + (at + cols) // P)
                        for j in range(cols // P):
                            last = nc.tensor.transpose(banks[bk][:, P * j:P * (j + 1)], xn[:, at // P + j, P * t:P * (t + 1)], ident[:, :])
                        last.then_inc(xt_full, 1)
                    pe.wait_ge(xt_los, 4 * g + 4)
                    if not isinstance(g, int):
                        pe.wait_ge(logit_done, g)
                    for j in range(GROUP):
                        out = banks[4][:, EXPERTS * j:EXPERTS * (j + 1)]
                        tok = bass.ds(g * CHUNK + j * P, P)
                        for t in range(2):
                            w = slice(EXPERTS * t, EXPERTS * (t + 1))
                            nc.tensor.matmul(out, xt_hi[:, t, tok], rt_hi[:, w], start=(t == 0), stop=False)
                            nc.tensor.matmul(out, xt_hi[:, t, tok], rt_lo[:, w], start=False, stop=False)
                            last = nc.tensor.matmul(out, xt_lo[:, t, tok], rt_hi[:, w], start=False, stop=(t == 1))
                    last.then_inc(logit_full, 1)

                pe.wait_ge(consts_ready, 4)
                groups(pe, transposes)
                pe.wait_ge(comb_ready, 1)

                def turn(k):
                    if k >= 2:
                        pe.wait_ge(ct_done, k - 1)
                    nc.tensor.transpose(banks[2 + k % 2][0:EXPERTS, 0:P], comb[:, EXPERTS * k:EXPERTS * (k + 1)], ident[:, :]).then_inc(ct_full, 1)

                turn(0)
                for k in range(TILES):
                    if k + 1 < TILES:
                        if k + 1 >= 2:
                            pass
                        turn(k + 1)
                    pe.wait_ge(ct_done, k + 1)
                    if k >= 2:
                        pe.wait_ge(bias_done, k - 1)
                    nc.tensor.matmul(banks[4 + k % 2][:, 0:DIM], comb_t[:, k % 2, :], db[:, :], start=True, stop=True).then_inc(bias_full, 1)
                pe.wait_ge(bias_done, TILES)

                def chunk(pair, par, c, n):
                    for u in range(UNITS):
                        f, b = order[u // 2], u % 2
                        k = n * UNITS + u
                        if b == 0:
                            pe.wait_ge(w_ready, pair * F_TILES + f + 1)
                        if u >= 2:
                            pe.wait_ge(z_done, k - 1)
                        toks = bass.ds(c * CHUNK + b * HALF, HALF)
                        for ps, w0 in ((up_ps[b], DIM), (gate_ps[b], 0)):
                            for t in range(2):
                                w = slice(w0 + P * t, w0 + P * (t + 1))
                                nc.tensor.matmul(ps[:, 0:HALF], w_hi[:, par, f, w], xt_hi[:, t, toks], start=(t == 0), stop=False)
                                nc.tensor.matmul(ps[:, 0:HALF], w_hi[:, par, f, w], xt_lo[:, t, toks], start=False, stop=False)
                                last = nc.tensor.matmul(ps[:, 0:HALF], w_lo[:, par, f, w], xt_hi[:, t, toks], start=False, stop=(t == 1))
                        last.then_inc(gu_full, 1)
                    for y in range(YS):
                        e, t = y // GROUP, y % GROUP
                        if t == 0:
                            pe.wait_ge(hlo_done, n * UNITS + (2 * (FULL_F + 1) if e == 0 else UNITS))
                        if y >= 2:
                            pe.wait_ge(y_done, n * YS + y - 1)
                        out = y_ps[y % 2][:, 0:DIM]
                        tok, down = slice(P * t, P * (t + 1)), slice(2 * DIM, 3 * DIM)
                        parts = [(f, slice(0, P)) for f in range(FULL_F * e, FULL_F * (e + 1))] + [(SHARED, slice(HEAD * e, HEAD * e + REM_F))]
                        for m, (f, rows) in enumerate(parts):
                            nc.tensor.matmul(out, h_hi[rows, f, tok], w_hi[rows, par, f, down], start=(m == 0), stop=False)
                            nc.tensor.matmul(out, h_hi[rows, f, tok], w_lo[rows, par, f, down], start=False, stop=False)
                            last = nc.tensor.matmul(out, h_lo[rows, f, tok], w_hi[rows, par, f, down], start=False, stop=(m == len(parts) - 1))
                        last.then_inc(y_full, 1)

                all_chunks(pe, chunk)


def layout_moe(a, out):
    gate, up, down = (a[f"L0_ffn_{n}_w"] for n in ("gp", "up", "down"))
    tiles, gbias, ubias = [], [], []
    for pair in range(EXPERT_PAIRS):
        for f in range(F_TILES):
            if f < SHARED:
                e, at = 2 * pair + f // FULL_F, P * (f % FULL_F)
                pieces = [(e, slice(at, at + P), 0)]
            else:
                pieces = [(2 * pair + r, slice(FULL_F * P, FF), HEAD * r) for r in range(2)]
            tile = np.zeros((P, HW_COLS), gate.dtype)
            gcol, ucol = np.zeros(P, gate.dtype), np.zeros(P, gate.dtype)
            for e, rows, at in pieces:
                n = rows.stop - rows.start
                for t in range(2):
                    tile[:, P * t + at:P * t + at + n] = gate[e, rows, P * t:P * (t + 1)].T
                    tile[:, DIM + P * t + at:DIM + P * t + at + n] = up[e, rows, P * t:P * (t + 1)].T
                tile[at:at + n, 2 * DIM:] = down[e, :, rows].T
                gcol[at:at + n] = a["L0_ffn_gp_b"][e, rows]
                ucol[at:at + n] = a["L0_ffn_up_b"][e, rows]
            tiles.append(tile)
            gbias.append(gcol)
            ubias.append(ucol)
    out["moe_w"] = np.concatenate(tiles, axis=1)
    out["moe_gate_b"], out["moe_up_b"] = np.stack(gbias, 1), np.stack(ubias, 1)
    out["moe_down_b"] = a["L0_ffn_down_b"]
    out["moe_router"] = a["L0_ffn_gate_w"].T.reshape(2, P, EXPERTS).transpose(1, 0, 2).reshape(P, 2 * EXPERTS)
    out["moe_router_b"] = a["L0_ffn_gate_b"].reshape(1, EXPERTS)
    out["moe_descending"] = np.arange(EXPERTS, 0, -1, dtype=np.float32).reshape(1, EXPERTS)


MOE_NAMES = ["moe_w", "moe_gate_b", "moe_up_b", "moe_down_b", "moe_router", "moe_router_b", "moe_descending"]


TINY = 1e-37
QMAX = 127.0
FFQ = 704
Q_TILES = -(-FFQ // P)
Q_LAST = FFQ - (Q_TILES - 1) * P
ROUND = 1.5 * 2.0 ** 23
QCOLS = 512
Q_CHUNKS = [(at, min(QCOLS, TOKENS - at)) for at in range(0, TOKENS, QCOLS)]


def mlp_phase(nc, x_in, x_out, w_gate, w_up, w_down, clip_x, clip_down, identity):
    name = "mlp"
    with ExitStack() as ctx:
        def sb(label, shape, dt):
            return ctx.enter_context(nc.sbuf_tensor(f"{name}_{label}", shape, dt))

        def sem(label):
            return ctx.enter_context(nc.semaphore(f"{name}_{label}"))

        FLAT = TILES * DIM
        x_sb = sb("x", [P, TILES, DIM], F32)
        big = sb("big", [P, Q_TILES * TOKENS], F32)
        y_sb = big[:, 0:FLAT].rearrange("p (t d) -> p t d", d=DIM)
        h_sb = big[:, :].rearrange("p (f t) -> p f t", t=TOKENS)
        yq = sb("yq", [P, TILES, DIM], F16)
        yq_t = sb("yq_t", [P, 2, TOKENS], F16)
        w_nat = sb("w_nat", [P, 2, Q_TILES, DIM], F32)
        wd_nat = sb("wd_nat", [P, 2, FFQ], F32)
        w_q = sb("w_q", [P, 2, Q_TILES, DIM], F16)
        wd_q = sb("wd_q", [P, 2, FFQ], F16)
        w_t = sb("w_t", [P, 2, 2, Q_TILES * P], F16)
        wd_t = sb("wd_t", [P, Q_TILES, DIM], F16)
        w_abs = sb("w_abs", [P, 2 * Q_TILES + 2], F32)
        w_scale = sb("w_scale", [P, 2 * Q_TILES + 2], F32)
        w_inv = sb("w_inv", [P, 2 * Q_TILES + 2], F32)
        w_act = sb("w_act", [P, 2 * Q_TILES], F32)
        dsc = sb("dsc", [P, 2], F32)
        diag = sb("diag", [P, 2, P], F32)
        ones = sb("ones", [P, P], F32)
        down_row = sb("down_row", [P, DIM], F32)
        silu_sb = sb("silu", [P, 2, QCOLS], F32)
        hq = sb("hq", [P, 2, Q_TILES, P], F32)
        hq16 = sb("hq16", [P, 2, Q_TILES, P], F16)
        out_sb = sb("out", [P, 2, DIM], F32)
        ident = sb("ident", [P, P], F32)
        ident16 = sb("ident16", [P, P], F16)
        clips = sb("clips", [P, 2], F32)
        sig = sb("sig", [P, 2], F32)
        stats = sb("stats", [P, TILES, 6], F32)
        mv = sb("mv", [P, TILES, 2], F32)
        veps = sb("veps", [P, TILES], F32)
        rstd = sb("rstd", [P, TILES], F32)
        expo = sb("expo", [P, TILES], F32)
        part = sb("part", [P, 2], F32)
        hmaxes = sb("hmaxes", [P, Q_TILES * len(Q_CHUNKS)], F32)
        amax = sb("amax", [P, 2], F32)
        scale = sb("scale", [P, 2], F32)
        inv = sb("inv", [P, 2], F32)

        banks = [ctx.enter_context(nc.psum_tensor(f"{name}_bank{i}", [P, 512], F32)) for i in range(6)]
        banks16 = [ctx.enter_context(nc.psum_tensor(f"{name}_t{i}", [P, 1024], F16)) for i in range(2)]
        gate_ps, up_ps, y_ps = banks[0:2], banks[2:4], banks[4:6]

        const_in, x_in_sem, w_in = sem("const_in"), sem("x_in"), sem("w_in")
        setup = sem("setup")
        pool_ready, sig_ready = sem("pool_ready"), sem("sig_ready")
        eps_ready, rstd_ready = sem("eps_ready"), sem("rstd_ready")
        part_ready, amax_ready = sem("part_ready"), sem("amax_ready")
        q_ready, wq_ready = sem("q_ready"), sem("wq_ready")
        t_full, t_done, yt_done, row_full = sem("t_full"), sem("t_done"), sem("yt_done"), sem("row_full")
        scales_ready = sem("scales_ready")
        gu_full, silu_done, hid_done = sem("gu_full"), sem("silu_done"), sem("hid_done")
        hq_ready, hq16_ready, o_full, o_mul, o_done = (sem(s) for s in ("hq_ready", "hq16_ready", "o_full", "o_mul", "o_done"))
        stored = [sem(f"stored{i}") for i in range(2)]

        W_TURNS = [("gu", g, t) for g in range(2) for t in range(2)] + [("down", i, 0) for i in range(Q_TILES)]
        UNITS = [(f, c) for c in range(len(Q_CHUNKS)) for f in range(Q_TILES)]

        def tile_rows(f):
            return P if f < Q_TILES - 1 else Q_LAST

        with nc.Block() as block:

            @block.sync
            def _(sp):
                x_tiles = x_in.rearrange("(t p) d -> p t d", p=P)
                sp.dma_start(x_sb[:, :, :], x_tiles).then_inc(x_in_sem, 16)
                for g, w in enumerate((w_gate, w_up)):
                    full = (Q_TILES - 1) * P
                    sp.dma_start(w_nat[:, g, 0:Q_TILES - 1, :], w[0:full, :].rearrange("(f p) d -> p f d", p=P)).then_inc(w_in, 16)
                    sp.dma_start(w_nat[0:Q_LAST, g, Q_TILES - 1, :], w[full:FFQ, :]).then_inc(w_in, 16)
                sp.dma_start(wd_nat[:, :, :], w_down.rearrange("(t p) f -> p t f", p=P)).then_inc(w_in, 16)
                sp.dma_start(ident[:, :], identity).then_inc(const_in, 16)
                sp.dma_start(clips[:, 0:1], clip_x.to_broadcast([P, 1])).then_inc(const_in, 16)
                sp.dma_start(clips[:, 1:2], clip_down.to_broadcast([P, 1])).then_inc(const_in, 16)
                for k in range(TILES):
                    sp.wait_ge(o_done, k + 1)
                    sp.dma_start(x_out[P * k:P * (k + 1), :], out_sb[:, k % 2, :]).then_inc(stored[k % 2], 16)
                for b in range(2):
                    sp.wait_ge(stored[b], 16 * len(range(b, TILES, 2)))

            @block.gpsimd
            def _(pool):
                nc.gpsimd.memset(expo[:, :], -0.5).then_inc(pool_ready, 1)
                pool.wait_ge(pool_ready, 1)
                nc.gpsimd.memset(w_nat[Q_LAST:P, :, Q_TILES - 1, :], 0.0).then_inc(pool_ready, 1)
                pool.wait_ge(pool_ready, 2)
                nc.gpsimd.memset(ones[:, :], 1.0).then_inc(pool_ready, 1)
                pool.wait_ge(pool_ready, 3)
                pool.wait_ge(eps_ready, 1)
                nc.gpsimd.tensor_tensor(rstd[:, :], veps[:, :], expo[:, :], ALU.pow).then_inc(rstd_ready, 1)
                for k in range(2):
                    pool.wait_ge(part_ready, k + 1)
                    nc.gpsimd.partition_all_reduce(amax[:, k:k + 1], part[:, k:k + 1], P, bass.bass_isa.ReduceOp.max).then_inc(amax_ready, 1)

            @block.scalar
            def _(act):
                act.wait_ge(const_in, 48)
                nc.scalar.activation(sig[:, :], clips[:, :], ACT.Sigmoid).then_inc(sig_ready, 1)
                nc.scalar.activation(ident16[:, :], ident[:, :], ACT.Copy).then_inc(sig_ready, 1)
                for k, (what, i, t) in enumerate(W_TURNS):
                    act.wait_ge(t_full, k + 1)
                    if what == "gu":
                        nc.scalar.activation(w_t[:, i, t, :], banks16[k % 2][:, 0:Q_TILES * P], ACT.Copy).then_inc(t_done, 1)
                    else:
                        rows = tile_rows(i)
                        nc.scalar.activation(wd_t[0:rows, i, :], banks16[k % 2][0:rows, 0:DIM], ACT.Copy).then_inc(t_done, 1)
                for k, (at, cols) in enumerate(Q_CHUNKS):
                    act.wait_ge(t_full, len(W_TURNS) + k + 1)
                    src = banks16[k % 2][:, :].rearrange("p (t c) -> p t c", t=2)[:, :, 0:cols]
                    nc.scalar.activation(yq_t[:, :, at:at + cols], src, ACT.Copy).then_inc(t_done, 1)
                act.wait_ge(scales_ready, 1)
                for k, (f, c) in enumerate(UNITS):
                    rows, cols = tile_rows(f), Q_CHUNKS[c][1]
                    act.wait_ge(gu_full, k + 1)
                    if k >= 2:
                        act.wait_ge(hid_done, k - 1)
                    nc.scalar.activation(silu_sb[0:rows, k % 2, 0:cols], gate_ps[k % 2][0:rows, 0:cols], ACT.Silu,
                                         scale=w_act[0:rows, f:f + 1]).then_inc(silu_done, 1)
                for k in range(TILES):
                    act.wait_ge(hq_ready, k + 1)
                    if k >= 2:
                        act.wait_ge(o_full, k - 1)
                    for lo, hi, rows in ((0, Q_TILES - 1, P), (Q_TILES - 1, Q_TILES, Q_LAST)):
                        last = nc.scalar.activation(hq16[0:rows, k % 2, lo:hi, :], hq[0:rows, k % 2, lo:hi, :], ACT.Copy, bias=-ROUND)
                    last.then_inc(hq16_ready, 1)

            @block.vector
            def _(dve):
                count = [0]

                def step(instruction):
                    count[0] += 1
                    instruction.then_inc(setup, 1)
                    dve.wait_ge(setup, count[0])

                def quantise(flat, inverse):
                    step(nc.vector.tensor_scalar(flat, flat, inverse, ROUND, ALU.mult, ALU.add))
                    step(nc.vector.tensor_scalar(flat, flat, ROUND + QMAX, ROUND - QMAX - 1.0, ALU.min, ALU.max))

                dve.wait_ge(x_in_sem, 16)
                for k in range(TILES):
                    last = nc.vector.bn_stats(stats[:, k, :], x_sb[:, k, :])
                step(last)
                for k in range(TILES):
                    last = nc.vector.bn_aggr(mv[:, k, :], stats[:, k, :])
                step(last)
                nc.vector.tensor_scalar(veps[:, :], mv[:, :, 1], LN_EPS, None, ALU.add).then_inc(eps_ready, 1)

                dve.wait_ge(pool_ready, 3)
                dve.wait_ge(w_in, 16 * 5)
                step(nc.vector.tensor_reduce(w_abs[:, 0:2 * Q_TILES], w_nat[:, :, :, :].rearrange("p g f d -> p (g f) d"), AX.X, ALU.max,
                                             apply_absolute_value=True))
                step(nc.vector.tensor_reduce(w_abs[:, 2 * Q_TILES:], wd_nat[:, :, :], AX.X, ALU.max, apply_absolute_value=True))
                step(nc.vector.tensor_scalar(w_scale[:, :], w_abs[:, :], 1.0 / QMAX, None, ALU.mult))
                step(nc.vector.tensor_scalar(w_inv[:, :], w_scale[:, :], TINY, None, ALU.max))
                step(nc.vector.reciprocal(w_inv[:, :], w_inv[:, :]))
                for g in range(2):
                    for f in range(Q_TILES):
                        quantise(w_nat[:, g, f, :], w_inv[:, g * Q_TILES + f:g * Q_TILES + f + 1])
                for t in range(2):
                    quantise(wd_nat[:, t, :], w_inv[:, 2 * Q_TILES + t:2 * Q_TILES + t + 1])
                nc.vector.tensor_scalar(w_q[:, :, :, :].rearrange("p g f d -> p (g f d)"), w_nat[:, :, :, :].rearrange("p g f d -> p (g f d)"),
                                        ROUND, None, ALU.subtract).then_inc(wq_ready, 1)
                nc.vector.tensor_scalar(wd_q[:, :, :].rearrange("p t f -> p (t f)"), wd_nat[:, :, :].rearrange("p t f -> p (t f)"),
                                        ROUND, None, ALU.subtract).then_inc(wq_ready, 1)

                dve.wait_ge(rstd_ready, 1)
                for k in range(TILES):
                    last = nc.vector.tensor_scalar(y_sb[:, k, :], x_sb[:, k, :], mv[:, k, 0:1], rstd[:, k:k + 1], ALU.subtract, ALU.mult)
                step(last)
                flat = big[:, 0:FLAT]
                nc.vector.tensor_reduce(part[:, 0:1], flat, AX.X, ALU.max, apply_absolute_value=True).then_inc(part_ready, 1)

                def activation_scale(k):
                    col = slice(k, k + 1)
                    dve.wait_ge(amax_ready, k + 1)
                    step(nc.vector.tensor_tensor(scale[:, col], sig[:, col], amax[:, col], ALU.mult))
                    step(nc.vector.tensor_scalar(scale[:, col], scale[:, col], 1.0 / QMAX, None, ALU.mult))
                    step(nc.vector.tensor_scalar(inv[:, col], scale[:, col], TINY, None, ALU.max))
                    step(nc.vector.reciprocal(inv[:, col], inv[:, col]))

                dve.wait_ge(sig_ready, 1)
                activation_scale(0)
                for k in range(CHUNKS):
                    part_flat = flat[:, k * GROUP * DIM:(k + 1) * GROUP * DIM]
                    quantise(part_flat, inv[:, 0:1])
                    nc.vector.tensor_scalar(yq[:, GROUP * k:GROUP * (k + 1), :].rearrange("p t d -> p (t d)"), part_flat, ROUND, None,
                                            ALU.subtract).then_inc(q_ready, 1)
                nc.vector.tensor_scalar(w_act[:, :], w_scale[:, 0:2 * Q_TILES], scale[:, 0:1], None, ALU.mult).then_inc(scales_ready, 1)
                dve.wait_ge(scales_ready, 1)
                dve.wait_ge(q_ready, CHUNKS)

                for k, (f, c) in enumerate(UNITS):
                    rows, (at, cols) = tile_rows(f), Q_CHUNKS[c]
                    dve.wait_ge(silu_done, k + 1)
                    nc.vector.scalar_tensor_tensor(h_sb[0:rows, f, at:at + cols], up_ps[k % 2][0:rows, 0:cols],
                                                   w_act[0:rows, Q_TILES + f:Q_TILES + f + 1], silu_sb[0:rows, k % 2, 0:cols],
                                                   ALU.mult, ALU.mult).then_inc(hid_done, 1)
                    if k == 0:
                        step(nc.vector.memset(hmaxes[:, :], 0.0))
                    dve.wait_ge(hid_done, k + 1)
                    last = nc.vector.tensor_reduce(hmaxes[0:rows, k:k + 1], h_sb[0:rows, f, at:at + cols], AX.X, ALU.max,
                                                   apply_absolute_value=True)
                step(last)
                nc.vector.tensor_reduce(part[:, 1:2], hmaxes[:, :], AX.X, ALU.max).then_inc(part_ready, 1)
                activation_scale(1)

                for t in range(2):
                    step(nc.vector.tensor_scalar(dsc[:, t:t + 1], w_scale[:, 2 * Q_TILES + t:2 * Q_TILES + t + 1], scale[:, 1:2], None, ALU.mult))
                    step(nc.vector.tensor_scalar(diag[:, t, :], ident[:, :], dsc[:, t:t + 1], None, ALU.mult))
                nc.vector.memset(dsc[:, :], 0.0).then_inc(scales_ready, 1)
                dve.wait_ge(row_full, 1)
                step(nc.vector.tensor_copy(down_row[:, :], banks[0][:, 0:DIM]))

                def combine(k):
                    dve.wait_ge(o_full, k + 1)
                    if k >= 2:
                        dve.wait_ge(stored[k % 2], 16 * (k // 2))
                    nc.vector.tensor_tensor(out_sb[:, k % 2, :], y_ps[k % 2][:, 0:DIM], down_row[:, :], ALU.mult).then_inc(o_mul, 1)
                    dve.wait_ge(o_mul, k + 1)
                    nc.vector.tensor_tensor(out_sb[:, k % 2, :], out_sb[:, k % 2, :], x_sb[:, k, :], ALU.add).then_inc(o_done, 1)

                for k in range(TILES):
                    if k >= 2:
                        dve.wait_ge(hq16_ready, k - 1)
                    for lo, hi, rows in ((0, Q_TILES - 1, P), (Q_TILES - 1, Q_TILES, Q_LAST)):
                        dst, src = hq[0:rows, k % 2, lo:hi, :], h_sb[0:rows, lo:hi, P * k:P * (k + 1)]
                        step(nc.vector.tensor_scalar(dst, src, inv[0:rows, 1:2], ROUND, ALU.mult, ALU.add))
                        last = nc.vector.tensor_scalar(dst, dst, ROUND + QMAX, ROUND - QMAX - 1.0, ALU.min, ALU.max)
                    last.then_inc(hq_ready, 1)
                    if k >= 1:
                        combine(k - 1)
                combine(TILES - 1)

            @block.tensor
            def _(pe):
                pe.wait_ge(sig_ready, 2)
                pe.wait_ge(wq_ready, 2)
                for k, (what, i, t) in enumerate(W_TURNS):
                    if k >= 2:
                        pe.wait_ge(t_done, k - 1)
                    if what == "gu":
                        for f in range(Q_TILES):
                            last = nc.tensor.transpose(banks16[k % 2][:, P * f:P * (f + 1)], w_q[:, i, f, P * t:P * (t + 1)], ident16[:, :])
                    else:
                        rows = tile_rows(i)
                        for d in range(2):
                            last = nc.tensor.transpose(banks16[k % 2][0:rows, P * d:P * (d + 1)], wd_q[:, d, P * i:P * i + rows], ident16[:, :])
                    last.then_inc(t_full, 1)
                n = len(W_TURNS)
                for k, (at, cols) in enumerate(Q_CHUNKS):
                    pe.wait_ge(t_done, n + k - 1)
                    pe.wait_ge(q_ready, -(-(at + cols) // CHUNK))
                    for t in range(2):
                        for j in range(cols // P):
                            col = QCOLS * t + P * j
                            last = nc.tensor.transpose(banks16[k % 2][:, col:col + P], yq[:, at // P + j, P * t:P * (t + 1)], ident16[:, :])
                    last.then_inc(t_full, 1)
                for k, (f, c) in enumerate(UNITS):
                    rows, (at, cols) = tile_rows(f), Q_CHUNKS[c]
                    pe.wait_ge(t_done, n + c + 1)
                    if k >= 2:
                        pe.wait_ge(hid_done, k - 1)
                    for g, ps in ((0, gate_ps), (1, up_ps)):
                        for t in range(2):
                            last = nc.tensor.matmul(ps[k % 2][0:rows, 0:cols], w_t[:, g, t, P * f:P * f + rows], yq_t[:, t, at:at + cols],
                                                    start=(t == 0), stop=(t == 1))
                    last.then_inc(gu_full, 1)
                pe.wait_ge(scales_ready, 2)
                for t in range(2):
                    last = nc.tensor.matmul(banks[0][:, P * t:P * (t + 1)], ones[:, :], diag[:, t, :], start=True, stop=True)
                last.then_inc(row_full, 1)
                for k in range(TILES):
                    pe.wait_ge(hq16_ready, k + 1)
                    if k >= 2:
                        pe.wait_ge(o_done, k - 1)
                    for f in range(Q_TILES):
                        rows = tile_rows(f)
                        last = nc.tensor.matmul(y_ps[k % 2][:, 0:DIM], hq16[0:rows, k % 2, f, :], wd_t[0:rows, f, :],
                                                start=(f == 0), stop=(f == Q_TILES - 1))
                    last.then_inc(o_full, 1)


MLP_NAMES = ["mlp_gate", "mlp_up", "mlp_down", "mlp_clip_x", "mlp_clip_down"]


ATT_COMMON = ["ctx_main", "ctx_rem", "identity"]
ATT_NAMES = [["a0_wq", "a0_wk_main", "a0_wk_rem", "a0_wv_main", "a0_wv_rem", "a0_wo", "a0_bo"],
             ["a1_wq", "a1_wk_main", "a1_wk_rem", "a1_wv_main", "a1_wv_rem", "a1_wo", "a1_bo", "a1_mask", "a1_gamma", "a1_beta"]]


ALL_NAMES = ["x"] + ATT_COMMON + ATT_NAMES[0] + ATT_NAMES[1] + MOE_NAMES + MLP_NAMES


def build(nc, d, out):
    rows = [nc.dram_tensor(f"rows{i}", (TOKENS, DIM), F32, kind="Internal").ap() for i in range(3)]
    run_attention(nc, 0, d, d["x"], rows[0])
    moe_phase(nc, rows[0], rows[1], *[d[n] for n in MOE_NAMES], d["identity"])
    run_attention(nc, 1, d, rows[1], rows[2])
    mlp_phase(nc, rows[2], out, *[d[n] for n in MLP_NAMES], d["identity"])


def run_attention(nc, layer, d, x_in, x_out):
    w = [d[n] for n in ATT_NAMES[layer]]
    attention_phase(nc, f"att{layer}", x_in, x_out, d["ctx_main"], d["ctx_rem"], *w[:7], d["identity"], *w[7:])


def layout(inputs):
    a = {k: np.asarray(v) for k, v in inputs.items()}
    out = {"x": a["x"].reshape(TOKENS, DIM), "identity": np.eye(P, dtype=np.float32)}
    ctx_t = a["ctx_768"].reshape(BATCH * KEYS, CTX).T
    out["ctx_main"] = ctx_t[0:P]
    out["ctx_rem"] = np.concatenate([ctx_t[P:CTX], ctx_t[P:CTX]])
    kv = a["L1_xattn_Wkv"]
    for layer, wk, wv in ((0, a["L0_xattn_Wk"], a["L0_xattn_Wv"]), (1, kv[:, 0:INNER], kv[:, INNER:])):
        n = f"a{layer}_"
        out[n + "wq"] = a[f"L{layer}_xattn_Wq"].reshape(2, P, INNER).transpose(1, 0, 2).reshape(P, 2 * INNER)
        for what, w in (("wk", wk), ("wv", wv)):
            out[n + what + "_main"] = w[0:P]
            out[n + what + "_rem"] = np.concatenate([w[P:CTX], w[P:CTX]])
        out[n + "wo"] = a[f"L{layer}_xattn_Wo"].reshape(PAIRS, P, DIM).transpose(1, 0, 2)
        out[n + "bo"] = a[f"L{layer}_xattn_bo"].reshape(1, DIM)
    out["a1_mask"] = a["mask_1x1xSxS2_bk0"].reshape(SEQ, KEYS)
    out["a1_gamma"] = a["L1_xattn_ln_gamma"].reshape(2, P).T
    out["a1_beta"] = a["L1_xattn_ln_beta"].reshape(2, P).T
    layout_moe(a, out)
    out["mlp_gate"], out["mlp_up"], out["mlp_down"] = (a[f"L1_ffn_w_{n}"] for n in ("gate", "up", "down"))
    out["mlp_clip_x"], out["mlp_clip_down"] = a["L1_ffn_clip_x"].reshape(1, 1), a["L1_ffn_clip_down"].reshape(1, 1)
    return {k: np.ascontiguousarray(v) for k, v in out.items()}


def kernel(**inputs):
    import concourse.bacc as bacc
    from concourse.bass_utils import run_bass_kernel_spmd

    nc = bacc.Bacc("TRN2", target_bir_lowering=False, num_devices=1)
    arrays = layout(inputs)
    aps = {n: nc.dram_tensor(f"in_{n}", arrays[n].shape, mybir.dt.from_np(arrays[n].dtype), kind="ExternalInput").ap() for n in ALL_NAMES}
    out = nc.dram_tensor("y", (TOKENS, DIM), F32, kind="ExternalOutput").ap()
    build(nc, aps, out)
    r = run_bass_kernel_spmd(nc, [{f"in_{n}": arrays[n] for n in ALL_NAMES}], core_ids=[0])
    return r.results[0]["y"].reshape(BATCH, SEQ, DIM)
```

```python
from contextlib import ExitStack

import numpy as np

import concourse.bass as bass
from concourse import mybir

F32 = mybir.dt.float32
F16 = mybir.dt.float16
I32, U32 = mybir.dt.int32, mybir.dt.uint32
ALU = mybir.AluOpType
ACT = mybir.ActivationFunctionType
AX = mybir.AxisListType

P = 128
BATCH, SEQ, DIM = 32, 100, 256
KEYS, CTX = 361, 192
HEADS, HEAD = 16, 64
INNER = HEADS * HEAD
PAIRS = HEADS // 2
KEY_TILES = 3
LAST_KEYS = KEYS - 2 * P
TOKENS = BATCH * SEQ
LN_EPS = 1e-5

X_SCALE = 64.0
CTX_SCALE = 64.0
W_SCALE = 256.0
QK_SCALE = 16.0
Q_EVAC = QK_SCALE / (X_SCALE * W_SCALE)
K_EVAC = QK_SCALE / (CTX_SCALE * W_SCALE)
V_EVAC = 1.0 / (CTX_SCALE * W_SCALE)
SCORE_SCALE = HEAD ** -0.5 / (QK_SCALE * QK_SCALE)
MASKED = -1e30

T_LAG, AV_LAG = 3, 4
O_STEP, XT_STEP = 5, 6
K_JOBS, Q_JOBS, V_JOBS = 8, 2, 6


def attention_phase(nc, name, x_in, x_out, ctx_main, ctx_rem, wq, wk_main, wk_rem, wv_main, wv_rem, wo,
                    bo_row, identity, mask=None, gamma=None, beta=None):
    second_ln = gamma is not None
    LNS = 2 if second_ln else 1
    with ExitStack() as ctx:
        def sb(label, shape, dt):
            return ctx.enter_context(nc.sbuf_tensor(f"{name}_{label}", shape, dt))

        used_semaphores = []

        def sem(label):
            used_semaphores.append(ctx.enter_context(nc.semaphore(f"{name}_{label}")))
            return used_semaphores[-1]

        w_stage = sb("w_stage", [P, 2, 2 * INNER], F32)
        wq_hi, wq_lo = sb("wq_hi", [P, 2 * INNER], F16), sb("wq_lo", [P, 2 * INNER], F16)
        wkv_hi = sb("wkv_hi", [P, 2, INNER], F16)
        wkv_lo = sb("wkv_lo", [P, 2, INNER], F16)
        wkv_rem_hi = sb("wkv_rem_hi", [P, 2, INNER], F16)
        wkv_rem_lo = sb("wkv_rem_lo", [P, 2, INNER], F16)
        wo_sb = sb("wo", [P, PAIRS, DIM], F32)
        bo_sb = sb("bo", [SEQ, DIM], F32)
        ident = sb("ident", [P, P], F32)
        expo = sb("expo", [SEQ, 1], F32)
        if second_ln:
            gb = sb("gb", [P, 2, 2], F32)
            gbs = sb("gbs", [P, 2, 2], F32)
            maskb = sb("maskb", [SEQ, KEYS], F32)
            mask_in = sb("mask_in", [SEQ, KEYS], mask.dtype)
            masked = sb("masked", [SEQ, 2, KEYS], F32)

        x_sb = sb("x", [SEQ, 2, DIM], F32)
        xb = sb("xb", [SEQ, 2, DIM], F32)
        xn = sb("xn", [SEQ, LNS, DIM], F32)
        stats = sb("stats", [SEQ, LNS, 6], F32)
        mv = sb("mv", [SEQ, LNS, 2], F32)
        veps = sb("veps", [SEQ, LNS], F32)
        rstd = sb("rstd", [SEQ, LNS], F32)
        c_main = sb("c_main", [P, 2, KEYS], F32)
        c_rem = sb("c_rem", [P, 2, KEYS], F32)
        c_hi = sb("c_hi", [P, 2, KEYS], F16)
        c_lo = sb("c_lo", [P, 2, KEYS], F16)
        c_stack = sb("c_stack", [P, 2, KEYS], F16)
        xt32 = sb("xt32", [P, 2 * SEQ], F32)
        xt_hi, xt_lo = sb("xt_hi", [P, 2 * SEQ], F16), sb("xt_lo", [P, 2 * SEQ], F16)
        k_stack = sb("k_stack", [P, 2, HEADS, KEYS], F16)
        q_hi = sb("q_hi", [P, 2, 2, PAIRS * SEQ], F16)
        q_lo = sb("q_lo", [P, 2, PAIRS * SEQ], F16)
        v_sb = sb("v", [P, 2, KEY_TILES, INNER], F32)
        probs = sb("probs", [SEQ, 4, KEY_TILES * P], F32)
        rowmax = sb("rowmax", [SEQ, HEADS], F32)
        bias = sb("bias", [SEQ, HEADS], F32)
        rowsum = sb("rowsum", [SEQ, HEADS], F32)
        rinv = sb("rinv", [SEQ, HEADS], F32)
        pt_sb = sb("pt", [P, 2, KEY_TILES * SEQ], F32)
        ot_sb = sb("ot", [P, PAIRS * SEQ], F32)
        out_sb = sb("out", [SEQ, 2, DIM], F32)

        def bank(label):
            return ctx.enter_context(nc.psum_tensor(f"{name}_{label}", [P, 512], F32))

        score_ps = [bank(f"score{i}") for i in range(2)]
        ring_ps = [bank(f"ring{i}") for i in range(2)]
        pt_ps = [bank(f"ptps{i}") for i in range(2)]
        av_ps = [bank(f"av{i}") for i in range(2)]

        const_in = sem("const_in")
        stage_in = [sem(f"stage_in{i}") for i in range(2)]
        stage_hi, stage_lo = sem("stage_hi"), sem("stage_lo")
        consts_ready = sem("consts_ready")
        carried = sem("carried")
        mask_step = sem("mask_step")
        x_landed = [sem(f"x_landed{i}") for i in range(2)]
        c_landed = [sem(f"c_landed{i}") for i in range(2)]
        stored = [sem(f"stored{i}") for i in range(2)]
        ln_stats, ln_aggr, ln_eps, ln_rstd, xn_ready = (sem(s) for s in ("ln_stats", "ln_aggr", "ln_eps", "ln_rstd", "xn_ready"))
        xb_ready, c_scaled, c_his, c_los, c_ready = (sem(s) for s in ("xb_ready", "c_scaled", "c_his", "c_los", "c_ready"))
        xth_ready, xt_ready = sem("xth_ready"), sem("xt_ready")
        ring_full = [sem(f"ring_full{i}") for i in range(2)]
        ring_free = [sem(f"ring_free{i}") for i in range(2)]
        hi_done = sem("hi_done")
        score_full, max_done, bias_done, exp_done = (sem(s) for s in ("score_full", "max_done", "bias_done", "exp_done"))
        rinv_done, norm_done, pt_full, pt_done = (sem(s) for s in ("rinv_done", "norm_done", "pt_full", "pt_done"))
        av_full, ot_done = sem("av_full"), sem("ot_done")

        JOBS = [("k", j) for j in range(K_JOBS)] + [("q", j) for j in range(Q_JOBS)] + [("v", j) for j in range(V_JOBS)]
        PER_BODY = len(JOBS) + 2

        def step_slots(s, project, output):
            out = [JOBS[s]] if project else []
            if output and s == O_STEP:
                out.append(("o", 0))
            if project and s == XT_STEP:
                out.append(("xt", 0))
            return out

        def slot_number(b, slot, kind):
            if kind == "prologue":
                n = ([("xt", 0)] + JOBS).index(slot)
                return n % 2, n // 2
            base = len(JOBS) + 1
            if kind == "tail":
                n = base + PER_BODY * (BATCH - 1) - 1 + 1
                return n % 2, n // 2
            order = [x for s in range(HEADS) for x in step_slots(s, kind != "last", kind != "first")]
            n = base + order.index(slot)
            if kind != "first":
                n -= 1
            return n % 2, n // 2 + (PER_BODY // 2) * b

        def carry(eng):
            eng.sem_inc(carried, 1)

        def alone(eng, semaphore, value):
            eng.wait_ge(semaphore, value)
            if not isinstance(value, int):
                carry(eng)

        def wait_emptied(eng, b, slot, kind):
            bk, used = slot_number(b, slot, kind)
            eng.wait_ge(ring_free[bk], used + 1)

        def wait_projected(eng, b, slot):
            if isinstance(b, int) and b == 0:
                wait_emptied(eng, 0, slot, "prologue")
            else:
                wait_emptied(eng, b - 1, slot, "mid")

        last_b = BATCH - 1

        def wait_output(eng, b, kind):
            wait_emptied(eng, b + 1, ("o", 0), kind)

        def each_batch(eng, body):
            body(0, 0, 0, "first")
            body(1, 1, 0, "mid")
            body(2, 0, 1, "mid")
            with eng.Fori(1, (BATCH - 4) // 2) as i:
                body(2 * i + 1, 1, i, "mid")
                body(2 * i + 2, 0, i + 1, "mid")
            body(BATCH - 3, 1, (BATCH - 3) // 2, "mid")
            body(BATCH - 2, 0, (BATCH - 2) // 2, "penultimate")
            body(BATCH - 1, 1, (BATCH - 1) // 2, "last")

        with nc.Block() as block:

            @block.sync
            def _(sp):
                def load_x(b, par, half, reuse):
                    if reuse:
                        sp.wait_ge(xb_ready, b - 1)
                        carry(sp)
                        sp.wait_ge(xn_ready, LNS * (b - 1))
                        carry(sp)
                    sp.dma_start(x_sb[:, par, :], x_in[bass.ds(b * SEQ, SEQ), :]).then_inc(x_landed[par], 16)

                def load_c(b, par, half, reuse):
                    if reuse:
                        sp.wait_ge(c_ready, b - 1)
                        carry(sp)
                        sp.wait_ge(c_los, b - 1)
                        carry(sp)
                    sp.dma_start(c_main[:, par, :], ctx_main[:, bass.ds(b * KEYS, KEYS)]).then_inc(c_landed[par], 16)
                    sp.dma_start(c_rem[:, par, :], ctx_rem[:, bass.ds(b * KEYS, KEYS)]).then_inc(c_landed[par], 16)

                def store(b, par, half, kind="mid"):
                    wait_output(sp, b, kind)
                    carry(sp)
                    sp.dma_start(x_out[bass.ds(b * SEQ, SEQ), :], out_sb[:, par, :]).then_inc(stored[par], 16)

                sp.dma_start(ident[:, :], identity).then_inc(const_in, 16)
                sp.dma_start(w_stage[:, 0, :], wq).then_inc(stage_in[0], 16)
                load_c(0, 0, 0, False)
                load_x(0, 0, 0, False)
                sp.dma_start(w_stage[:, 1, 0:INNER], wk_main).then_inc(stage_in[1], 16)
                sp.dma_start(w_stage[:, 1, INNER:2 * INNER], wv_main).then_inc(stage_in[1], 16)
                if second_ln:
                    sp.dma_start(gb[:, 0, :], gamma).then_inc(const_in, 16)
                    sp.dma_start(gb[:, 1, :], beta).then_inc(const_in, 16)
                    sp.dma_start(mask_in[:, :], mask).then_inc(const_in, 16)
                sp.dma_start(bo_sb[:, :], bo_row.to_broadcast([SEQ, DIM])).then_inc(const_in, 16)
                sp.dma_start(wo_sb[:, :, :], wo).then_inc(const_in, 16)
                load_c(1, 1, 0, False)
                load_x(1, 1, 0, False)
                sp.wait_ge(stage_lo, 1)
                sp.dma_start(w_stage[:, 0, 0:INNER], wk_rem).then_inc(stage_in[0], 16)
                sp.dma_start(w_stage[:, 0, INNER:2 * INNER], wv_rem).then_inc(stage_in[0], 16)

                def body(b, par, half, kind):
                    if kind != "last":
                        load_later(b + 2, par, half + 1)
                    if kind != "first":
                        store(b - 1, 1 - par, half - 1 if par == 0 else half)

                def load_later(b, par, half):
                    load_x(b, par, half, True)
                    load_c(b, par, half, True)

                body(0, 0, 0, "first")
                with sp.Fori(0, (BATCH - 4) // 2) as i:
                    body(2 * i + 1, 1, i, "mid")
                    body(2 * i + 2, 0, i + 1, "mid")
                body(BATCH - 3, 1, 0, "mid")
                store(BATCH - 3, 1, 0)
                store(BATCH - 2, 0, 0, "last")
                store(BATCH - 1, 1, 0, "tail")
                for par in range(2):
                    sp.wait_ge(stored[par], 16 * (BATCH // 2))

            @block.gpsimd
            def _(pool):
                def rstds(n, ln):
                    k = LNS * n + ln
                    alone(pool, ln_aggr, k + 1)
                    nc.gpsimd.tensor_scalar(veps[:, ln:ln + 1], mv[:, ln, 1:2], LN_EPS, None, ALU.add).then_inc(ln_eps, 1)
                    pool.wait_ge(ln_eps, k + 1)
                    nc.gpsimd.tensor_tensor(rstd[:, ln:ln + 1], veps[:, ln:ln + 1], expo[:, :], ALU.pow).then_inc(ln_rstd, 1)

                def add_bias(n, par, reuse):
                    if reuse:
                        wait_output(pool, n - 2, "mid")
                    nc.gpsimd.tensor_tensor(xb[:, par, :], x_sb[:, par, :], bo_sb[:, :], ALU.add).then_inc(xb_ready, 1)

                def scale_context(n, par, half, reuse):
                    if reuse:
                        pool.wait_ge(score_full, HEADS * (n - 2) + 1)
                    alone(pool, c_landed[par], 32 * half + 32)
                    nc.gpsimd.tensor_scalar(c_main[:, par, :], c_main[:, par, :], CTX_SCALE, 1.0, ALU.mult, ALU.mult)
                    nc.gpsimd.tensor_scalar(c_rem[:, par, :], c_rem[:, par, :], CTX_SCALE, 1.0, ALU.mult, ALU.mult).then_inc(c_scaled, 1)

                def context_lo(n, par):
                    pool.wait_ge(c_his, n + 1)
                    nc.gpsimd.tensor_tensor(c_lo[:, par, :], c_main[:, par, :], c_hi[:, par, :], ALU.subtract).then_inc(c_los, 1)

                def split_xt(n):
                    wait_projected(pool, n, ("xt", 0))
                    carry(pool)
                    nc.gpsimd.tensor_copy(xt_hi[:, :], xt32[:, :]).then_inc(xth_ready, 1)
                    pool.wait_ge(xth_ready, n + 1)
                    nc.gpsimd.tensor_tensor(xt_lo[:, :], xt32[:, :], xt_hi[:, :], ALU.subtract).then_inc(xt_ready, 1)

                def normalise(b, h):
                    alone(pool, rinv_done, HEADS * b + h + 1)
                    nc.gpsimd.tensor_scalar(probs[:, h % 4, 0:KEYS], probs[:, h % 4, 0:KEYS], rinv[:, h:h + 1], 1.0,
                                            ALU.mult, ALU.mult).then_inc(norm_done, 1)

                nc.gpsimd.memset(expo[:, :], -0.5).then_inc(consts_ready, 1)
                nc.gpsimd.memset(probs[:, :, KEYS:KEY_TILES * P], 0.0).then_inc(consts_ready, 1)
                pool.wait_ge(consts_ready, 2)
                scale_context(0, 0, 0, False)
                context_lo(0, 0)
                for ln in range(LNS):
                    rstds(0, ln)
                pool.wait_ge(const_in, 16 * (6 if second_ln else 3))
                if second_ln:
                    nc.gpsimd.tensor_scalar(gbs[:, :, :].rearrange("p a b -> p (a b)"), gb[:, :, :].rearrange("p a b -> p (a b)"),
                                            X_SCALE, 1.0, ALU.mult, ALU.mult).then_inc(consts_ready, 1)
                    nc.gpsimd.tensor_copy(maskb[:, :], mask_in[:, :]).then_inc(mask_step, 1)
                    pool.wait_ge(mask_step, 1)
                    nc.gpsimd.tensor_scalar(maskb[:, :], maskb[:, :], -MASKED, MASKED, ALU.mult, ALU.add).then_inc(mask_step, 1)
                add_bias(0, 0, False)
                split_xt(0)
                scale_context(1, 1, 0, False)
                context_lo(1, 1)

                def body(b, par, half, kind):
                    if kind != "first":
                        normalise(b - 1, HEADS - 1)
                    for s in range(HEADS):
                        if s >= 1:
                            normalise(b, s - 1)
                        if kind == "last":
                            continue
                        if s == 1:
                            rstds(b + 1, 0)
                        if s == 3 and second_ln:
                            rstds(b + 1, 1)
                        if s == XT_STEP + 1:
                            split_xt(b + 1)
                        if s == 10:
                            add_bias(b + 1, 1 - par, kind != "first")
                        if kind in ("first", "mid"):
                            if s == 2:
                                scale_context(b + 2, par, half + 1, True)
                            if s == 4:
                                context_lo(b + 2, par)

                each_batch(pool, body)
                normalise(BATCH - 1, HEADS - 1)

            @block.scalar
            def _(act):
                def context_hi(n, par):
                    alone(act, c_scaled, n + 1)
                    nc.scalar.activation(c_hi[:, par, :], c_main[:, par, :], ACT.Copy)
                    nc.scalar.activation(c_stack[:, par, :], c_rem[:, par, :], ACT.Copy).then_inc(c_his, 1)

                context_hi(0, 0)
                for k, (src, dst) in enumerate(((0, wq_hi), (1, wkv_hi), (0, wkv_rem_hi))):
                    act.wait_ge(stage_in[src], (16, 32, 48)[k])
                    flat = dst[:, :] if k == 0 else dst[:, :, :].rearrange("p a b -> p (a b)")
                    nc.scalar.activation(flat, w_stage[:, src, :], ACT.Copy, scale=W_SCALE).then_inc(stage_hi, 1)

                def evac_xt(n, kind, b):
                    bk, used = slot_number(b, ("xt", 0), kind)
                    act.wait_ge(ring_full[bk], used + 1)
                    if kind == "prologue":
                        if second_ln:
                            act.wait_ge(consts_ready, 3)
                    else:
                        act.wait_ge(xt_ready, n)
                    if second_ln:
                        for t in range(2):
                            last = nc.scalar.activation(xt32[:, t * SEQ:(t + 1) * SEQ], ring_ps[bk][:, t * SEQ:(t + 1) * SEQ],
                                                        ACT.Identity, scale=gbs[:, 0, t:t + 1], bias=gbs[:, 1, t:t + 1])
                    else:
                        last = nc.scalar.activation(xt32[:, :], ring_ps[bk][:, 0:2 * SEQ], ACT.Copy, scale=X_SCALE)
                    last.then_inc(ring_free[bk], 1)

                def job(n, par, slot, kind, b):
                    what, j = slot
                    bk, used = slot_number(b, slot, kind)
                    act.wait_ge(ring_full[bk], used + 1)
                    if what == "k":
                        for r in range(2):
                            rows = slice(HEAD * r, HEAD * r + HEAD)
                            last = nc.scalar.activation(k_stack[rows, par, 2 * j + r, :], ring_ps[bk][rows, 0:KEYS],
                                                        ACT.Copy, scale=K_EVAC)
                            last.then_inc(hi_done, 1)
                    if what == "q":
                        cols = slice(4 * SEQ * j, 4 * SEQ * (j + 1))
                        for r in range(2):
                            for half_rows in range(2):
                                last = nc.scalar.activation(q_hi[HEAD * half_rows:HEAD * (half_rows + 1), par, r, cols],
                                                            ring_ps[bk][HEAD * r:HEAD * (r + 1), 0:4 * SEQ],
                                                            ACT.Copy, scale=Q_EVAC)
                        last.then_inc(hi_done, 2)
                    if what == "v":
                        t, c = j // 2, j % 2
                        rows = LAST_KEYS if t == 2 else P
                        last = nc.scalar.activation(v_sb[0:rows, par, t, 512 * c:512 * (c + 1)], ring_ps[bk][0:rows, :],
                                                    ACT.Copy, scale=V_EVAC)
                        last.then_inc(ring_free[bk], 1)

                def exp(b, h):
                    act.wait_ge(bias_done, HEADS * b + h + 1)
                    if not (isinstance(b, int) and b == 0 and h < 4):
                        act.wait_ge(pt_full, HEADS * b + h - 3)
                    src = masked[:, h % 2, :] if second_ln else score_ps[h % 2][0:SEQ, 0:KEYS]
                    nc.scalar.activation(probs[:, h % 4, 0:KEYS], src, ACT.Exp, scale=SCORE_SCALE, bias=bias[:, h:h + 1],
                                         accum_out=rowsum[:, h:h + 1]).then_inc(exp_done, 1)

                def evac_av(b, c):
                    act.wait_ge(av_full, HEADS * b + 8 * (c + 1))
                    nc.scalar.activation(ot_sb[:, 4 * SEQ * c:4 * SEQ * (c + 1)], av_ps[c][:, 0:4 * SEQ], ACT.Copy).then_inc(ot_done, 1)

                act.wait_ge(consts_ready, 2)
                evac_xt(0, "prologue", 0)
                for slot in JOBS:
                    job(0, 0, slot, "prologue", 0)
                context_hi(1, 1)

                def body(b, par, half, kind):
                    for s in range(HEADS):
                        for slot in step_slots(s, kind != "last", kind != "first"):
                            if slot[0] == "xt":
                                evac_xt(b + 1, kind, b)
                            elif slot[0] != "o":
                                job(b + 1, 1 - par, slot, kind, b)
                        exp(b, s)
                        if s == 3 and kind in ("first", "mid"):
                            context_hi(b + 2, par)
                        if kind != "first" and s == AV_LAG - 1:
                            evac_av(b - 1, 1)
                        if s == 8 + AV_LAG - 1:
                            evac_av(b, 0)

                each_batch(act, body)
                evac_av(last_b, 1)

            @block.vector
            def _(dve):
                def split_weights(k, src, hi, lo):
                    dve.wait_ge(stage_hi, k + 1)
                    flat_hi = hi[:, :] if k == 0 else hi[:, :, :].rearrange("p a b -> p (a b)")
                    flat_lo = lo[:, :] if k == 0 else lo[:, :, :].rearrange("p a b -> p (a b)")
                    nc.vector.scalar_tensor_tensor(flat_lo, w_stage[:, src, :], W_SCALE, flat_hi, ALU.mult,
                                                   ALU.subtract).then_inc(stage_lo, 1)

                def layernorm_stats(n, par, half):
                    dve.wait_ge(x_landed[par], 16 * half + 16)
                    nc.vector.bn_stats(stats[:, 0, :], x_sb[:, par, :]).then_inc(ln_stats, 1)
                    alone(dve, ln_stats, LNS * n + 1)
                    nc.vector.bn_aggr(mv[:, 0, :], stats[:, 0, :]).then_inc(ln_aggr, 1)

                def layernorm_apply(n, par):
                    dve.wait_ge(ln_rstd, LNS * n + 1)
                    nc.vector.tensor_scalar(xn[:, 0, :], x_sb[:, par, :], mv[:, 0, 0:1], rstd[:, 0:1], ALU.subtract,
                                            ALU.mult).then_inc(xn_ready, 1)
                    if second_ln:
                        dve.wait_ge(xn_ready, LNS * n + 1)
                        nc.vector.bn_stats(stats[:, 1, :], xn[:, 0, :]).then_inc(ln_stats, 1)
                        alone(dve, ln_stats, LNS * n + 2)
                        nc.vector.bn_aggr(mv[:, 1, :], stats[:, 1, :]).then_inc(ln_aggr, 1)

                def layernorm_apply2(n):
                    dve.wait_ge(ln_rstd, LNS * n + 2)
                    nc.vector.tensor_scalar(xn[:, 1, :], xn[:, 0, :], mv[:, 1, 0:1], rstd[:, 1:2], ALU.subtract,
                                            ALU.mult).then_inc(xn_ready, 1)

                hi_per_batch = 2 * (K_JOBS + Q_JOBS)

                def job(n, par, slot, kind, b):
                    what, j = slot
                    bk, used = slot_number(b, slot, kind)
                    at = JOBS.index(slot)
                    for r in range(2):
                        rows, other = slice(HEAD * r, HEAD * r + HEAD), slice(HEAD * (1 - r), HEAD * (2 - r))
                        dve.wait_ge(hi_done, hi_per_batch * n + 2 * at + (r + 1 if what == "k" else 2))
                        if what == "k":
                            last = nc.vector.scalar_tensor_tensor(k_stack[other, par, 2 * j + r, :], ring_ps[bk][rows, 0:KEYS], K_EVAC,
                                                                  k_stack[rows, par, 2 * j + r, :], ALU.mult, ALU.subtract)
                        else:
                            cols = slice(4 * SEQ * j, 4 * SEQ * (j + 1))
                            last = nc.vector.scalar_tensor_tensor(q_lo[rows, par, cols], ring_ps[bk][rows, 0:4 * SEQ], Q_EVAC,
                                                                  q_hi[rows, par, r, cols], ALU.mult, ALU.subtract)
                    last.then_inc(ring_free[bk], 1)

                def row_max(b, h):
                    dve.wait_ge(score_full, HEADS * b + h + 1)
                    src = score_ps[h % 2][0:SEQ, 0:KEYS]
                    if second_ln:
                        if not (isinstance(b, int) and b == 0 and h < 2):
                            dve.wait_ge(exp_done, HEADS * b + h - 1)
                        carry(dve)
                        nc.vector.tensor_tensor_reduce(masked[:, h % 2, :], src, maskb[:, :], 1.0, -3.0e38, ALU.add, ALU.max,
                                                       rowmax[:, h:h + 1]).then_inc(max_done, 1)
                    else:
                        nc.vector.reduce_max(rowmax[:, h:h + 1], src, AX.X).then_inc(max_done, 1)
                    dve.wait_ge(max_done, HEADS * b + h + 1)
                    nc.vector.tensor_scalar(bias[:, h:h + 1], rowmax[:, h:h + 1], -SCORE_SCALE, None, ALU.mult).then_inc(bias_done, 1)

                def invert(b, h):
                    dve.wait_ge(exp_done, HEADS * b + h + 1)
                    nc.vector.reciprocal(rinv[:, h:h + 1], rowsum[:, h:h + 1]).then_inc(rinv_done, 1)

                def evac_pt(b, h):
                    dve.wait_ge(pt_full, HEADS * b + h + 1)
                    if not (isinstance(b, int) and b == 0 and h < 2):
                        dve.wait_ge(av_full, HEADS * b + h - 1)
                    nc.vector.tensor_copy(pt_sb[:, h % 2, :], pt_ps[h % 2][:, 0:KEY_TILES * SEQ]).then_inc(pt_done, 1)

                def output_sum(b, par, half, kind, body_b):
                    bk, used = slot_number(body_b, ("o", 0), kind)
                    dve.wait_ge(ring_full[bk], used + 1)
                    dve.wait_ge(xb_ready, b + 1)
                    if not (isinstance(b, int) and b < 2):
                        dve.wait_ge(stored[par], 16 * half)
                    nc.vector.tensor_tensor(out_sb[:, par, :], ring_ps[bk][0:SEQ, 0:DIM], xb[:, par, :],
                                            ALU.add).then_inc(ring_free[bk], 1)

                def context_stack_lo(n, par):
                    alone(dve, c_his, n + 1)
                    nc.vector.tensor_tensor(c_stack[HEAD:P, par, :], c_rem[HEAD:P, par, :], c_stack[HEAD:P, par, :],
                                            ALU.subtract).then_inc(c_ready, 1)

                layernorm_stats(0, 0, 0)
                context_stack_lo(0, 0)
                split_weights(0, 0, wq_hi, wq_lo)
                dve.wait_ge(consts_ready, 2)
                layernorm_apply(0, 0)
                split_weights(1, 1, wkv_hi, wkv_lo)
                if second_ln:
                    layernorm_apply2(0)
                    dve.wait_ge(mask_step, 2)
                split_weights(2, 0, wkv_rem_hi, wkv_rem_lo)
                for slot in JOBS:
                    if slot[0] != "v":
                        job(0, 0, slot, "prologue", 0)
                context_stack_lo(1, 1)

                def body(b, par, half, kind):
                    late = []
                    for s in range(HEADS):
                        for slot in late:
                            if slot[0] in "kq":
                                job(b + 1, 1 - par, slot, kind, b)
                            if slot[0] == "o":
                                output_sum(b - 1, 1 - par, half if par == 1 else half - 1, kind, b)
                        late = step_slots(s, kind != "last", kind != "first")
                        row_max(b, s)
                        if s >= 1:
                            invert(b, s - 1)
                        elif kind != "first":
                            invert(b - 1, HEADS - 1)
                        if s >= T_LAG:
                            evac_pt(b, s - T_LAG)
                        elif kind != "first":
                            evac_pt(b - 1, HEADS + s - T_LAG)
                        if kind != "last":
                            if s == 0:
                                layernorm_stats(b + 1, 1 - par, half if par == 0 else half + 1)
                            if s == 2:
                                layernorm_apply(b + 1, 1 - par)
                            if s == 5 and kind != "penultimate":
                                context_stack_lo(b + 2, par)
                            if s == 4 and second_ln:
                                layernorm_apply2(b + 1)

                each_batch(dve, body)
                invert(last_b, HEADS - 1)
                for h in range(HEADS - T_LAG, HEADS):
                    evac_pt(last_b, h)
                output_sum(last_b, 1, last_b // 2, "tail", 0)

            @block.tensor
            def _(pe):
                def take_slot(slot, kind, b):
                    bk, used = slot_number(b, slot, kind)
                    if not (isinstance(used, int) and used == 0):
                        pe.wait_ge(ring_free[bk], used)
                    return bk

                def transpose_x(kind, n, b):
                    bk = take_slot(("xt", 0), kind, b)
                    pe.wait_ge(xn_ready, LNS * (n + 1))
                    for t in range(2):
                        last = nc.tensor.transpose(ring_ps[bk][:, t * SEQ:(t + 1) * SEQ], xn[:, LNS - 1, t * P:(t + 1) * P],
                                                   ident[0:SEQ, 0:SEQ])
                    last.then_inc(ring_full[bk], 1)

                def job(slot, par, kind, n, b):
                    what, j = slot
                    bk = take_slot(slot, kind, b)
                    if slot == ("k", 0):
                        pe.wait_ge(c_los, n + 1)
                        pe.wait_ge(c_ready, n + 1)
                    if slot == ("q", 0):
                        pe.wait_ge(xt_ready, n + 1)
                    if what == "k":
                        cols = slice(P * j, P * (j + 1))
                        out = ring_ps[bk][:, 0:KEYS]
                        nc.tensor.matmul(out, wkv_hi[:, 0, cols], c_hi[:, par, :], start=True, stop=False)
                        nc.tensor.matmul(out, wkv_hi[:, 0, cols], c_lo[:, par, :], start=False, stop=False)
                        nc.tensor.matmul(out, wkv_lo[:, 0, cols], c_hi[:, par, :], start=False, stop=False)
                        nc.tensor.matmul(out, wkv_rem_hi[:, 0, cols], c_stack[:, par, :], start=False, stop=False)
                        last = nc.tensor.matmul(out, wkv_rem_lo[0:HEAD, 0, cols], c_stack[0:HEAD, par, :], start=False, stop=True)
                    if what == "q":
                        for g in range(4):
                            out = ring_ps[bk][:, SEQ * g:SEQ * (g + 1)]
                            for t in range(2):
                                w = slice(INNER * t + P * (4 * j + g), INNER * t + P * (4 * j + g + 1))
                                xs = slice(SEQ * t, SEQ * (t + 1))
                                nc.tensor.matmul(out, wq_hi[:, w], xt_hi[:, xs], start=(t == 0), stop=False)
                                nc.tensor.matmul(out, wq_hi[:, w], xt_lo[:, xs], start=False, stop=False)
                                last = nc.tensor.matmul(out, wq_lo[:, w], xt_hi[:, xs], start=False, stop=(t == 1))
                    if what == "v":
                        t, c = j // 2, j % 2
                        rows = LAST_KEYS if t == 2 else P
                        keys, cols = slice(P * t, P * t + rows), slice(512 * c, 512 * (c + 1))
                        out = ring_ps[bk][0:rows, :]
                        nc.tensor.matmul(out, c_hi[:, par, keys], wkv_hi[:, 1, cols], start=True, stop=False)
                        nc.tensor.matmul(out, c_hi[:, par, keys], wkv_lo[:, 1, cols], start=False, stop=False)
                        nc.tensor.matmul(out, c_lo[:, par, keys], wkv_hi[:, 1, cols], start=False, stop=False)
                        nc.tensor.matmul(out, c_stack[:, par, keys], wkv_rem_hi[:, 1, cols], start=False, stop=False)
                        last = nc.tensor.matmul(out, c_stack[0:HEAD, par, keys], wkv_rem_lo[0:HEAD, 1, cols], start=False, stop=True)
                    last.then_inc(ring_full[bk], 1)

                def scores(b, par, h):
                    if h == 0:
                        wait_projected(pe, b, ("q", Q_JOBS - 1))
                    if not (isinstance(b, int) and b == 0 and h < 2):
                        pe.wait_ge(max_done if second_ln else exp_done, HEADS * b + h - 1)
                    j, r = h // 2, h % 2
                    rows, cols = slice(HEAD * r, HEAD * (r + 1)), slice(SEQ * j, SEQ * (j + 1))
                    out = score_ps[h % 2][0:SEQ, 0:KEYS]
                    nc.tensor.matmul(out, q_hi[:, par, r, cols], k_stack[:, par, h, :], start=True, stop=False)
                    nc.tensor.matmul(out, q_lo[rows, par, cols], k_stack[rows, par, h, :], start=False, stop=True).then_inc(score_full, 1)

                def transpose_probs(b, h):
                    pe.wait_ge(norm_done, HEADS * b + h + 1)
                    if not (isinstance(b, int) and b == 0 and h < 2):
                        pe.wait_ge(pt_done, HEADS * b + h - 1)
                    for t in range(KEY_TILES):
                        last = nc.tensor.transpose(pt_ps[h % 2][:, SEQ * t:SEQ * (t + 1)], probs[:, h % 4, P * t:P * (t + 1)],
                                                   ident[0:SEQ, 0:SEQ])
                    last.then_inc(pt_full, 1)

                def values(b, par, h):
                    c, j, r = h // 8, (h % 8) // 2, h % 2
                    pe.wait_ge(pt_done, HEADS * b + h + 1)
                    if h == 0:
                        wait_projected(pe, b, ("v", V_JOBS - 2))
                        wait_projected(pe, b, ("v", V_JOBS - 1))
                    if h % 8 == 0 and not (isinstance(b, int) and b == 0):
                        pe.wait_ge(ot_done, 2 * b - 1 + c)
                    out = av_ps[c][HEAD * r:HEAD * (r + 1), SEQ * j:SEQ * (j + 1)]
                    for t in range(KEY_TILES):
                        rows = LAST_KEYS if t == 2 else P
                        last = nc.tensor.matmul(out, v_sb[0:rows, par, t, HEAD * h:HEAD * (h + 1)],
                                                pt_sb[0:rows, h % 2, SEQ * t:SEQ * (t + 1)], start=(t == 0), stop=(t == 2))
                    last.then_inc(av_full, 1)

                def output(b, kind, body_b):
                    bk = take_slot(("o", 0), kind, body_b)
                    pe.wait_ge(ot_done, 2 * b + 2)
                    for j in range(PAIRS):
                        last = nc.tensor.matmul(ring_ps[bk][0:SEQ, 0:DIM], ot_sb[:, SEQ * j:SEQ * (j + 1)], wo_sb[:, j, :],
                                                start=(j == 0), stop=(j == PAIRS - 1))
                    last.then_inc(ring_full[bk], 1)

                pe.wait_ge(const_in, 16 * (6 if second_ln else 3))
                transpose_x("prologue", 0, 0)
                pe.wait_ge(stage_lo, 3)
                for slot in JOBS:
                    job(slot, 0, "prologue", 0, 0)

                def body(b, par, half, kind):
                    for s in range(HEADS):
                        scores(b, par, s)
                        if s >= T_LAG:
                            transpose_probs(b, s - T_LAG)
                        elif kind != "first":
                            transpose_probs(b - 1, HEADS + s - T_LAG)
                        for slot in step_slots(s, kind != "last", kind != "first"):
                            if slot[0] == "xt":
                                transpose_x(kind, b + 1, b)
                            elif slot[0] == "o":
                                output(b - 1, kind, b)
                            else:
                                job(slot, 1 - par, kind, b + 1, b)
                        if s >= AV_LAG:
                            values(b, par, s - AV_LAG)
                        elif kind != "first":
                            values(b - 1, 1 - par, HEADS + s - AV_LAG)

                each_batch(pe, body)
                for s in range(HEADS, HEADS + AV_LAG):
                    if s < HEADS + T_LAG:
                        transpose_probs(last_b, s - T_LAG)
                    values(last_b, 1, s - AV_LAG)
                output(last_b, "tail", 0)

        return used_semaphores


EXPERTS, FF = 8, 816
TOP = 2
F_TILES = -(-FF // P)
F_LAST = FF - (F_TILES - 1) * P
TILES = TOKENS // P
GROUP = 5
GROUPS = TILES // GROUP
CHUNK = GROUP * P
BLOCKS = (TOP * TOKENS + EXPERTS * (P - 1)) // P
DUMP = TOP * TOKENS
H_SCALE = 16.0
GU_SCALE = X_SCALE * W_SCALE
Y_SCALE = H_SCALE * W_SCALE
UP_AT, DOWN_AT = 2 * FF, 4 * FF
EXPERT_COLS = 4 * FF + F_TILES * DIM
PIECE = EXPERT_COLS // 8
PIECES = EXPERTS * EXPERT_COLS // PIECE
PIECES_PER_GROUP = 6
HALF_TILES = (range(0, 4), range(4, F_TILES))
HALF_PARTS = (((P, 0, 4 * P),), ((P, 0, 2 * P), (F_LAST, 2 * P, 3 * P)))
T_BANK = 4 * P
FLOOR = 1.5 * 2.0 ** 23
FLOOR_SHIFT = 63.5 / P


def moe_alone(eng, semaphore, value, carried):
    eng.wait_ge(semaphore, value)
    if not isinstance(value, int):
        eng.sem_inc(carried, 1)


def moe_phase(nc, x_in, x_out, weights, gate_bias, up_bias, down_bias, router, router_bias, descending, numbers,
              tile_numbers, before, identity, finished):
    xn_rows = nc.dram_tensor("moe_xn", (TOKENS, DIM), F32, kind="Internal").ap()
    y_rows = nc.dram_tensor("moe_y", (DUMP + BLOCKS * P, DIM), F32, kind="Internal").ap()
    with nc.sbuf_tensor("moe_comb", [P, TILES * EXPERTS], F32) as comb, \
            nc.sbuf_tensor("moe_top_w", [P, TOP, TILES], F32) as top_w:
        with ExitStack() as ctx:
            def sb(label, shape, dt):
                return ctx.enter_context(nc.sbuf_tensor(f"moe_{label}", shape, dt))

            w_hi = sb("w_hi", [P, EXPERTS * EXPERT_COLS], F16)
            w_lo = sb("w_lo", [P, EXPERTS * EXPERT_COLS], F16)
            source = sb("source", [P, BLOCKS], U32)
            target = sb("target", [P, BLOCKS], U32)
            weights_at = sb("weights_at", [P, BLOCKS + 1], I32)
            biases_at = sb("biases_at", [P, BLOCKS + 1], I32)
            moe_route(nc, x_in, xn_rows, weights, router, router_bias, descending, numbers, tile_numbers, before,
                      identity, w_hi, w_lo, comb, top_w, source, target, weights_at, biases_at, finished)
            moe_experts(nc, xn_rows, y_rows, gate_bias, up_bias, identity, w_hi, w_lo, source, target, weights_at, biases_at)
        moe_sum(nc, x_in, y_rows, x_out, down_bias, identity, comb, top_w)


def moe_route(nc, x_in, xn_rows, weights, router, router_bias, descending, numbers, tile_numbers, before, identity,
              w_hi, w_lo, comb, top_w, source, target, weights_at, biases_at, finished):
    name = "route"
    with ExitStack() as ctx:
        def sb(label, shape, dt):
            return ctx.enter_context(nc.sbuf_tensor(f"{name}_{label}", shape, dt))

        def sem(label):
            return ctx.enter_context(nc.semaphore(f"{name}_{label}"))

        R = TILES * EXPERTS
        x_sb = sb("x", [P, 2, GROUP, DIM], F32)
        xn = sb("xn", [P, GROUP, DIM], F32)
        xt_hi = sb("xt_hi", [P, 2, CHUNK], F16)
        xt_lo = sb("xt_lo", [P, 2, CHUNK], F16)
        w_stage = sb("w_stage", [P, 2, PIECE], F32)
        ident = sb("ident", [P, P], F32)
        expo = sb("expo", [P, GROUP], F32)
        stats = sb("stats", [P, GROUP, 6], F32)
        mv = sb("mv", [P, GROUP, 2], F32)
        veps = sb("veps", [P, GROUP], F32)
        rstd = sb("rstd", [P, GROUP], F32)
        rt_in = sb("rt_in", [P, 2 * EXPERTS], F32)
        rt_hi = sb("rt_hi", [P, 2 * EXPERTS], F16)
        rt_lo = sb("rt_lo", [P, 2 * EXPERTS], F16)
        rtb = sb("rtb", [P, EXPERTS], F32)
        desc = sb("desc", [P, EXPERTS], F32)
        number = sb("number", [P, P + 1], F32)
        tile_no = sb("tile_no", [P, TOP * TILES + BLOCKS], F32)
        less = sb("less", [P, P], F16)
        ones = sb("ones", [P, P], F16)
        logits = sb("logits", [P, R], F32)
        pr = sb("pr", [P, R], F32)
        one = [sb(f"onehot{i}", [P, R], F32) for i in range(TOP)]
        pick = sb("pick", [P, R], F32)
        top = [sb(f"top{i}", [P, TILES], F32) for i in range(TOP)]
        first = sb("first", [P, TILES], F32)
        tsum = sb("tsum", [P, TILES], F32)
        chosen = sb("chosen", [P, R], F16)
        E1 = EXPERTS + 1
        counts = [sb(f"counts{i}", [P, (TILES + 1) * EXPERTS], F32) for i in range(2)]
        bases = [sb(f"bases{i}", [P, E1], F32) for i in range(2)]
        base_slots = sb("base_slots", [P, EXPERTS], F32)
        place = sb("place", [P, TOP * TILES], F32)
        place_block = sb("place_block", [P, TOP * TILES], F32)
        place_slot = sb("place_slot", [P, TOP * TILES], F32)
        slot_hot = sb("slot_hot", [P, TILES, P], F16)
        block_hot = sb("block_hot", [P, TILES, 2, BLOCKS], F16)
        table = [sb(f"table{i}", [P, BLOCKS], F32) for i in range(3)]

        banks = [ctx.enter_context(nc.psum_tensor(f"{name}_bank{i}", [P, 512], F32)) for i in range(7)]
        logit_ps, count_ps, table_ps = banks[4], banks[5], banks[6]

        const_in = sem("const_in")
        x_landed = [sem(f"x_landed{i}") for i in range(2)]
        w_landed = [sem(f"w_landed{i}") for i in range(2)]
        w_his, w_los = sem("w_his"), sem("w_los")
        consts_ready, carried = sem("consts_ready"), sem("carried")
        ln_stats, ln_aggr, ln_eps, ln_rstd, xn_ready = (sem(s) for s in ("ln_stats", "ln_aggr", "ln_eps", "ln_rstd", "xn_ready"))
        xn_stored = sem("xn_stored")
        xt_full, xt_his, xt_los = sem("xt_full"), sem("xt_his"), sem("xt_los")
        logit_full, logit_done = sem("logit_full"), sem("logit_done")
        route, exp_done = sem("route"), sem("exp_done")
        chosen_ready, count_full, hot_ready, table_full = (sem(s) for s in ("chosen_ready", "count_full", "hot_ready", "table_full"))

        CONSTS = 8

        def groups(eng, body):
            body(0, 0, 0)
            with eng.Fori(0, (GROUPS - 1) // 2) as i:
                body(2 * i + 1, 1, i)
                body(2 * i + 2, 0, i + 1)

        def alone(eng, semaphore, value):
            moe_alone(eng, semaphore, value, carried)

        def xt_pieces():
            return [(2 * t + k, t, k * T_BANK, (T_BANK, CHUNK - T_BANK)[k]) for t in range(2) for k in range(2)]

        def in_pairs(eng, first_piece, pieces, body):
            with eng.Fori(0, pieces // 2) as j:
                body(2 * j + first_piece, 0, j + first_piece // 2)
                body(2 * j + first_piece + 1, 1, j + first_piece // 2)

        GROUPED = GROUPS * PIECES_PER_GROUP

        def grouped_pieces(body, g):
            for j in range(0, PIECES_PER_GROUP, 2):
                half = g * (PIECES_PER_GROUP // 2) + j // 2
                body(g * PIECES_PER_GROUP + j, 0, half)
                body(g * PIECES_PER_GROUP + j + 1, 1, half)

        with nc.Block() as block:

            @block.sync
            def _(sp):
                x_tiles = x_in.rearrange("(t p) d -> p t d", p=P)
                xn_tiles = xn_rows.rearrange("(t p) d -> p t d", p=P)

                def load_x(g, buf, half):
                    sp.dma_start(x_sb[:, buf, :, :], x_tiles[:, bass.ds(GROUP * g, GROUP), :]).then_inc(x_landed[buf], 16)

                load_x(0, 0, 0)
                for dst, src in ((ident[:, :], identity), (rt_in[:, :], router), (rtb[:, :], router_bias.to_broadcast([P, EXPERTS])),
                                 (desc[:, :], descending.to_broadcast([P, EXPERTS]))):
                    sp.dma_start(dst, src).then_inc(const_in, 16)
                load_x(1, 1, 0)
                for dst, src in ((number[:, :], numbers), (tile_no[:, :], tile_numbers), (less[:, :], before[:, 0:P]),
                                 (ones[:, :], before[:, P:2 * P])):
                    sp.dma_start(dst, src).then_inc(const_in, 16)

                def load_piece(n, buf, half, reuse=True):
                    if reuse:
                        alone(sp, w_los, n - 1)
                    sp.dma_start(w_stage[:, buf, :], weights[:, bass.ds(n * PIECE, PIECE)]).then_inc(w_landed[buf], 16)

                for g in range(GROUPS):
                    for j in range(PIECES_PER_GROUP):
                        n = g * PIECES_PER_GROUP + j
                        load_piece(n, n % 2, n // 2, n >= 2)
                    sp.wait_ge(xn_ready, GROUP * (g + 1))
                    sp.dma_start(xn_tiles[:, GROUP * g:GROUP * (g + 1), :], xn[:, :, :]).then_inc(xn_stored, 16)
                    if g + 2 < GROUPS:
                        load_x(g + 2, g % 2, 0)
                in_pairs(sp, GROUPED, PIECES - GROUPED, load_piece)
                sp.wait_ge(xn_stored, 16 * GROUPS)

            @block.gpsimd
            def _(pool):
                nc.gpsimd.memset(expo[:, :], -0.5).then_inc(consts_ready, 1)
                pool.wait_ge(consts_ready, 1)

                def rstds(g, buf, half):
                    pool.wait_ge(ln_eps, g + 1)
                    nc.gpsimd.tensor_tensor(rstd[:, :], veps[:, :], expo[:, :], ALU.pow).then_inc(ln_rstd, 1)

                groups(pool, rstds)
                for semaphore in finished:
                    pool.sem_clear(semaphore)

            @block.scalar
            def _(act):
                def piece_hi(n, buf, half):
                    alone(act, w_landed[buf], 16 * half + 16)
                    nc.scalar.activation(w_hi[:, bass.ds(n * PIECE, PIECE)], w_stage[:, buf, :], ACT.Copy, scale=W_SCALE).then_inc(w_his, 1)

                act.wait_ge(const_in, 16 * CONSTS)
                nc.scalar.activation(rt_hi[:, :], rt_in[:, :], ACT.Copy, scale=W_SCALE).then_inc(consts_ready, 1)

                def group(g, buf, half):
                    for n, (bk, t, at, cols) in enumerate(xt_pieces()):
                        act.wait_ge(xt_full, 4 * g + n + 1)
                        if not isinstance(g, int):
                            act.wait_ge(logit_full, g)
                            act.sem_inc(carried, 1)
                        nc.scalar.activation(xt_hi[:, t, at:at + cols], banks[bk][:, 0:cols], ACT.Copy,
                                             scale=X_SCALE).then_inc(xt_his, 1)
                    grouped_pieces(piece_hi, g)

                groups(act, group)
                act.wait_ge(route, 3)
                nc.scalar.activation(pr[:, :], logits[:, :], ACT.Exp).then_inc(exp_done, 1)
                in_pairs(act, GROUPED, PIECES - GROUPED, piece_hi)

            @block.vector
            def _(dve):
                def piece_lo(n, buf, half):
                    dve.wait_ge(w_his, n + 1)
                    where = bass.ds(n * PIECE, PIECE)
                    nc.vector.scalar_tensor_tensor(w_lo[:, where], w_stage[:, buf, :], W_SCALE, w_hi[:, where],
                                                   ALU.mult, ALU.subtract).then_inc(w_los, 1)

                def group(g, buf, half):
                    dve.wait_ge(x_landed[buf], 16 * half + 16)
                    for k in range(GROUP):
                        nc.vector.bn_stats(stats[:, k, :], x_sb[:, buf, k, :]).then_inc(ln_stats, 1)
                    alone(dve, ln_stats, GROUP * g + GROUP)
                    for k in range(GROUP):
                        nc.vector.bn_aggr(mv[:, k, :], stats[:, k, :]).then_inc(ln_aggr, 1)
                    dve.wait_ge(ln_aggr, GROUP * g + GROUP)
                    nc.vector.tensor_scalar(veps[:, :], mv[:, :, 1], LN_EPS, None, ALU.add).then_inc(ln_eps, 1)
                    if not isinstance(g, int):
                        dve.wait_ge(xt_full, 4 * g)
                        dve.sem_inc(carried, 1)
                        dve.wait_ge(xn_stored, 16 * g)
                        dve.sem_inc(carried, 1)
                    dve.wait_ge(ln_rstd, g + 1)
                    for k in range(GROUP):
                        nc.vector.tensor_scalar(xn[:, k, :], x_sb[:, buf, k, :], mv[:, k, 0:1], rstd[:, k:k + 1], ALU.subtract,
                                                ALU.mult).then_inc(xn_ready, 1)
                    for n, (bk, t, at, cols) in enumerate(xt_pieces()):
                        dve.wait_ge(xt_his, 4 * g + n + 1)
                        nc.vector.scalar_tensor_tensor(xt_lo[:, t, at:at + cols], banks[bk][:, 0:cols], X_SCALE,
                                                       xt_hi[:, t, at:at + cols], ALU.mult, ALU.subtract).then_inc(xt_los, 1)
                    grouped_pieces(piece_lo, g)
                    dve.wait_ge(logit_full, g + 1)
                    nc.vector.tensor_scalar(logits[:, bass.ds(g * GROUP * EXPERTS, GROUP * EXPERTS)], logit_ps[:, 0:GROUP * EXPERTS],
                                            1.0 / GU_SCALE, None, ALU.mult).then_inc(logit_done, 1)

                dve.wait_ge(consts_ready, 2)
                nc.vector.scalar_tensor_tensor(rt_lo[:, :], rt_in[:, :], W_SCALE, rt_hi[:, :], ALU.mult, ALU.subtract).then_inc(consts_ready, 1)
                groups(dve, group)

                steps = [0]

                def step(instruction):
                    steps[0] += 1
                    instruction.then_inc(route, 1)
                    dve.wait_ge(route, steps[0])

                def by_tile(t):
                    return t[:, :].rearrange("p (t e) -> p t e", e=EXPERTS)

                def wide(t):
                    return t[:, :].unsqueeze(2).to_broadcast([P, TILES, EXPERTS])

                def each(t, n=TILES):
                    return t.unsqueeze(1).to_broadcast([P, n, t.shape[1]])

                dve.wait_ge(logit_done, GROUPS)
                step(nc.vector.tensor_tensor(by_tile(logits), by_tile(logits), each(rtb[:, :]), ALU.add))
                step(nc.vector.reduce_max(top[0][:, :], by_tile(logits), AX.X))
                step(nc.vector.tensor_tensor(by_tile(logits), by_tile(logits), wide(top[0]), ALU.subtract))
                dve.wait_ge(exp_done, 1)
                step(nc.vector.reduce_sum(tsum[:, :], by_tile(pr), AX.X))
                step(nc.vector.reciprocal(first[:, :], tsum[:, :]))
                step(nc.vector.tensor_tensor(by_tile(pr), by_tile(pr), wide(first), ALU.mult))
                step(nc.vector.tensor_copy(comb[:, :], pr[:, :]))
                for i in range(TOP):
                    step(nc.vector.reduce_max(top[i][:, :], by_tile(comb), AX.X))
                    step(nc.vector.tensor_tensor(by_tile(pick), by_tile(comb), wide(top[i]), ALU.is_equal))
                    step(nc.vector.tensor_tensor(by_tile(pick), by_tile(pick), each(desc[:, :]), ALU.mult))
                    step(nc.vector.reduce_max(first[:, :], by_tile(pick), AX.X))
                    step(nc.vector.tensor_tensor(by_tile(one[i]), by_tile(pick), wide(first), ALU.is_equal))
                    if i == 0:
                        step(nc.vector.scalar_tensor_tensor(comb[:, :], one[0][:, :], -2.0, comb[:, :], ALU.mult, ALU.add))
                step(nc.vector.tensor_tensor(pick[:, :], one[0][:, :], one[1][:, :], ALU.add))
                nc.vector.tensor_copy(chosen[:, :], pick[:, :]).then_inc(chosen_ready, 1)
                step(nc.vector.tensor_tensor(tsum[:, :], top[0][:, :], top[1][:, :], ALU.add))
                step(nc.vector.tensor_scalar(tsum[:, :], tsum[:, :], 1e-20, None, ALU.add))
                step(nc.vector.reciprocal(first[:, :], tsum[:, :]))
                step(nc.vector.tensor_tensor(pick[:, :], pick[:, :], pr[:, :], ALU.mult))
                for i in range(TOP):
                    nc.vector.tensor_tensor(top_w[:, i, :], top[i][:, :], first[:, :], ALU.mult)
                step(nc.vector.tensor_tensor(by_tile(comb), by_tile(pick), wide(first), ALU.mult))

                def running_sums(buffers, entries, width):
                    src, dst, shift = 0, 1, 1
                    while shift < entries:
                        s, d, cut = buffers[src], buffers[dst], shift * width
                        nc.vector.tensor_copy(d[:, 0:cut], s[:, 0:cut])
                        step(nc.vector.tensor_tensor(d[:, cut:entries * width], s[:, cut:entries * width],
                                                     s[:, 0:entries * width - cut], ALU.add))
                        src, dst, shift = dst, src, 2 * shift
                    return buffers[src]

                dve.wait_ge(count_full, 1)
                nc.vector.memset(counts[0][:, 0:EXPERTS], 0.0)
                step(nc.vector.tensor_copy(counts[0][:, EXPERTS:], count_ps[:, R:2 * R]))
                so_far = running_sums(counts, TILES + 1, EXPERTS)
                nc.vector.memset(bases[0][:, 0:1], 0.0)
                step(nc.vector.tensor_scalar(base_slots[:, :], so_far[:, R:], 1.0 / P, (P - 1.0) / P - FLOOR_SHIFT, ALU.mult, ALU.add))
                step(nc.vector.tensor_scalar(base_slots[:, :], base_slots[:, :], FLOOR, None, ALU.add))
                step(nc.vector.tensor_scalar(bases[0][:, 1:], base_slots[:, :], FLOOR, None, ALU.subtract))
                base = running_sums(bases, E1, 1)
                step(nc.vector.tensor_scalar(base_slots[:, :], base[:, 0:EXPERTS], float(P), None, ALU.mult))
                so_far_tiles = so_far[:, 0:R].rearrange("p (t e) -> p t e", e=EXPERTS)
                step(nc.vector.tensor_tensor(by_tile(pick), so_far_tiles, each(base_slots[:, :]), ALU.add))
                step(nc.vector.tensor_tensor(pick[:, :], pick[:, :], count_ps[:, 0:R], ALU.add))
                for i in range(TOP):
                    step(nc.vector.tensor_tensor(one[i][:, :], one[i][:, :], pick[:, :], ALU.mult))
                    step(nc.vector.reduce_sum(place[:, TILES * i:TILES * (i + 1)], by_tile(one[i]), AX.X))
                step(nc.vector.tensor_scalar(place_block[:, :], place[:, :], 1.0 / P, -FLOOR_SHIFT, ALU.mult, ALU.add))
                step(nc.vector.tensor_scalar(place_block[:, :], place_block[:, :], FLOOR, None, ALU.add))
                step(nc.vector.tensor_scalar(place_block[:, :], place_block[:, :], FLOOR, None, ALU.subtract))
                step(nc.vector.scalar_tensor_tensor(place_slot[:, :], place_block[:, :], -float(P), place[:, :], ALU.mult, ALU.add))
                for i in range(TOP):
                    ts = slice(TILES * i, TILES * (i + 1))
                    if i >= 1:
                        dve.wait_ge(table_full, 1)
                    nc.vector.tensor_tensor(slot_hot[:, :, :], place_slot[:, ts].unsqueeze(2).to_broadcast([P, TILES, P]),
                                            each(number[:, 0:P]), ALU.is_equal)
                    step(nc.vector.tensor_tensor(block_hot[:, :, 0, :], place_block[:, ts].unsqueeze(2).to_broadcast([P, TILES, BLOCKS]),
                                                 each(number[:, 0:BLOCKS]), ALU.is_equal))
                    step(nc.vector.tensor_scalar(block_hot[:, :, 1, :], block_hot[:, :, 0, :], number[:, P:P + 1], None, ALU.mult))
                    nc.vector.tensor_tensor(block_hot[:, :, 0, :], block_hot[:, :, 0, :],
                                            tile_no[:, ts].unsqueeze(2).to_broadcast([P, TILES, BLOCKS]), ALU.mult).then_inc(hot_ready, 1)
                more = EXPERTS - 1
                reached = x_sb[:, 0, 0:2, :].rearrange("p a d -> p (a d)")[:, 0:BLOCKS * more].rearrange("p (b e) -> p b e", e=more)
                step(nc.vector.tensor_tensor(reached, number[:, 0:BLOCKS].unsqueeze(2).to_broadcast([P, BLOCKS, more]),
                                             each(base[:, 1:EXPERTS], BLOCKS), ALU.is_ge))
                step(nc.vector.reduce_sum(table[0][:, :], reached, AX.X))
                for at, cols in ((weights_at, EXPERT_COLS), (biases_at, F_TILES)):
                    nc.vector.memset(at[:, 0:1], 0)
                    step(nc.vector.tensor_scalar(table[1][:, :], table[0][:, :], float(cols), None, ALU.mult))
                    step(nc.vector.tensor_copy(at[:, 1:], table[1][:, :]))
                dve.wait_ge(table_full, 2)
                got_tile, got_part = table_ps[:, 0:BLOCKS], table_ps[:, BLOCKS:2 * BLOCKS]
                empty, row, extra = (t[:, :] for t in table)
                step(nc.vector.tensor_scalar(empty, got_tile, 0.0, None, ALU.is_equal))
                step(nc.vector.tensor_scalar(row, got_tile, float(P), float(P), ALU.mult, ALU.subtract))
                step(nc.vector.tensor_tensor(row, row, got_part, ALU.add))
                step(nc.vector.scalar_tensor_tensor(row, empty, float(P), row, ALU.mult, ALU.add))
                step(nc.vector.tensor_scalar(extra, tile_no[:, TOP * TILES:], float(DUMP), None, ALU.add))
                step(nc.vector.tensor_tensor(extra, extra, empty, ALU.mult))
                step(nc.vector.tensor_tensor(extra, extra, row, ALU.add))
                step(nc.vector.tensor_copy(target[:, :], extra))
                step(nc.vector.tensor_scalar(empty, row, float(TOKENS), float(-TOKENS), ALU.is_ge, ALU.mult))
                step(nc.vector.tensor_tensor(row, row, empty, ALU.add))
                step(nc.vector.tensor_copy(source[:, :], row))
                in_pairs(dve, GROUPED, PIECES - GROUPED, piece_lo)

            @block.tensor
            def _(pe):
                def group(g, buf, half):
                    for k, (bk, t, at, cols) in enumerate(xt_pieces()):
                        if not isinstance(g, int):
                            pe.wait_ge(xt_los, 4 * g - 3 + k)
                        pe.wait_ge(xn_ready, GROUP * g + (at + cols) // P)
                        for j in range(cols // P):
                            last = nc.tensor.transpose(banks[bk][:, P * j:P * (j + 1)], xn[:, at // P + j, P * t:P * (t + 1)], ident[:, :])
                        last.then_inc(xt_full, 1)
                    pe.wait_ge(xt_los, 4 * g + 4)
                    if not isinstance(g, int):
                        pe.wait_ge(logit_done, g)
                    for j in range(GROUP):
                        out = logit_ps[:, EXPERTS * j:EXPERTS * (j + 1)]
                        tok = slice(j * P, (j + 1) * P)
                        for t in range(2):
                            w = slice(EXPERTS * t, EXPERTS * (t + 1))
                            nc.tensor.matmul(out, xt_hi[:, t, tok], rt_hi[:, w], start=(t == 0), stop=False)
                            nc.tensor.matmul(out, xt_hi[:, t, tok], rt_lo[:, w], start=False, stop=False)
                            last = nc.tensor.matmul(out, xt_lo[:, t, tok], rt_hi[:, w], start=False, stop=(t == 1))
                    last.then_inc(logit_full, 1)

                pe.wait_ge(consts_ready, 3)
                groups(pe, group)
                pe.wait_ge(chosen_ready, 1)
                nc.tensor.matmul(count_ps[:, 0:R], less[:, :], chosen[:, :], start=True, stop=True)
                nc.tensor.matmul(count_ps[:, R:2 * R], ones[:, :], chosen[:, :], start=True, stop=True).then_inc(count_full, 1)
                for i in range(TOP):
                    pe.wait_ge(hot_ready, i + 1)
                    for t in range(TILES):
                        last = nc.tensor.matmul(table_ps[:, 0:2 * BLOCKS], slot_hot[:, t, :],
                                                block_hot[:, t, :, :].rearrange("p a b -> p (a b)"),
                                                start=(i == 0 and t == 0), stop=(i == TOP - 1 and t == TILES - 1))
                    last.then_inc(table_full, 1)


def moe_experts(nc, xn_rows, y_rows, gate_bias, up_bias, identity, w_hi, w_lo, source, target, weights_at, biases_at):
    name = "experts"
    with ExitStack() as ctx:
        def sb(label, shape, dt):
            return ctx.enter_context(nc.sbuf_tensor(f"{name}_{label}", shape, dt))

        def sem(label):
            return ctx.enter_context(nc.semaphore(f"{name}_{label}"))

        ident = sb("ident", [P, P], F32)
        gb = sb("gb", [P, EXPERTS * F_TILES], F32)
        gbs = sb("gbs", [P, EXPERTS * F_TILES], F32)
        ub = sb("ub", [P, EXPERTS * F_TILES], F32)
        take, put = sb("take", [P, 2], U32), sb("put", [P, 2], U32)
        xg = sb("xg", [P, 2, DIM], F32)
        xt_hi, xt_lo = sb("xt_hi", [P, 2, DIM], F16), sb("xt_lo", [P, 2, DIM], F16)
        up_sb = sb("up", [P, 2, 4 * P], F32)
        z_sb = sb("z", [P, 2, 4 * P], F32)
        h_sb = sb("h", [P, 2, 4 * P], F32)
        h_hi = sb("h_hi", [P, 2, 8 * P], F16)
        h_lo = sb("h_lo", [P, 2, 8 * P], F16)
        y_sb = sb("y", [P, 2, DIM], F32)

        banks = [ctx.enter_context(nc.psum_tensor(f"{name}_bank{i}", [P, 512], F32)) for i in range(7)]
        gate_ps, up_ps, y_ps, t_ps = banks[0:2], banks[2:4], banks[4:6], banks[6]

        const_in, consts_ready, carried = sem("const_in"), sem("consts_ready"), sem("carried")
        taken, gathered = sem("taken"), [sem(f"gathered{i}") for i in range(2)]
        put_ready, scattered = sem("put_ready"), [sem(f"scattered{i}") for i in range(2)]
        xt_full, xt_his, xt_los = sem("xt_full"), sem("xt_his"), sem("xt_los")
        gu_full, up_done, z_done, h_done, hhi_done, hlo_done = (sem(s) for s in ("gu_full", "up_done", "z_done", "h_done", "hhi_done", "hlo_done"))
        y_full, y_done = sem("y_full"), sem("y_done")

        def alone(eng, semaphore, value):
            moe_alone(eng, semaphore, value, carried)

        def starts(b):
            return isinstance(b, int) and b < 2

        def each_block(eng, table, limit, body):
            def entries(b, n):
                return nc.values_load_multi_w_load_instructions(table[0:1, bass.ds(b, n)], engines=[eng.engine],
                                                                min_val=0, max_val=limit)[1]

            def pair(b, half):
                last, this, following = entries(b, 3)
                body(b, 0, half, this, last)
                body(b + 1, 1, half, following, this)

            pair(0, 0)
            pair(2, 1)
            with eng.Fori(2, (BLOCKS - 1) // 2) as i:
                pair(2 * i, i)
            last, this = entries(BLOCKS - 1, 2)
            body(BLOCKS - 1, 0, (BLOCKS - 1) // 2, this, last)
            return this

        with nc.Block() as block:

            @block.sync
            def _(sp):
                for dst, src in ((gb, gate_bias), (ub, up_bias), (ident, identity)):
                    sp.dma_start(dst[:, :], src).then_inc(const_in, 16)

            @block.gpsimd
            def _(pool):
                def gather(b, par, half):
                    if not starts(b):
                        alone(pool, xt_full, b - 1)
                    nc.gpsimd.tensor_copy(take[:, par:par + 1], source[:, bass.ds(b, 1)]).then_inc(taken, 1)
                    alone(pool, taken, b + 1)
                    pool.indirect_dma_start(xg[:, par, :], None, xn_rows, bass.IndirectOffsetOnAxis(take[:, par:par + 1], 0)).then_inc(gathered[par], 16)

                def scatter(b, par, half):
                    if not starts(b):
                        alone(pool, scattered[par], 16 * half)
                    nc.gpsimd.tensor_copy(put[:, par:par + 1], target[:, bass.ds(b, 1)]).then_inc(put_ready, 1)
                    alone(pool, put_ready, b + 1)
                    alone(pool, y_done, b + 1)
                    pool.indirect_dma_start(y_rows, bass.IndirectOffsetOnAxis(put[:, par:par + 1], 0), y_sb[:, par, :], None).then_inc(scattered[par], 16)

                gather(0, 0, 0)
                gather(1, 1, 0)
                gather(2, 0, 1)
                scatter(0, 0, 0)
                gather(3, 1, 1)
                scatter(1, 1, 0)
                with pool.Fori(2, (BLOCKS - 1) // 2) as i:
                    gather(2 * i, 0, i)
                    scatter(2 * i - 2, 0, i - 1)
                    gather(2 * i + 1, 1, i)
                    scatter(2 * i - 1, 1, i - 1)
                gather(BLOCKS - 1, 0, (BLOCKS - 1) // 2)
                for b in range(BLOCKS - 3, BLOCKS):
                    scatter(b, b % 2, b // 2)
                for par in range(2):
                    pool.wait_ge(scattered[par], 16 * ((BLOCKS + 1 - par) // 2))

            @block.scalar
            def _(act):
                act.wait_ge(const_in, 16 * 3)
                nc.scalar.activation(gbs[:, :], gb[:, :], ACT.Copy, scale=GU_SCALE).then_inc(consts_ready, 1)

                def turned(b, par):
                    act.wait_ge(xt_full, b + 1)
                    nc.scalar.activation(xt_hi[:, par, :], t_ps[:, 0:DIM], ACT.Copy, scale=X_SCALE).then_inc(xt_his, 1)

                def up(b, half, e):
                    alone(act, gu_full, 2 * b + half + 1)
                    for j, f in enumerate(HALF_TILES[half]):
                        rows, cols = (P if f < F_TILES - 1 else F_LAST), slice(P * j, P * (j + 1))
                        last = nc.scalar.activation(up_sb[0:rows, half, cols], up_ps[half][0:rows, cols], ACT.Identity,
                                                    scale=1.0 / GU_SCALE, bias=ub[0:rows, bass.ds(e + f, 1)])
                    last.then_inc(up_done, 1)

                def silu(b, half):
                    act.wait_ge(z_done, 2 * b + half + 1)
                    if not (isinstance(b, int) and b == 0):
                        act.sem_inc(carried, 1)
                        alone(act, hlo_done, 2 * b + half - 1)
                    for rows, lo, hi in HALF_PARTS[half]:
                        last = nc.scalar.activation(h_sb[0:rows, half, lo:hi], z_sb[0:rows, half, lo:hi], ACT.Silu, scale=1.0 / GU_SCALE)
                    last.then_inc(h_done, 1)

                def out(b, par, half):
                    if not starts(b):
                        act.wait_ge(scattered[par], 16 * half)
                        act.sem_inc(carried, 1)
                    act.wait_ge(y_full, b + 1)
                    nc.scalar.activation(y_sb[:, par, :], y_ps[par][:, 0:DIM], ACT.Copy, scale=1.0 / Y_SCALE).then_inc(y_done, 1)

                turned(0, 0)

                def body(b, par, half, e, e_before):
                    up(b, 0, e)
                    if not (isinstance(b, int) and b == BLOCKS - 1):
                        turned(b + 1, 1 - par)
                    silu(b, 0)
                    if not (isinstance(b, int) and b == 0):
                        out(b - 1, 1 - par, half if par == 1 else half - 1)
                    up(b, 1, e)
                    silu(b, 1)

                each_block(act, biases_at, (EXPERTS - 1) * F_TILES, body)
                out(BLOCKS - 1, 0, (BLOCKS - 1) // 2)

            @block.vector
            def _(dve):
                def turned(b, par):
                    dve.wait_ge(xt_his, b + 1)
                    nc.vector.scalar_tensor_tensor(xt_lo[:, par, :], t_ps[:, 0:DIM], X_SCALE, xt_hi[:, par, :], ALU.mult,
                                                   ALU.subtract).then_inc(xt_los, 1)

                def product(b, half, e):
                    dve.wait_ge(up_done, 2 * b + half + 1)
                    for j, f in enumerate(HALF_TILES[half]):
                        rows, cols = (P if f < F_TILES - 1 else F_LAST), slice(P * j, P * (j + 1))
                        last = nc.vector.scalar_tensor_tensor(z_sb[0:rows, half, cols], gate_ps[half][0:rows, cols],
                                                              gbs[0:rows, bass.ds(e + f, 1)], up_sb[0:rows, half, cols],
                                                              ALU.add, ALU.mult)
                    last.then_inc(z_done, 1)

                def cut(b, par, half):
                    if not starts(b):
                        alone(dve, y_full, b - 1)
                    dve.wait_ge(h_done, 2 * b + half + 1)
                    for rows, lo, hi in HALF_PARTS[half]:
                        to = slice(4 * P * half + lo, 4 * P * half + hi)
                        last = nc.vector.tensor_scalar(h_hi[0:rows, par, to], h_sb[0:rows, half, lo:hi], H_SCALE, None, ALU.mult)
                    last.then_inc(hhi_done, 1)
                    dve.wait_ge(hhi_done, 2 * b + half + 1)
                    for rows, lo, hi in HALF_PARTS[half]:
                        to = slice(4 * P * half + lo, 4 * P * half + hi)
                        last = nc.vector.scalar_tensor_tensor(h_lo[0:rows, par, to], h_sb[0:rows, half, lo:hi], H_SCALE,
                                                              h_hi[0:rows, par, to], ALU.mult, ALU.subtract)
                    last.then_inc(hlo_done, 1)

                turned(0, 0)
                dve.wait_ge(consts_ready, 1)

                def body(b, par, half, e, e_before):
                    product(b, 0, e)
                    if not (isinstance(b, int) and b == BLOCKS - 1):
                        turned(b + 1, 1 - par)
                    cut(b, par, 0)
                    product(b, 1, e)
                    cut(b, par, 1)

                each_block(dve, biases_at, (EXPERTS - 1) * F_TILES, body)

            @block.tensor
            def _(pe):
                def turn(b, par, half):
                    pe.wait_ge(gathered[par], 16 * half + 16)
                    if not (isinstance(b, int) and b == 0):
                        pe.wait_ge(xt_los, b)
                    for t in range(2):
                        last = nc.tensor.transpose(t_ps[:, P * t:P * (t + 1)], xg[:, par, P * t:P * (t + 1)], ident[:, :])
                    last.then_inc(xt_full, 1)

                def hidden(b, par, half, e):
                    if not (isinstance(b, int) and b == 0):
                        pe.wait_ge(z_done, 2 * b + half - 1)
                    if half == 0:
                        pe.wait_ge(xt_los, b + 1)
                    for ps, w0 in ((up_ps[half], UP_AT), (gate_ps[half], 0)):
                        for j, f in enumerate(HALF_TILES[half]):
                            rows = P if f < F_TILES - 1 else F_LAST
                            out = ps[0:rows, P * j:P * (j + 1)]
                            for t in range(2):
                                w = bass.ds(e + (w0 + FF * t + P * f), rows)
                                xs = slice(P * t, P * (t + 1))
                                nc.tensor.matmul(out, w_hi[:, w], xt_hi[:, par, xs], start=(t == 0), stop=False)
                                nc.tensor.matmul(out, w_hi[:, w], xt_lo[:, par, xs], start=False, stop=False)
                                last = nc.tensor.matmul(out, w_lo[:, w], xt_hi[:, par, xs], start=False, stop=(t == 1))
                    last.then_inc(gu_full, 1)

                def down(b, par, e):
                    pe.wait_ge(hlo_done, 2 * b + 2)
                    if not starts(b):
                        pe.wait_ge(y_done, b - 1)
                    out = y_ps[par][:, 0:DIM]
                    for f in range(F_TILES):
                        rows = P if f < F_TILES - 1 else F_LAST
                        w = bass.ds(e + (DOWN_AT + DIM * f), DIM)
                        hs = slice(P * f, P * (f + 1))
                        nc.tensor.matmul(out, h_hi[0:rows, par, hs], w_hi[0:rows, w], start=(f == 0), stop=False)
                        nc.tensor.matmul(out, h_hi[0:rows, par, hs], w_lo[0:rows, w], start=False, stop=False)
                        last = nc.tensor.matmul(out, h_lo[0:rows, par, hs], w_hi[0:rows, w], start=False, stop=(f == F_TILES - 1))
                    last.then_inc(y_full, 1)

                pe.wait_ge(const_in, 16 * 3)
                turn(0, 0, 0)

                def body(b, par, half, e, e_before):
                    hidden(b, par, 0, e)
                    if not (isinstance(b, int) and b == 0):
                        down(b - 1, 1 - par, e_before)
                    if not (isinstance(b, int) and b == BLOCKS - 1):
                        turn(b + 1, 1 - par, half if par == 0 else half + 1)
                    hidden(b, par, 1, e)

                last = each_block(pe, weights_at, (EXPERTS - 1) * EXPERT_COLS, body)
                down(BLOCKS - 1, 0, last)


def moe_sum(nc, x_in, y_rows, x_out, down_bias, identity, comb, top_w):
    name = "sum"
    with ExitStack() as ctx:
        def sb(label, shape, dt):
            return ctx.enter_context(nc.sbuf_tensor(f"{name}_{label}", shape, dt))

        def sem(label):
            return ctx.enter_context(nc.semaphore(f"{name}_{label}"))

        acc = sb("acc", [P, TILES, DIM], F32)
        y = [sb(f"y{i}", [P, TILES, DIM], F32) for i in range(TOP)]
        ident = sb("ident", [P, P], F32)
        db = sb("db", [EXPERTS, DIM], F32)
        comb_t = sb("comb_t", [EXPERTS, 2, P], F32)
        turn_ps = [ctx.enter_context(nc.psum_tensor(f"{name}_turn{i}", [P, 512], F32)) for i in range(2)]
        bias_ps = [ctx.enter_context(nc.psum_tensor(f"{name}_bias{i}", [P, 512], F32)) for i in range(2)]
        const_in, stored = sem("const_in"), sem("stored")
        landed = [sem(f"landed{i}") for i in range(GROUPS)]
        ct_full, ct_done, bias_full, bias_done = (sem(s) for s in ("ct_full", "ct_done", "bias_full", "bias_done"))
        first_done, sum_done = sem("first_done"), sem("sum_done")

        with nc.Block() as block:

            @block.sync
            def _(sp):
                def tiles(rows):
                    return rows.rearrange("(t p) d -> p t d", p=P)

                sp.dma_start(ident[:, :], identity).then_inc(const_in, 16)
                sp.dma_start(db[:, :], down_bias).then_inc(const_in, 16)
                for g in range(GROUPS):
                    ts = slice(GROUP * g, GROUP * (g + 1))
                    sp.dma_start(acc[:, ts, :], tiles(x_in)[:, ts, :]).then_inc(landed[g], 16)
                    for i in range(TOP):
                        sp.dma_start(y[i][:, ts, :], tiles(y_rows[TOKENS * i:TOKENS * (i + 1), :])[:, ts, :]).then_inc(landed[g], 16)
                for g in range(GROUPS):
                    ts = slice(GROUP * g, GROUP * (g + 1))
                    sp.wait_ge(sum_done, GROUP * (g + 1))
                    sp.dma_start(tiles(x_out)[:, ts, :], acc[:, ts, :]).then_inc(stored, 16)
                sp.wait_ge(stored, 16 * GROUPS)

            @block.scalar
            def _(act):
                for k in range(TILES):
                    act.wait_ge(ct_full, k + 1)
                    if k >= 2:
                        act.wait_ge(bias_full, k - 1)
                    nc.scalar.activation(comb_t[:, k % 2, :], turn_ps[k % 2][0:EXPERTS, 0:P], ACT.Copy).then_inc(ct_done, 1)

            @block.vector
            def _(dve):
                for k in range(TILES):
                    if k % GROUP == 0:
                        dve.wait_ge(landed[k // GROUP], 16 * (TOP + 1))
                    dve.wait_ge(bias_full, k + 1)
                    nc.vector.tensor_tensor(acc[:, k, :], acc[:, k, :], bias_ps[k % 2][:, 0:DIM], ALU.add).then_inc(bias_done, 1)
                    dve.wait_ge(bias_done, k + 1)
                    nc.vector.scalar_tensor_tensor(acc[:, k, :], y[0][:, k, :], top_w[:, 0, k:k + 1], acc[:, k, :], ALU.mult,
                                                   ALU.add).then_inc(first_done, 1)
                    dve.wait_ge(first_done, k + 1)
                    nc.vector.scalar_tensor_tensor(acc[:, k, :], y[1][:, k, :], top_w[:, 1, k:k + 1], acc[:, k, :], ALU.mult,
                                                   ALU.add).then_inc(sum_done, 1)

            @block.tensor
            def _(pe):
                pe.wait_ge(const_in, 32)

                def turn(k):
                    if k >= 2:
                        pe.wait_ge(ct_done, k - 1)
                    nc.tensor.transpose(turn_ps[k % 2][0:EXPERTS, 0:P], comb[:, EXPERTS * k:EXPERTS * (k + 1)], ident[:, :]).then_inc(ct_full, 1)

                turn(0)
                for k in range(TILES):
                    if k + 1 < TILES:
                        turn(k + 1)
                    pe.wait_ge(ct_done, k + 1)
                    if k >= 2:
                        pe.wait_ge(bias_done, k - 1)
                    nc.tensor.matmul(bias_ps[k % 2][:, 0:DIM], comb_t[:, k % 2, :], db[:, :], start=True, stop=True).then_inc(bias_full, 1)


def layout_moe(a, out):
    gate, up, down = (a[f"L0_ffn_{n}_w"] for n in ("gp", "up", "down"))
    pad = F_TILES * P - FF
    cols = []
    for e in range(EXPERTS):
        for w in (gate, up):
            cols.append(w[e].T.reshape(2, P, FF).transpose(1, 0, 2).reshape(P, 2 * FF))
        cols.append(np.pad(down[e].T, ((0, pad), (0, 0))).reshape(F_TILES, P, DIM).transpose(1, 0, 2).reshape(P, F_TILES * DIM))
    out["moe_w"] = np.concatenate(cols, axis=1)
    for key, n in (("moe_gate_b", "gp"), ("moe_up_b", "up")):
        out[key] = np.pad(a[f"L0_ffn_{n}_b"], ((0, 0), (0, pad))).reshape(EXPERTS * F_TILES, P).T
    out["moe_down_b"] = a["L0_ffn_down_b"]
    out["moe_router"] = a["L0_ffn_gate_w"].T.reshape(2, P, EXPERTS).transpose(1, 0, 2).reshape(P, 2 * EXPERTS)
    out["moe_router_b"] = a["L0_ffn_gate_b"].reshape(1, EXPERTS)
    out["moe_descending"] = np.arange(EXPERTS, 0, -1, dtype=np.float32).reshape(1, EXPERTS)
    p = np.arange(P, dtype=np.float32)
    out["moe_numbers"] = np.concatenate([np.tile(p, (P, 1)), p[:, None]], axis=1)
    out["moe_tile_numbers"] = np.concatenate([np.tile(np.arange(1, TOP * TILES + 1, dtype=np.float32), (P, 1)),
                                              np.arange(BLOCKS, dtype=np.float32)[None, :] * P + p[:, None]], axis=1)
    out["moe_before"] = np.concatenate([np.triu(np.ones((P, P), np.float16), 1), np.ones((P, P), np.float16)], axis=1)


MOE_NAMES = ["moe_w", "moe_gate_b", "moe_up_b", "moe_down_b", "moe_router", "moe_router_b", "moe_descending", "moe_numbers",
             "moe_tile_numbers", "moe_before"]


TINY = 1e-37
QMAX = 127.0
FFQ = 704
Q_TILES = -(-FFQ // P)
Q_LAST = FFQ - (Q_TILES - 1) * P
ROUND = 1.5 * 2.0 ** 23
QCOLS = 512
Q_CHUNKS = [(at, min(QCOLS, TOKENS - at)) for at in range(0, TOKENS, QCOLS)]


def mlp_phase(nc, x_in, x_out, w_gate, w_up, w_down, clip_x, clip_down, identity):
    name = "mlp"
    with ExitStack() as ctx:
        def sb(label, shape, dt):
            return ctx.enter_context(nc.sbuf_tensor(f"{name}_{label}", shape, dt))

        def sem(label):
            return ctx.enter_context(nc.semaphore(f"{name}_{label}"))

        FLAT = TILES * DIM
        x_sb = sb("x", [P, TILES, DIM], F32)
        big = sb("big", [P, Q_TILES * TOKENS], F32)
        y_sb = big[:, 0:FLAT].rearrange("p (t d) -> p t d", d=DIM)
        h_sb = big[:, :].rearrange("p (f t) -> p f t", t=TOKENS)
        yq = sb("yq", [P, TILES, DIM], F16)
        yq_t = sb("yq_t", [P, 2, TOKENS], F16)
        w_nat = sb("w_nat", [P, 2, Q_TILES, DIM], F32)
        wd_nat = sb("wd_nat", [P, 2, FFQ], F32)
        w_q = sb("w_q", [P, 2, Q_TILES, DIM], F16)
        wd_q = sb("wd_q", [P, 2, FFQ], F16)
        w_t = sb("w_t", [P, 2, 2, Q_TILES * P], F16)
        wd_t = sb("wd_t", [P, Q_TILES, DIM], F16)
        w_abs = sb("w_abs", [P, 2 * Q_TILES + 2], F32)
        w_scale = sb("w_scale", [P, 2 * Q_TILES + 2], F32)
        w_inv = sb("w_inv", [P, 2 * Q_TILES + 2], F32)
        w_act = sb("w_act", [P, 2 * Q_TILES], F32)
        dsc = sb("dsc", [P, 2], F32)
        diag = sb("diag", [P, 2, P], F32)
        ones = sb("ones", [P, P], F32)
        down_row = sb("down_row", [P, DIM], F32)
        silu_sb = sb("silu", [P, 2, QCOLS], F32)
        hq = sb("hq", [P, 2, Q_TILES, P], F32)
        hq16 = sb("hq16", [P, 2, Q_TILES, P], F16)
        out_sb = sb("out", [P, 2, DIM], F32)
        ident = sb("ident", [P, P], F32)
        ident16 = sb("ident16", [P, P], F16)
        clips = sb("clips", [P, 2], F32)
        sig = sb("sig", [P, 2], F32)
        stats = sb("stats", [P, TILES, 6], F32)
        mv = sb("mv", [P, TILES, 2], F32)
        veps = sb("veps", [P, TILES], F32)
        rstd = sb("rstd", [P, TILES], F32)
        expo = sb("expo", [P, TILES], F32)
        part = sb("part", [P, 2], F32)
        hmaxes = sb("hmaxes", [P, Q_TILES * len(Q_CHUNKS)], F32)
        amax = sb("amax", [P, 2], F32)
        scale = sb("scale", [P, 2], F32)
        inv = sb("inv", [P, 2], F32)

        banks = [ctx.enter_context(nc.psum_tensor(f"{name}_bank{i}", [P, 512], F32)) for i in range(6)]
        banks16 = [ctx.enter_context(nc.psum_tensor(f"{name}_t{i}", [P, 1024], F16)) for i in range(2)]
        gate_ps, up_ps, y_ps = banks[0:2], banks[2:4], banks[4:6]

        const_in, x_in_sem, w_in = sem("const_in"), sem("x_in"), sem("w_in")
        setup = sem("setup")
        pool_ready, sig_ready = sem("pool_ready"), sem("sig_ready")
        eps_ready, rstd_ready = sem("eps_ready"), sem("rstd_ready")
        part_ready, amax_ready = sem("part_ready"), sem("amax_ready")
        q_ready, wq_ready = sem("q_ready"), sem("wq_ready")
        t_full, t_done, yt_done, row_full = sem("t_full"), sem("t_done"), sem("yt_done"), sem("row_full")
        scales_ready = sem("scales_ready")
        gu_full, silu_done, hid_done = sem("gu_full"), sem("silu_done"), sem("hid_done")
        hq_ready, hq16_ready, o_full, o_mul, o_done = (sem(s) for s in ("hq_ready", "hq16_ready", "o_full", "o_mul", "o_done"))
        stored = [sem(f"stored{i}") for i in range(2)]

        W_TURNS = [("gu", g, t) for g in range(2) for t in range(2)] + [("down", i, 0) for i in range(Q_TILES)]
        UNITS = [(f, c) for c in range(len(Q_CHUNKS)) for f in range(Q_TILES)]

        def tile_rows(f):
            return P if f < Q_TILES - 1 else Q_LAST

        with nc.Block() as block:

            @block.sync
            def _(sp):
                x_tiles = x_in.rearrange("(t p) d -> p t d", p=P)
                sp.dma_start(x_sb[:, :, :], x_tiles).then_inc(x_in_sem, 16)
                for g, w in enumerate((w_gate, w_up)):
                    full = (Q_TILES - 1) * P
                    sp.dma_start(w_nat[:, g, 0:Q_TILES - 1, :], w[0:full, :].rearrange("(f p) d -> p f d", p=P)).then_inc(w_in, 16)
                    sp.dma_start(w_nat[0:Q_LAST, g, Q_TILES - 1, :], w[full:FFQ, :]).then_inc(w_in, 16)
                sp.dma_start(wd_nat[:, :, :], w_down.rearrange("(t p) f -> p t f", p=P)).then_inc(w_in, 16)
                sp.dma_start(ident[:, :], identity).then_inc(const_in, 16)
                sp.dma_start(clips[:, 0:1], clip_x.to_broadcast([P, 1])).then_inc(const_in, 16)
                sp.dma_start(clips[:, 1:2], clip_down.to_broadcast([P, 1])).then_inc(const_in, 16)
                for k in range(TILES):
                    sp.wait_ge(o_done, k + 1)
                    sp.dma_start(x_out[P * k:P * (k + 1), :], out_sb[:, k % 2, :]).then_inc(stored[k % 2], 16)
                for b in range(2):
                    sp.wait_ge(stored[b], 16 * len(range(b, TILES, 2)))

            @block.gpsimd
            def _(pool):
                nc.gpsimd.memset(expo[:, :], -0.5).then_inc(pool_ready, 1)
                pool.wait_ge(pool_ready, 1)
                nc.gpsimd.memset(w_nat[Q_LAST:P, :, Q_TILES - 1, :], 0.0).then_inc(pool_ready, 1)
                pool.wait_ge(pool_ready, 2)
                nc.gpsimd.memset(ones[:, :], 1.0).then_inc(pool_ready, 1)
                pool.wait_ge(pool_ready, 3)
                pool.wait_ge(eps_ready, 1)
                nc.gpsimd.tensor_tensor(rstd[:, :], veps[:, :], expo[:, :], ALU.pow).then_inc(rstd_ready, 1)
                for k in range(2):
                    pool.wait_ge(part_ready, k + 1)
                    nc.gpsimd.partition_all_reduce(amax[:, k:k + 1], part[:, k:k + 1], P, bass.bass_isa.ReduceOp.max).then_inc(amax_ready, 1)

            @block.scalar
            def _(act):
                act.wait_ge(const_in, 48)
                nc.scalar.activation(sig[:, :], clips[:, :], ACT.Sigmoid).then_inc(sig_ready, 1)
                nc.scalar.activation(ident16[:, :], ident[:, :], ACT.Copy).then_inc(sig_ready, 1)
                for k, (what, i, t) in enumerate(W_TURNS):
                    act.wait_ge(t_full, k + 1)
                    if what == "gu":
                        nc.scalar.activation(w_t[:, i, t, :], banks16[k % 2][:, 0:Q_TILES * P], ACT.Copy).then_inc(t_done, 1)
                    else:
                        rows = tile_rows(i)
                        nc.scalar.activation(wd_t[0:rows, i, :], banks16[k % 2][0:rows, 0:DIM], ACT.Copy).then_inc(t_done, 1)
                for k, (at, cols) in enumerate(Q_CHUNKS):
                    act.wait_ge(t_full, len(W_TURNS) + k + 1)
                    src = banks16[k % 2][:, :].rearrange("p (t c) -> p t c", t=2)[:, :, 0:cols]
                    nc.scalar.activation(yq_t[:, :, at:at + cols], src, ACT.Copy).then_inc(t_done, 1)
                act.wait_ge(scales_ready, 1)
                for k, (f, c) in enumerate(UNITS):
                    rows, cols = tile_rows(f), Q_CHUNKS[c][1]
                    act.wait_ge(gu_full, k + 1)
                    if k >= 2:
                        act.wait_ge(hid_done, k - 1)
                    nc.scalar.activation(silu_sb[0:rows, k % 2, 0:cols], gate_ps[k % 2][0:rows, 0:cols], ACT.Silu,
                                         scale=w_act[0:rows, f:f + 1]).then_inc(silu_done, 1)
                for k in range(TILES):
                    act.wait_ge(hq_ready, k + 1)
                    if k >= 2:
                        act.wait_ge(o_full, k - 1)
                    for lo, hi, rows in ((0, Q_TILES - 1, P), (Q_TILES - 1, Q_TILES, Q_LAST)):
                        last = nc.scalar.activation(hq16[0:rows, k % 2, lo:hi, :], hq[0:rows, k % 2, lo:hi, :], ACT.Copy, bias=-ROUND)
                    last.then_inc(hq16_ready, 1)

            @block.vector
            def _(dve):
                count = [0]

                def step(instruction):
                    count[0] += 1
                    instruction.then_inc(setup, 1)
                    dve.wait_ge(setup, count[0])

                def quantise(flat, inverse):
                    step(nc.vector.tensor_scalar(flat, flat, inverse, ROUND, ALU.mult, ALU.add))
                    step(nc.vector.tensor_scalar(flat, flat, ROUND + QMAX, ROUND - QMAX - 1.0, ALU.min, ALU.max))

                dve.wait_ge(x_in_sem, 16)
                for k in range(TILES):
                    last = nc.vector.bn_stats(stats[:, k, :], x_sb[:, k, :])
                step(last)
                for k in range(TILES):
                    last = nc.vector.bn_aggr(mv[:, k, :], stats[:, k, :])
                step(last)
                nc.vector.tensor_scalar(veps[:, :], mv[:, :, 1], LN_EPS, None, ALU.add).then_inc(eps_ready, 1)

                dve.wait_ge(pool_ready, 3)
                dve.wait_ge(w_in, 16 * 5)
                step(nc.vector.tensor_reduce(w_abs[:, 0:2 * Q_TILES], w_nat[:, :, :, :].rearrange("p g f d -> p (g f) d"), AX.X, ALU.max,
                                             apply_absolute_value=True))
                step(nc.vector.tensor_reduce(w_abs[:, 2 * Q_TILES:], wd_nat[:, :, :], AX.X, ALU.max, apply_absolute_value=True))
                step(nc.vector.tensor_scalar(w_scale[:, :], w_abs[:, :], 1.0 / QMAX, None, ALU.mult))
                step(nc.vector.tensor_scalar(w_inv[:, :], w_scale[:, :], TINY, None, ALU.max))
                step(nc.vector.reciprocal(w_inv[:, :], w_inv[:, :]))
                for g in range(2):
                    for f in range(Q_TILES):
                        quantise(w_nat[:, g, f, :], w_inv[:, g * Q_TILES + f:g * Q_TILES + f + 1])
                for t in range(2):
                    quantise(wd_nat[:, t, :], w_inv[:, 2 * Q_TILES + t:2 * Q_TILES + t + 1])
                nc.vector.tensor_scalar(w_q[:, :, :, :].rearrange("p g f d -> p (g f d)"), w_nat[:, :, :, :].rearrange("p g f d -> p (g f d)"),
                                        ROUND, None, ALU.subtract).then_inc(wq_ready, 1)
                nc.vector.tensor_scalar(wd_q[:, :, :].rearrange("p t f -> p (t f)"), wd_nat[:, :, :].rearrange("p t f -> p (t f)"),
                                        ROUND, None, ALU.subtract).then_inc(wq_ready, 1)

                dve.wait_ge(rstd_ready, 1)
                for k in range(TILES):
                    last = nc.vector.tensor_scalar(y_sb[:, k, :], x_sb[:, k, :], mv[:, k, 0:1], rstd[:, k:k + 1], ALU.subtract, ALU.mult)
                step(last)
                flat = big[:, 0:FLAT]
                nc.vector.tensor_reduce(part[:, 0:1], flat, AX.X, ALU.max, apply_absolute_value=True).then_inc(part_ready, 1)

                def activation_scale(k):
                    col = slice(k, k + 1)
                    dve.wait_ge(amax_ready, k + 1)
                    step(nc.vector.tensor_tensor(scale[:, col], sig[:, col], amax[:, col], ALU.mult))
                    step(nc.vector.tensor_scalar(scale[:, col], scale[:, col], 1.0 / QMAX, None, ALU.mult))
                    step(nc.vector.tensor_scalar(inv[:, col], scale[:, col], TINY, None, ALU.max))
                    step(nc.vector.reciprocal(inv[:, col], inv[:, col]))

                dve.wait_ge(sig_ready, 1)
                activation_scale(0)
                for k in range(GROUPS):
                    part_flat = flat[:, k * GROUP * DIM:(k + 1) * GROUP * DIM]
                    quantise(part_flat, inv[:, 0:1])
                    nc.vector.tensor_scalar(yq[:, GROUP * k:GROUP * (k + 1), :].rearrange("p t d -> p (t d)"), part_flat, ROUND, None,
                                            ALU.subtract).then_inc(q_ready, 1)
                nc.vector.tensor_scalar(w_act[:, :], w_scale[:, 0:2 * Q_TILES], scale[:, 0:1], None, ALU.mult).then_inc(scales_ready, 1)
                dve.wait_ge(scales_ready, 1)
                dve.wait_ge(q_ready, GROUPS)

                for k, (f, c) in enumerate(UNITS):
                    rows, (at, cols) = tile_rows(f), Q_CHUNKS[c]
                    dve.wait_ge(silu_done, k + 1)
                    nc.vector.scalar_tensor_tensor(h_sb[0:rows, f, at:at + cols], up_ps[k % 2][0:rows, 0:cols],
                                                   w_act[0:rows, Q_TILES + f:Q_TILES + f + 1], silu_sb[0:rows, k % 2, 0:cols],
                                                   ALU.mult, ALU.mult).then_inc(hid_done, 1)
                    if k == 0:
                        step(nc.vector.memset(hmaxes[:, :], 0.0))
                    dve.wait_ge(hid_done, k + 1)
                    last = nc.vector.tensor_reduce(hmaxes[0:rows, k:k + 1], h_sb[0:rows, f, at:at + cols], AX.X, ALU.max,
                                                   apply_absolute_value=True)
                step(last)
                nc.vector.tensor_reduce(part[:, 1:2], hmaxes[:, :], AX.X, ALU.max).then_inc(part_ready, 1)
                activation_scale(1)

                for t in range(2):
                    step(nc.vector.tensor_scalar(dsc[:, t:t + 1], w_scale[:, 2 * Q_TILES + t:2 * Q_TILES + t + 1], scale[:, 1:2], None, ALU.mult))
                    step(nc.vector.tensor_scalar(diag[:, t, :], ident[:, :], dsc[:, t:t + 1], None, ALU.mult))
                nc.vector.memset(dsc[:, :], 0.0).then_inc(scales_ready, 1)
                dve.wait_ge(row_full, 1)
                step(nc.vector.tensor_copy(down_row[:, :], banks[0][:, 0:DIM]))

                def combine(k):
                    dve.wait_ge(o_full, k + 1)
                    if k >= 2:
                        dve.wait_ge(stored[k % 2], 16 * (k // 2))
                    nc.vector.tensor_tensor(out_sb[:, k % 2, :], y_ps[k % 2][:, 0:DIM], down_row[:, :], ALU.mult).then_inc(o_mul, 1)
                    dve.wait_ge(o_mul, k + 1)
                    nc.vector.tensor_tensor(out_sb[:, k % 2, :], out_sb[:, k % 2, :], x_sb[:, k, :], ALU.add).then_inc(o_done, 1)

                for k in range(TILES):
                    if k >= 2:
                        dve.wait_ge(hq16_ready, k - 1)
                    for lo, hi, rows in ((0, Q_TILES - 1, P), (Q_TILES - 1, Q_TILES, Q_LAST)):
                        dst, src = hq[0:rows, k % 2, lo:hi, :], h_sb[0:rows, lo:hi, P * k:P * (k + 1)]
                        step(nc.vector.tensor_scalar(dst, src, inv[0:rows, 1:2], ROUND, ALU.mult, ALU.add))
                        last = nc.vector.tensor_scalar(dst, dst, ROUND + QMAX, ROUND - QMAX - 1.0, ALU.min, ALU.max)
                    last.then_inc(hq_ready, 1)
                    if k >= 1:
                        combine(k - 1)
                combine(TILES - 1)

            @block.tensor
            def _(pe):
                pe.wait_ge(sig_ready, 2)
                pe.wait_ge(wq_ready, 2)
                for k, (what, i, t) in enumerate(W_TURNS):
                    if k >= 2:
                        pe.wait_ge(t_done, k - 1)
                    if what == "gu":
                        for f in range(Q_TILES):
                            last = nc.tensor.transpose(banks16[k % 2][:, P * f:P * (f + 1)], w_q[:, i, f, P * t:P * (t + 1)], ident16[:, :])
                    else:
                        rows = tile_rows(i)
                        for d in range(2):
                            last = nc.tensor.transpose(banks16[k % 2][0:rows, P * d:P * (d + 1)], wd_q[:, d, P * i:P * i + rows], ident16[:, :])
                    last.then_inc(t_full, 1)
                n = len(W_TURNS)
                for k, (at, cols) in enumerate(Q_CHUNKS):
                    pe.wait_ge(t_done, n + k - 1)
                    pe.wait_ge(q_ready, -(-(at + cols) // CHUNK))
                    for t in range(2):
                        for j in range(cols // P):
                            col = QCOLS * t + P * j
                            last = nc.tensor.transpose(banks16[k % 2][:, col:col + P], yq[:, at // P + j, P * t:P * (t + 1)], ident16[:, :])
                    last.then_inc(t_full, 1)
                for k, (f, c) in enumerate(UNITS):
                    rows, (at, cols) = tile_rows(f), Q_CHUNKS[c]
                    pe.wait_ge(t_done, n + c + 1)
                    if k >= 2:
                        pe.wait_ge(hid_done, k - 1)
                    for g, ps in ((0, gate_ps), (1, up_ps)):
                        for t in range(2):
                            last = nc.tensor.matmul(ps[k % 2][0:rows, 0:cols], w_t[:, g, t, P * f:P * f + rows], yq_t[:, t, at:at + cols],
                                                    start=(t == 0), stop=(t == 1))
                    last.then_inc(gu_full, 1)
                pe.wait_ge(scales_ready, 2)
                for t in range(2):
                    last = nc.tensor.matmul(banks[0][:, P * t:P * (t + 1)], ones[:, :], diag[:, t, :], start=True, stop=True)
                last.then_inc(row_full, 1)
                for k in range(TILES):
                    pe.wait_ge(hq16_ready, k + 1)
                    if k >= 2:
                        pe.wait_ge(o_done, k - 1)
                    for f in range(Q_TILES):
                        rows = tile_rows(f)
                        last = nc.tensor.matmul(y_ps[k % 2][:, 0:DIM], hq16[0:rows, k % 2, f, :], wd_t[0:rows, f, :],
                                                start=(f == 0), stop=(f == Q_TILES - 1))
                    last.then_inc(o_full, 1)


MLP_NAMES = ["mlp_gate", "mlp_up", "mlp_down", "mlp_clip_x", "mlp_clip_down"]


ATT_COMMON = ["ctx_main", "ctx_rem", "identity"]
ATT_NAMES = [["a0_wq", "a0_wk_main", "a0_wk_rem", "a0_wv_main", "a0_wv_rem", "a0_wo", "a0_bo"],
             ["a1_wq", "a1_wk_main", "a1_wk_rem", "a1_wv_main", "a1_wv_rem", "a1_wo", "a1_bo", "a1_mask", "a1_gamma", "a1_beta"]]


ALL_NAMES = ["x"] + ATT_COMMON + ATT_NAMES[0] + ATT_NAMES[1] + MOE_NAMES + MLP_NAMES


def build(nc, d, out):
    rows = [nc.dram_tensor(f"rows{i}", (TOKENS, DIM), F32, kind="Internal").ap() for i in range(3)]
    finished = run_attention(nc, 0, d, d["x"], rows[0])
    moe_phase(nc, rows[0], rows[1], *[d[n] for n in MOE_NAMES], d["identity"], finished)
    run_attention(nc, 1, d, rows[1], rows[2])
    mlp_phase(nc, rows[2], out, *[d[n] for n in MLP_NAMES], d["identity"])


def run_attention(nc, layer, d, x_in, x_out):
    w = [d[n] for n in ATT_NAMES[layer]]
    return attention_phase(nc, f"att{layer}", x_in, x_out, d["ctx_main"], d["ctx_rem"], *w[:7], d["identity"], *w[7:])


def layout(inputs):
    a = {k: np.asarray(v) for k, v in inputs.items()}
    out = {"x": a["x"].reshape(TOKENS, DIM), "identity": np.eye(P, dtype=np.float32)}
    ctx_t = a["ctx_768"].reshape(BATCH * KEYS, CTX).T
    out["ctx_main"] = ctx_t[0:P]
    out["ctx_rem"] = np.concatenate([ctx_t[P:CTX], ctx_t[P:CTX]])
    kv = a["L1_xattn_Wkv"]
    for layer, wk, wv in ((0, a["L0_xattn_Wk"], a["L0_xattn_Wv"]), (1, kv[:, 0:INNER], kv[:, INNER:])):
        n = f"a{layer}_"
        out[n + "wq"] = a[f"L{layer}_xattn_Wq"].reshape(2, P, INNER).transpose(1, 0, 2).reshape(P, 2 * INNER)
        for what, w in (("wk", wk), ("wv", wv)):
            out[n + what + "_main"] = w[0:P]
            out[n + what + "_rem"] = np.concatenate([w[P:CTX], w[P:CTX]])
        out[n + "wo"] = a[f"L{layer}_xattn_Wo"].reshape(PAIRS, P, DIM).transpose(1, 0, 2)
        out[n + "bo"] = a[f"L{layer}_xattn_bo"].reshape(1, DIM)
    out["a1_mask"] = a["mask_1x1xSxS2_bk0"].reshape(SEQ, KEYS)
    out["a1_gamma"] = a["L1_xattn_ln_gamma"].reshape(2, P).T
    out["a1_beta"] = a["L1_xattn_ln_beta"].reshape(2, P).T
    layout_moe(a, out)
    out["mlp_gate"], out["mlp_up"], out["mlp_down"] = (a[f"L1_ffn_w_{n}"] for n in ("gate", "up", "down"))
    out["mlp_clip_x"], out["mlp_clip_down"] = a["L1_ffn_clip_x"].reshape(1, 1), a["L1_ffn_clip_down"].reshape(1, 1)
    return {k: np.ascontiguousarray(v) for k, v in out.items()}


def kernel(**inputs):
    import concourse.bacc as bacc
    from concourse.bass_utils import run_bass_kernel_spmd

    nc = bacc.Bacc("TRN2", target_bir_lowering=False, num_devices=1)
    arrays = layout(inputs)
    aps = {n: nc.dram_tensor(f"in_{n}", arrays[n].shape, mybir.dt.from_np(arrays[n].dtype), kind="ExternalInput").ap() for n in ALL_NAMES}
    out = nc.dram_tensor("y", (TOKENS, DIM), F32, kind="ExternalOutput").ap()
    build(nc, aps, out)
    r = run_bass_kernel_spmd(nc, [{f"in_{n}": arrays[n] for n in ALL_NAMES}], core_ids=[0])
    return r.results[0]["y"].reshape(BATCH, SEQ, DIM)
```
